# Optimizing a Trainium2 kernel written in Bass

```python
import numpy as np
import jax
import jax.numpy as jnp

def _softmax(x, axis=-1):
    return jax.nn.softmax(x, axis=axis)

def _gelu(x):
    return jax.nn.gelu(x, approximate=True)

def _silu(x):
    return jax.nn.silu(x)

def _sigmoid(x):
    return jax.nn.sigmoid(x)

def _layernorm(x, axis=-1, eps=1e-05):
    m = jnp.mean(x, axis=axis, keepdims=True)
    v = jnp.var(x, axis=axis, keepdims=True)
    return (x - m) / jnp.sqrt(v + eps)

def _scatter_add(tgt, idx, src, axis=0):
    return tgt.at[idx].add(src)

def _segment_sum(src, seg, n):
    return jax.ops.segment_sum(src, seg, n)
kernel_name = 'mk_decoder_postln_d2_seqx_r8_7844e1'

def setup_inputs(seed: int=0):
    np.random.seed(seed)
    _w = jnp.asarray

    def _rec_inputs():
        import jax
        import jax.numpy as jnp
        _rk = jax.random.key(seed)
        x = -0.0002928 + 1 * jax.random.normal(jax.random.fold_in(_rk, 1), (1, 1024, 128), jnp.float32)
        _lenS = 1024 - jax.random.randint(jax.random.fold_in(_rk, 7), (1,), 0, max(1, 1024 // 4) + 1, jnp.int32)
        _lenS2 = 6404 - jax.random.randint(jax.random.fold_in(_rk, 8), (1,), 0, max(1, 6404 // 4) + 1, jnp.int32)
        _ctx_768P = jax.random.normal(jax.random.fold_in(_rk, 11), (1, 16, 96), jnp.float32)
        _ctx_768c = jax.random.dirichlet(jax.random.fold_in(_rk, 511), 0.3 * jnp.ones((16,), jnp.float32), (1, 6404))
        _ctx_768t = jnp.einsum('bsk,bkd->bsd', _ctx_768c, _ctx_768P)
        _ctx_768t = _ctx_768t * jax.lax.rsqrt(jnp.mean(jnp.square(_ctx_768t)) + 1e-12) * 0.953939
        ctx_768 = 2.09791e-05 + 1.00001 * (_ctx_768t + 0.3 * jax.random.normal(jax.random.fold_in(_rk, 611), (1, 6404, 96), jnp.float32))
        return (x, ctx_768)
    x, ctx_768 = _rec_inputs()

    def _L0_attn_setup():
        import jax, jax.numpy as jnp
        import numpy as np
        EMBED_DIM = 128
        NUM_HEADS = 8
        NUM_POINTS = 4
        B, N = (4, 1024)
        key = jax.random.key(seed)
        ks = jax.random.split(key, 8)
        C, H, P = (EMBED_DIM, NUM_HEADS, NUM_POINTS)
        sc = 1.0 / np.sqrt(C)
        x = jax.random.normal(ks[0], (B, N, C), dtype=jnp.float32)
        W_off = jax.random.normal(ks[1], (C, H * P * 2), dtype=jnp.float32) * sc
        b_off = jax.random.normal(ks[2], (H * P * 2,), dtype=jnp.float32) * 0.1
        W_attn = jax.random.normal(ks[3], (C, H * P), dtype=jnp.float32) * sc
        b_attn = jax.random.normal(ks[4], (H * P,), dtype=jnp.float32) * 0.1
        W_out = jax.random.normal(ks[5], (C, C), dtype=jnp.float32) * sc
        b_out = jax.random.normal(ks[6], (C,), dtype=jnp.float32) * 0.1
        return {'x': x, 'W_off': W_off, 'b_off': b_off, 'W_attn': W_attn, 'b_attn': b_attn, 'W_out': W_out, 'b_out': b_out}
    _L0_attn_all = _L0_attn_setup()
    _L0_attn_in = {k: v for k, v in _L0_attn_all.items() if k in ('W_off', 'b_off', 'W_attn', 'b_attn', 'W_out', 'b_out')}
    del _L0_attn_all

    def _L0_xattn_setup():
        import jax, jax.numpy as jnp
        import numpy as np
        N_HEADS = 16
        EMBED_DIM = 128
        CROSS_DIM = 96
        HEAD_DIM = EMBED_DIM // N_HEADS
        key = jax.random.key(seed)
        ks = jax.random.split(key, 12)
        B, SQ, SKV = (2, 256, 256)
        s_in = 1.0 / np.sqrt(EMBED_DIM)
        s_cross = 1.0 / np.sqrt(CROSS_DIM)
        return {'x': jax.random.normal(ks[0], (B, SQ, EMBED_DIM), jnp.float32), 'y': jax.random.normal(ks[1], (B, SKV, CROSS_DIM), jnp.float32), 'wq': jax.random.normal(ks[2], (EMBED_DIM, EMBED_DIM), jnp.float32) * s_in, 'bq': jax.random.normal(ks[3], (EMBED_DIM,), jnp.float32) * s_in, 'wk': jax.random.normal(ks[4], (EMBED_DIM, CROSS_DIM), jnp.float32) * s_cross, 'bk': jax.random.normal(ks[5], (EMBED_DIM,), jnp.float32) * s_cross, 'wv': jax.random.normal(ks[6], (EMBED_DIM, CROSS_DIM), jnp.float32) * s_cross, 'bv': jax.random.normal(ks[7], (EMBED_DIM,), jnp.float32) * s_cross, 'wo': jax.random.normal(ks[8], (EMBED_DIM, EMBED_DIM), jnp.float32) * s_in, 'bo': jax.random.normal(ks[9], (EMBED_DIM,), jnp.float32) * s_in}
    _L0_xattn_all = _L0_xattn_setup()
    _L0_xattn_in = {k: v for k, v in _L0_xattn_all.items() if k in ('wq', 'bq', 'wk', 'bk', 'wv', 'bv', 'wo', 'bo')}
    del _L0_xattn_all

    def _L0_ffn_setup():
        import jax, jax.numpy as jnp
        import numpy as np
        NUM_EXPERTS = 8
        N_EMBD = 128
        D_FF = 4 * N_EMBD
        B, S = (4, 256)
        key = jax.random.key(seed)
        ks = jax.random.split(key, 6)
        x = jax.random.normal(ks[0], (B, S, N_EMBD), dtype=jnp.float32)
        gate_w = jax.random.normal(ks[1], (N_EMBD, NUM_EXPERTS), dtype=jnp.float32) * 0.02
        w1 = jax.random.normal(ks[2], (NUM_EXPERTS, N_EMBD, D_FF), dtype=jnp.float32) * 0.02
        b1 = jnp.zeros((NUM_EXPERTS, D_FF), dtype=jnp.float32)
        w2 = jax.random.normal(ks[3], (NUM_EXPERTS, D_FF, N_EMBD), dtype=jnp.float32) * 0.02
        b2 = jnp.zeros((NUM_EXPERTS, N_EMBD), dtype=jnp.float32)
        return {'x': x, 'gate_w': gate_w, 'w1': w1, 'b1': b1, 'w2': w2, 'b2': b2}
    _L0_ffn_all = _L0_ffn_setup()
    _L0_ffn_in = {k: v for k, v in _L0_ffn_all.items() if k in ('gate_w', 'w1', 'b1', 'w2', 'b2')}
    del _L0_ffn_all

    def _L1_attn_setup():
        import jax, jax.numpy as jnp
        import numpy as np
        B, L, H, N = (16, 128, 128, 64)

        def _s4_block(x, log_dt, A_real_log, A_imag, C_real, C_imag, D, W_out, b_out):
            Lq = x.shape[1]
            dt = jnp.exp(log_dt)
            A = -jnp.exp(A_real_log) + 1j * A_imag
            C = C_real + 1j * C_imag
            dtA = dt[:, None] * A
            coef = C * (jnp.exp(dtA) - 1.0) / A
            vand = jnp.exp(dtA[:, :, None] * jnp.arange(Lq, dtype=jnp.float32))
            kern = 2.0 * jnp.einsum('hn,hnl->hl', coef, vand).real
            n = 2 * Lq
            k_f = jnp.fft.rfft(kern, n=n)
            u_f = jnp.fft.rfft(x, n=n, axis=1)
            y = jnp.fft.irfft(u_f * k_f.T[None], n=n, axis=1)[:, :Lq, :]
            y = jax.nn.gelu(y + x * D)
            z = y @ W_out + b_out
            a, g = jnp.split(z, 2, axis=-1)
            return a * jax.nn.sigmoid(g)
        key = jax.random.key(seed)
        k = jax.random.split(key, 8)
        x = jax.random.normal(k[0], (B, L, H), dtype=jnp.float32)
        log_dt = np.log(0.001) + jax.random.uniform(k[1], (H,), dtype=jnp.float32) * (np.log(0.1) - np.log(0.001))
        A_real_log = jnp.log(0.5 * jnp.ones((H, N), dtype=jnp.float32))
        A_imag = jnp.pi * jnp.broadcast_to(jnp.arange(N, dtype=jnp.float32), (H, N))
        C_real = jax.random.normal(k[2], (H, N), dtype=jnp.float32) * 0.5 ** 0.5
        C_imag = jax.random.normal(k[3], (H, N), dtype=jnp.float32) * 0.5 ** 0.5
        D = jax.random.normal(k[4], (H,), dtype=jnp.float32)
        W_out = jax.random.normal(k[5], (H, 2 * H), dtype=jnp.float32) / np.sqrt(H)
        b_out = jnp.zeros((2 * H,), dtype=jnp.float32)
        return dict(x=x, log_dt=log_dt, A_real_log=A_real_log, A_imag=A_imag, C_real=C_real, C_imag=C_imag, D=D, W_out=W_out, b_out=b_out)
    _L1_attn_all = _L1_attn_setup()
    _L1_attn_in = {k: v for k, v in _L1_attn_all.items() if k in ('log_dt', 'A_real_log', 'A_imag', 'C_real', 'C_imag', 'D', 'W_out', 'b_out')}
    del _L1_attn_all

    def _L1_xattn_setup():
        import jax, jax.numpy as jnp
        import numpy as np
        import math
        E = 128
        EV = 128
        FFN = 512
        DINO = 96
        B, S, P = (64, 64, 32)

        def bitnet_linear(x, W, b):
            w_scale = jnp.maximum(jnp.mean(jnp.abs(W)), 1e-05)
            qW = jnp.sign(W) * (jnp.abs(W) > 0.5 * w_scale).astype(W.dtype)
            i_scale = jnp.maximum(jnp.max(jnp.abs(x)), 1e-08) / 127.0
            qx = jnp.clip(jnp.round(x / i_scale), -128.0, 127.0)
            out = jnp.einsum('...i,oi->...o', qx, qW) * (w_scale * i_scale)
            return out + b
        key = jax.random.key(seed)
        ks = iter(jax.random.split(key, 32))

        def lin_w(fin, fout):
            return jax.random.normal(next(ks), (fout, fin), jnp.float32) * math.sqrt(2.0 / fin)
        return {'text_embeddings': jax.random.normal(next(ks), (B, S, E), jnp.float32), 'dinov2_features': jax.random.normal(next(ks), (B, P, DINO), jnp.float32), 'W_d2v': lin_w(DINO, EV), 'b_d2v': jnp.zeros((EV,), jnp.float32), 'W_img': lin_w(EV, E), 'b_img': jnp.zeros((E,), jnp.float32), 'W_txt': lin_w(E, E), 'b_txt': jnp.zeros((E,), jnp.float32), 'W_att0': lin_w(E, E // 2), 'b_att0': jnp.zeros((E // 2,), jnp.float32), 'W_att1': lin_w(E, E // 2), 'b_att1': jnp.zeros((E // 2,), jnp.float32), 'W_f1': lin_w(2 * E, FFN), 'b_f1': jnp.zeros((FFN,), jnp.float32), 'W_f2': lin_w(FFN, E), 'b_f2': jnp.zeros((E,), jnp.float32)}
    _L1_xattn_all = _L1_xattn_setup()
    _L1_xattn_in = {k: v for k, v in _L1_xattn_all.items() if k in ('W_d2v', 'b_d2v', 'W_img', 'b_img', 'W_txt', 'b_txt', 'W_att0', 'b_att0', 'W_att1', 'b_att1', 'W_f1', 'b_f1', 'W_f2', 'b_f2')}
    del _L1_xattn_all

    def _L1_ffn_setup():
        import jax, jax.numpy as jnp
        import numpy as np
        B, S, D = (2, 256, 128)
        E, F, TOP_K = (8, 256, 2)
        key = jax.random.key(seed)
        ks = jax.random.split(key, 5)
        scale = 0.02
        return {'x': jax.random.normal(ks[0], (B, S, D), dtype=jnp.float32), 'gate_w': jax.random.normal(ks[1], (E, D), dtype=jnp.float32) * scale, 'w_gate': jax.random.normal(ks[2], (E, D, F), dtype=jnp.float32) * scale, 'w_up': jax.random.normal(ks[3], (E, D, F), dtype=jnp.float32) * scale, 'w_down': jax.random.normal(ks[4], (E, F, D), dtype=jnp.float32) * scale}
    _L1_ffn_all = _L1_ffn_setup()
    _L1_ffn_in = {k: v for k, v in _L1_ffn_all.items() if k in ('gate_w', 'w_gate', 'w_up', 'w_down')}
    del _L1_ffn_all
    return {'x': x, 'ctx_768': ctx_768, 'L0_attn_W_off': _L0_attn_in['W_off'], 'L0_attn_b_off': _L0_attn_in['b_off'], 'L0_attn_W_attn': _L0_attn_in['W_attn'], 'L0_attn_b_attn': _L0_attn_in['b_attn'], 'L0_attn_W_out': _L0_attn_in['W_out'], 'L0_attn_b_out': _L0_attn_in['b_out'], 'L0_xattn_wq': _L0_xattn_in['wq'], 'L0_xattn_bq': _L0_xattn_in['bq'], 'L0_xattn_wk': _L0_xattn_in['wk'], 'L0_xattn_bk': _L0_xattn_in['bk'], 'L0_xattn_wv': _L0_xattn_in['wv'], 'L0_xattn_bv': _L0_xattn_in['bv'], 'L0_xattn_wo': _L0_xattn_in['wo'], 'L0_xattn_bo': _L0_xattn_in['bo'], 'L0_ffn_gate_w': _L0_ffn_in['gate_w'], 'L0_ffn_w1': _L0_ffn_in['w1'], 'L0_ffn_b1': _L0_ffn_in['b1'], 'L0_ffn_w2': _L0_ffn_in['w2'], 'L0_ffn_b2': _L0_ffn_in['b2'], 'L1_attn_log_dt': _L1_attn_in['log_dt'], 'L1_attn_A_real_log': _L1_attn_in['A_real_log'], 'L1_attn_A_imag': _L1_attn_in['A_imag'], 'L1_attn_C_real': _L1_attn_in['C_real'], 'L1_attn_C_imag': _L1_attn_in['C_imag'], 'L1_attn_D': _L1_attn_in['D'], 'L1_attn_W_out': _L1_attn_in['W_out'], 'L1_attn_b_out': _L1_attn_in['b_out'], 'L1_xattn_W_d2v': _L1_xattn_in['W_d2v'], 'L1_xattn_b_d2v': _L1_xattn_in['b_d2v'], 'L1_xattn_W_img': _L1_xattn_in['W_img'], 'L1_xattn_b_img': _L1_xattn_in['b_img'], 'L1_xattn_W_txt': _L1_xattn_in['W_txt'], 'L1_xattn_b_txt': _L1_xattn_in['b_txt'], 'L1_xattn_W_att0': _L1_xattn_in['W_att0'], 'L1_xattn_b_att0': _L1_xattn_in['b_att0'], 'L1_xattn_W_att1': _L1_xattn_in['W_att1'], 'L1_xattn_b_att1': _L1_xattn_in['b_att1'], 'L1_xattn_W_f1': _L1_xattn_in['W_f1'], 'L1_xattn_b_f1': _L1_xattn_in['b_f1'], 'L1_xattn_W_f2': _L1_xattn_in['W_f2'], 'L1_xattn_b_f2': _L1_xattn_in['b_f2'], 'L1_ffn_gate_w': _L1_ffn_in['gate_w'], 'L1_ffn_w_gate': _L1_ffn_in['w_gate'], 'L1_ffn_w_up': _L1_ffn_in['w_up'], 'L1_ffn_w_down': _L1_ffn_in['w_down']}

def reference(x, ctx_768, L0_attn_W_off, L0_attn_b_off, L0_attn_W_attn, L0_attn_b_attn, L0_attn_W_out, L0_attn_b_out, L0_xattn_wq, L0_xattn_bq, L0_xattn_wk, L0_xattn_bk, L0_xattn_wv, L0_xattn_bv, L0_xattn_wo, L0_xattn_bo, L0_ffn_gate_w, L0_ffn_w1, L0_ffn_b1, L0_ffn_w2, L0_ffn_b2, L1_attn_log_dt, L1_attn_A_real_log, L1_attn_A_imag, L1_attn_C_real, L1_attn_C_imag, L1_attn_D, L1_attn_W_out, L1_attn_b_out, L1_xattn_W_d2v, L1_xattn_b_d2v, L1_xattn_W_img, L1_xattn_b_img, L1_xattn_W_txt, L1_xattn_b_txt, L1_xattn_W_att0, L1_xattn_b_att0, L1_xattn_W_att1, L1_xattn_b_att1, L1_xattn_W_f1, L1_xattn_b_f1, L1_xattn_W_f2, L1_xattn_b_f2, L1_ffn_gate_w, L1_ffn_w_gate, L1_ffn_w_up, L1_ffn_w_down):
    import jax
    import jax.numpy as jnp

    def _L0_attn_ref(x, W_off, b_off, W_attn, b_attn, W_out, b_out):
        import jax, jax.numpy as jnp
        import numpy as np
        EMBED_DIM = 128
        NUM_HEADS = 8
        NUM_POINTS = 4
        B, N = (4, 1024)
        Bx, Nx, C = x.shape
        H, P = (NUM_HEADS, NUM_POINTS)
        off = (x @ W_off + b_off).reshape(Bx, Nx, H, P, 2)
        w = jax.nn.softmax((x @ W_attn + b_attn).reshape(Bx, Nx, H, P), axis=-1)
        idx = off[..., 0].astype(jnp.int32)
        idx = jnp.where(idx < 0, idx + C, idx)
        idx = jnp.clip(idx, 0, C - 1)
        x0 = x[:, 0, :]
        g = jnp.take_along_axis(x0, idx.reshape(Bx, -1), axis=1).reshape(Bx, Nx, H, P)
        s = jnp.sum(g * w, axis=(2, 3))
        out = jnp.broadcast_to(s[..., None], (Bx, Nx, C))
        return out @ W_out + b_out

    def _L0_xattn_ref(x, y, wq, bq, wk, bk, wv, bv, wo, bo):
        import jax, jax.numpy as jnp
        import numpy as np
        N_HEADS = 16
        EMBED_DIM = 128
        CROSS_DIM = 96
        HEAD_DIM = EMBED_DIM // N_HEADS
        B, SQ, E = x.shape
        q = x @ wq.T + bq
        k = y @ wk.T + bk
        v = y @ wv.T + bv
        q = q.reshape(B, SQ, N_HEADS, HEAD_DIM).transpose(0, 2, 1, 3)
        k = k.reshape(B, -1, N_HEADS, HEAD_DIM).transpose(0, 2, 1, 3)
        v = v.reshape(B, -1, N_HEADS, HEAD_DIM).transpose(0, 2, 1, 3)
        scale = 1.0 / jnp.sqrt(jnp.asarray(HEAD_DIM, x.dtype))
        score = jnp.einsum('bhqd,bhkd->bhqk', q, k) * scale
        attn = jax.nn.softmax(score, axis=-1)
        out = jnp.einsum('bhqk,bhkd->bhqd', attn, v)
        out = out.transpose(0, 2, 1, 3).reshape(B, SQ, E)
        return out @ wo.T + bo

    def _L0_ffn_ref(x, gate_w, w1, b1, w2, b2):
        import jax, jax.numpy as jnp
        import numpy as np
        NUM_EXPERTS = 8
        N_EMBD = 128
        D_FF = 4 * N_EMBD
        B, S = (4, 256)
        Bb, Ss, D = x.shape
        x_flat = x.reshape(-1, D)
        router_logits = x_flat @ gate_w
        router_probs = jax.nn.softmax(router_logits, axis=-1)
        expert_idx = jnp.argmax(router_probs, axis=-1)
        expert_w = jnp.take_along_axis(router_probs, expert_idx[:, None], axis=1)[:, 0]
        out = jnp.zeros_like(x_flat)
        for e in range(NUM_EXPERTS):
            h = jax.nn.gelu(x_flat @ w1[e] + b1[e], approximate=False)
            y = h @ w2[e] + b2[e]
            sel = expert_idx == e
            out = out + jnp.where(sel, expert_w, 0.0)[:, None] * y
        return out.reshape(Bb, Ss, D)

    def _L1_attn_ref(x, log_dt, A_real_log, A_imag, C_real, C_imag, D, W_out, b_out):
        import jax, jax.numpy as jnp
        import numpy as np
        B, L, H, N = (16, 128, 128, 64)

        def _s4_block(x, log_dt, A_real_log, A_imag, C_real, C_imag, D, W_out, b_out):
            Lq = x.shape[1]
            dt = jnp.exp(log_dt)
            A = -jnp.exp(A_real_log) + 1j * A_imag
            C = C_real + 1j * C_imag
            dtA = dt[:, None] * A
            coef = C * (jnp.exp(dtA) - 1.0) / A
            vand = jnp.exp(dtA[:, :, None] * jnp.arange(Lq, dtype=jnp.float32))
            kern = 2.0 * jnp.einsum('hn,hnl->hl', coef, vand).real
            n = 2 * Lq
            k_f = jnp.fft.rfft(kern, n=n)
            u_f = jnp.fft.rfft(x, n=n, axis=1)
            y = jnp.fft.irfft(u_f * k_f.T[None], n=n, axis=1)[:, :Lq, :]
            y = jax.nn.gelu(y + x * D)
            z = y @ W_out + b_out
            a, g = jnp.split(z, 2, axis=-1)
            return a * jax.nn.sigmoid(g)
        return _s4_block(x, log_dt, A_real_log, A_imag, C_real, C_imag, D, W_out, b_out)

    def _L1_xattn_ref(text_embeddings, dinov2_features, W_d2v, b_d2v, W_img, b_img, W_txt, b_txt, W_att0, b_att0, W_att1, b_att1, W_f1, b_f1, W_f2, b_f2):
        import jax, jax.numpy as jnp
        import numpy as np
        import math
        E = 128
        EV = 128
        FFN = 512
        DINO = 96
        B, S, P = (64, 64, 32)

        def bitnet_linear(x, W, b):
            w_scale = jnp.maximum(jnp.mean(jnp.abs(W)), 1e-05)
            qW = jnp.sign(W) * (jnp.abs(W) > 0.5 * w_scale).astype(W.dtype)
            i_scale = jnp.maximum(jnp.max(jnp.abs(x)), 1e-08) / 127.0
            qx = jnp.clip(jnp.round(x / i_scale), -128.0, 127.0)
            out = jnp.einsum('...i,oi->...o', qx, qW) * (w_scale * i_scale)
            return out + b
        b, s, e = text_embeddings.shape
        vis = bitnet_linear(dinov2_features, W_d2v, b_d2v)
        image_embeds = bitnet_linear(vis, W_img, b_img)
        fused = bitnet_linear(text_embeddings, W_txt, b_txt)
        inv_sqrt_e = 1.0 / math.sqrt(e)
        for Wa, ba in ((W_att0, b_att0), (W_att1, b_att1)):
            kv = bitnet_linear(image_embeds, Wa, ba)
            k = jnp.concatenate([kv, kv], axis=-1)
            scores = jnp.einsum('bse,bpe->bsp', fused, k) * inv_sqrt_e
            attn = jax.nn.softmax(scores, axis=-1)
            fused = fused + 0.1 * jnp.einsum('bsp,bpe->bse', attn, k)
        avg_img = jnp.mean(image_embeds, axis=1, keepdims=True)
        concatenated = jnp.concatenate([fused, jnp.broadcast_to(avg_img, (b, s, e))], axis=-1)
        h = jax.nn.relu(bitnet_linear(concatenated, W_f1, b_f1))
        return bitnet_linear(h, W_f2, b_f2)

    def _L1_ffn_ref(x, gate_w, w_gate, w_up, w_down):
        import jax, jax.numpy as jnp
        import numpy as np
        B, S, D = (2, 256, 128)
        E, F, TOP_K = (8, 256, 2)
        b, s, d = x.shape
        xt = x.reshape(-1, d)
        T = xt.shape[0]
        logits = xt @ gate_w.T
        top_v, top_i = jax.lax.top_k(logits, TOP_K)
        top_w = jax.nn.softmax(top_v, axis=-1)
        w_dense = jnp.zeros_like(logits).at[jnp.arange(T)[:, None], top_i].add(top_w)
        g = jnp.einsum('td,edf->tef', xt, w_gate)
        u = jnp.einsum('td,edf->tef', xt, w_up)
        h = jax.nn.silu(g) * u
        y = jnp.einsum('tef,efd,te->td', h, w_down, w_dense)
        return y.reshape(b, s, d)
    x = _layernorm(x + _L0_attn_ref(x, L0_attn_W_off, L0_attn_b_off, L0_attn_W_attn, L0_attn_b_attn, L0_attn_W_out, L0_attn_b_out), axis=-1)
    x = _layernorm(x + _L0_xattn_ref(x, ctx_768, L0_xattn_wq, L0_xattn_bq, L0_xattn_wk, L0_xattn_bk, L0_xattn_wv, L0_xattn_bv, L0_xattn_wo, L0_xattn_bo), axis=-1)
    x = _layernorm(x + _L0_ffn_ref(x, L0_ffn_gate_w, L0_ffn_w1, L0_ffn_b1, L0_ffn_w2, L0_ffn_b2), axis=-1)
    x = _layernorm(x + _L1_attn_ref(x, L1_attn_log_dt, L1_attn_A_real_log, L1_attn_A_imag, L1_attn_C_real, L1_attn_C_imag, L1_attn_D, L1_attn_W_out, L1_attn_b_out), axis=-1)
    x = _layernorm(x + _L1_xattn_ref(x, ctx_768, L1_xattn_W_d2v, L1_xattn_b_d2v, L1_xattn_W_img, L1_xattn_b_img, L1_xattn_W_txt, L1_xattn_b_txt, L1_xattn_W_att0, L1_xattn_b_att0, L1_xattn_W_att1, L1_xattn_b_att1, L1_xattn_W_f1, L1_xattn_b_f1, L1_xattn_W_f2, L1_xattn_b_f2), axis=-1)
    x = _layernorm(x + _L1_ffn_ref(x, L1_ffn_gate_w, L1_ffn_w_gate, L1_ffn_w_up, L1_ffn_w_down), axis=-1)
    return x

_drawn_inputs = setup_inputs


def setup_inputs(seed=0):
    import zlib

    import numpy as np

    out = dict(_drawn_inputs(seed))
    spreads = {'L0_ffn_b1': (0.0, 0.8),
     'L0_ffn_b2': (0.0, 0.528),
     'L1_attn_A_real_log': (-0.6931471824645996, 0.2),
     'L1_attn_b_out': (0.0, 0.1),
     'L1_xattn_b_d2v': (0.0, 0.1),
     'L1_xattn_b_img': (0.0, 0.1),
     'L1_xattn_b_txt': (0.0, 0.1),
     'L1_xattn_b_att0': (0.0, 0.8),
     'L1_xattn_b_att1': (0.0, 0.8),
     'L1_xattn_b_f1': (0.0, 0.1),
     'L1_xattn_b_f2': (0.0, 0.1)}
    factors = {'L0_attn_W_off': 6.229,
     'L0_attn_b_off': 8.0,
     'L0_attn_W_attn': 7.706,
     'L0_attn_b_attn': 8.0,
     'L0_attn_b_out': 6.145,
     'L0_xattn_bq': 3.747,
     'L0_xattn_bk': 8.0,
     'L0_ffn_gate_w': 3.573,
     'L0_ffn_w1': 5.538,
     'L0_ffn_w2': 5.629,
     'L1_ffn_gate_w': 8.0,
     'L1_ffn_w_gate': 8.0,
     'L1_ffn_w_up': 8.0,
     'L1_ffn_w_down': 8.0}
    for name, (base, spread) in spreads.items():
        noise = np.random.default_rng([zlib.crc32(name.encode()), seed]).standard_normal(out[name].shape)
        drawn = base * np.exp(spread * noise) if base else spread * noise
        out[name] = jnp.asarray(drawn.astype(out[name].dtype))
    for name, factor in factors.items():
        out[name] = (out[name] * factor).astype(out[name].dtype)
    return out
```

```python
from contextlib import ExitStack

import numpy as np

import concourse.bass as bass
from concourse import mybir

F32 = mybir.dt.float32
BF16 = mybir.dt.bfloat16
ALU = mybir.AluOpType
ACT = mybir.ActivationFunctionType
AX = mybir.AxisListType
RADD = bass.bass_isa.ReduceOp.add
RMAX = bass.bass_isa.ReduceOp.max

P = 128
NT = 1024
TT = NT // P
HALF = 512
KV = 6404
KT = -(-KV // P)
KP = KT * P
CD = 96
TPB = 3
NB = KT // TPB
BLK = TPB * P
SUB = BLK // 2
LASTV = KV - (KT - 1) * P
NH, HD = 16, 8
NPAIR = NH // 2
HPO = 32
NE = 8
FF0, FF1 = 512, 256
NF = 1024
NS = 64
MAGIC = 12582912.0
TWO_PI = 6.283185307179586
TWO_PI_HI = 6.28125
TWO_PI_LO = TWO_PI - TWO_PI_HI
PI_BELOW = 3.1415925
LN2 = 0.6931471805599453
LN2_HI = 0.693359375
LN2_LO = LN2 - LN2_HI
EPS = 1e-5
BIG = 1.0e38
Q_PART = (0, 0, 1, 1, 0, 2)
K_PART = (0, 1, 0, 1, 2, 0)
SPLIT_ROWS = len(Q_PART) * HD
SCORE_ROWS = SPLIT_ROWS + 2


class Chain:

    def __init__(self, sem):
        self.sem, self.n = sem, 0

    def __call__(self, eng, ins):
        self.n += 1
        ins.then_inc(self.sem, 1)
        eng.wait_ge(self.sem, self.n)


class Machine:

    def __init__(self, nc, ctx, a):
        self.nc, self.ctx, self.a = nc, ctx, a
        self.stage_sems = []
        self.ps = ctx.enter_context(nc.psum_tensor("ps", [P, 8, 512], F32))
        self.ident = self.sb("ident", [P, P])
        self.identb = self.sb("identb", [P, P], BF16)
        self.ones_row = self.sb("ones_row", [1, HALF])
        self.eps = self.sb("eps", [P, 1])
        self.xtok = self.sb("xtok", [P, TT, P])
        self.xT = self.sb("xT", [P, NT])
        self.padm = self.sb("padm", [P, 1])
        self.dve = Chain(self.sem("dve_own"))
        self.act = Chain(self.sem("act_own"))
        self.pool = Chain(self.sem("pool_own"))
        self.stage_sems = []

    def sb(self, name, shape, dt=F32, ctx=None):
        return (ctx or self.ctx).enter_context(self.nc.sbuf_tensor(name + "_sb", shape, dt))

    def sem(self, name):
        self.stage_sems.append(self.nc.alloc_semaphore(name))
        return self.stage_sems[-1]

    def end_stage(self):
        self.nc.clear_and_free_semaphores(self.stage_sems)
        self.nc.all_engine_barrier()
        self.stage_sems = []


def setup(m):
    nc, a = m.nc, m.a
    loaded = m.sem("setup_loaded")
    with nc.Block() as block:
        @block.sync
        def _(sp):
            sp.dma_start(m.ident[:], a["c_ident"]).then_inc(loaded, 16)
            sp.dma_start(m.padm[:], a["c_pad"]).then_inc(loaded, 16)
            sp.dma_start(m.xtok[:], a["x_tok"].rearrange("(t p) d -> p t d", p=P)).then_inc(loaded, 16)
            sp.dma_start(m.xT[:], a["x_T"]).then_inc(loaded, 16)

        @block.vector
        def _(dve):
            nc.vector.memset(m.ones_row[:], 1.0)
            nc.vector.memset(m.eps[:], EPS)
            dve.wait_ge(loaded, 64)
            nc.vector.tensor_copy(m.identb[:], m.ident[:])


def layernorm(m, name, y, out=None):
    nc = m.nc
    with ExitStack() as ctx:
        res = m.sb(name + "_res", [P, TT, P], ctx=ctx)
        stats = m.sb(name + "_stats", [P, TT, 6], ctx=ctx)
        mv = m.sb(name + "_mv", [P, TT, 2], ctx=ctx)
        std = m.sb(name + "_std", [P, TT], ctx=ctx)
        rstd = m.sb(name + "_rstd", [P, TT], ctx=ctx)
        var_ready, std_ready, x_ready, xt_ps, stored = (
            m.sem(f"{name}_{s}") for s in ("var", "std", "x", "xt", "stored"))
        block = ctx.enter_context(nc.Block())

        @block.vector
        def _(dve):
            for g in range(2):
                m.dve(dve, nc.vector.tensor_tensor(res[:, 4 * g:4 * g + 4, :], y[:, 4 * g:4 * g + 4, :],
                                                   m.xtok[:, 4 * g:4 * g + 4, :], ALU.add))
            for t in range(TT):
                m.dve(dve, nc.vector.bn_stats(stats[:, t, :], res[:, t, :]))
            for t in range(TT):
                last = nc.vector.bn_aggr(mv[:, t, :], stats[:, t, :])
                last.then_inc(var_ready, 1)
            dve.wait_ge(std_ready, 1)
            m.dve(dve, nc.vector.reciprocal(rstd[:], std[:]))
            for t in range(TT):
                nc.vector.tensor_scalar(m.xtok[:, t, :], res[:, t, :], mv[:, t, 0:1], rstd[:, t:t + 1],
                                        ALU.subtract, ALU.mult).then_inc(x_ready, 1)
            if out is None:
                dve.wait_ge(xt_ps, 1)
                nc.vector.tensor_copy(m.xT[:, 0:HALF], m.ps[:, 6, :])

        @block.scalar
        def _(act):
            act.wait_ge(var_ready, TT)
            nc.scalar.activation(std[:], mv[:, :, 1], ACT.Sqrt, bias=m.eps[:, 0:1]).then_inc(std_ready, 1)
            if out is None:
                act.wait_ge(xt_ps, 2)
                nc.scalar.activation(m.xT[:, HALF:NT], m.ps[:, 7, :], ACT.Copy)

        @block.tensor
        def _(pe):
            if out is None:
                for t in range(TT):
                    pe.wait_ge(x_ready, t + 1)
                    ins = nc.tensor.transpose(m.ps[:, 6 + t // 4, (t % 4) * P:(t % 4 + 1) * P], m.xtok[:, t, :], m.ident[:])
                    if t % 4 == 3:
                        ins.then_inc(xt_ps, 1)

        @block.sync
        def _(sp):
            if out is not None:
                sp.wait_ge(x_ready, TT)
                sp.dma_start(out.rearrange("(t p) d -> p t d", p=P), m.xtok[:]).then_inc(stored, 16)
                sp.wait_ge(stored, 16)


def deform_attention(m):
    nc, a = m.nc, m.a
    with ExitStack() as ctx:
        def sb(name, shape, dt=F32):
            return m.sb("da_" + name, shape, dt, ctx)

        w = sb("w", [P, 2 * HPO])
        b = sb("b", [1, 2 * HPO])
        wout = sb("wout", [P, P])
        bout = sb("bout", [1, P])
        iota = sb("iota", [P, 1])
        ones = sb("ones", [P, HPO])
        sh = [P, TT, HPO]
        lg, off, mag, fl, gt, sg, neg, idx, prob = (sb(n, sh) for n in ("lg", "off", "mag", "fl", "gt", "sg", "neg", "idx", "prob"))
        mx, den = sb("mx", [P, TT * 8]), sb("den", [P, TT * 8])
        x0r = sb("x0r", [P, 1])
        zx = [sb(f"zx{s}", [P, P + HPO], BF16) for s in range(3)]
        flip = sb("flip", [HPO, HPO])
        sel = sb("sel", [HPO, HPO, P], BF16)
        idxT = sb("idxT", [HPO, NT], BF16)
        wT = sb("wT", [HPO, NT])
        hot = sb("hot", [P, 2, HALF], BF16)
        gw = sb("gw", [HPO, NT])
        cs = sb("cs", [HPO, P])
        loaded, proj, lg_ready, e_ready, t_ready, tps, oh_in, bc, oh, cs_ps, gsum, gw_ready = (
            m.sem("da_" + s) for s in ("loaded", "proj", "lg", "exp", "tok", "tps", "ohin", "bcast", "onehot", "cs", "gsum", "gw"))
        op = m.ps[:, 0, :].rearrange("p (t c) -> p t c", t=TT)

        def g4(t):
            return t[:].rearrange("p t (h q) -> p (t h) q", q=4)

        def b4(t):
            return t[:].unsqueeze(2).to_broadcast([P, TT * 8, 4])

        with nc.Block() as block:
            @block.sync
            def _(sp):
                for dst, src in ((w, "da_w"), (b, "da_b"), (wout, "da_wout"), (bout, "da_bout"), (iota, "c_iota"),
                                 (flip, "c_flip")):
                    sp.dma_start(dst[:], a[src]).then_inc(loaded, 16)

            @block.tensor
            def _(pe):
                pe.wait_ge(loaded, 96)
                for t in range(TT):
                    nc.tensor.matmul(op[:, t, :], m.xT[:, t * P:(t + 1) * P], w[:], start=True, stop=False)
                    nc.tensor.matmul(op[:, t, :], m.ones_row[0:1, 0:P], b[:], start=False, stop=True).then_inc(proj, 1)
                pe.wait_ge(t_ready, 2)
                for t in range(TT):
                    c = slice((t % 4) * P, (t % 4 + 1) * P)
                    nc.tensor.transpose(m.ps[0:HPO, 1 + t // 4, c], idx[:, t, :], m.ident[:])
                    nc.tensor.transpose(m.ps[0:HPO, 3 + t // 4, c], prob[:, t, :], m.ident[:]).then_inc(tps, 1)
                pe.wait_ge(oh_in, 1)
                nc.tensor.matmul(m.ps[0:HPO, 5, 0:P], ones[:], wout[:], start=True, stop=True).then_inc(cs_ps, 1)

            @block.vector
            def _(dve):
                def own(ins):
                    m.dve(dve, ins)

                nc.vector.memset(ones[:], 1.0).then_inc(oh_in, 1)
                for z in zx:
                    own(nc.vector.memset(z[:], 0.0))
                own(nc.vector.tensor_copy(zx[0][:, HPO - 1:HPO], m.xT[:, 0:1]))
                own(nc.vector.tensor_tensor(x0r[:], m.xT[:, 0:1], zx[0][:, HPO - 1:HPO], ALU.subtract))
                own(nc.vector.tensor_copy(zx[1][:, HPO - 1:HPO], x0r[:]))
                own(nc.vector.tensor_tensor(zx[2][:, HPO - 1:HPO], x0r[:], zx[1][:, HPO - 1:HPO], ALU.subtract))
                dve.wait_ge(loaded, 96)
                own(nc.vector.tensor_copy(sel[:], flip[:].unsqueeze(2).to_broadcast([HPO, HPO, P])))
                dve.wait_ge(proj, TT)
                own(nc.vector.tensor_copy(lg[:], op[:, :, HPO:2 * HPO]))
                own(nc.vector.tensor_reduce(mx[:], g4(lg), AX.X, ALU.max))
                nc.vector.tensor_tensor(g4(lg), g4(lg), b4(mx), ALU.subtract).then_inc(lg_ready, 1)
                own(nc.vector.tensor_copy(off[:], op[:, :, 0:HPO]))
                own(nc.vector.scalar_tensor_tensor(mag[:], off[:], -1.0, off[:], ALU.mult, ALU.max))
                own(nc.vector.tensor_scalar(mag[:], mag[:], 1000.0, None, ALU.min))
                own(nc.vector.tensor_scalar(fl[:], mag[:], MAGIC, MAGIC, ALU.add, ALU.subtract))
                own(nc.vector.tensor_tensor(gt[:], fl[:], mag[:], ALU.is_gt))
                own(nc.vector.tensor_tensor(fl[:], fl[:], gt[:], ALU.subtract))
                own(nc.vector.tensor_scalar(sg[:], off[:], 0.0, -2.0, ALU.is_lt, ALU.mult))
                own(nc.vector.tensor_scalar(sg[:], sg[:], 1.0, None, ALU.add))
                own(nc.vector.tensor_tensor(fl[:], fl[:], sg[:], ALU.mult))
                own(nc.vector.tensor_scalar(neg[:], fl[:], 0.0, float(P), ALU.is_lt, ALU.mult))
                own(nc.vector.tensor_tensor(fl[:], fl[:], neg[:], ALU.add))
                nc.vector.tensor_scalar(idx[:], fl[:], 0.0, float(P - 1), ALU.max, ALU.min).then_inc(t_ready, 1)
                dve.wait_ge(e_ready, 1)
                own(nc.vector.tensor_reduce(den[:], g4(lg), AX.X, ALU.add))
                own(nc.vector.reciprocal(den[:], den[:]))
                nc.vector.tensor_tensor(g4(prob), g4(lg), b4(den), ALU.mult).then_inc(t_ready, 1)
                dve.wait_ge(tps, TT)
                nc.vector.tensor_copy(idxT[:], m.ps[0:HPO, 1:3, :].rearrange("p a b -> p (a b)"))
                nc.vector.tensor_copy(wT[:], m.ps[0:HPO, 3:5, :].rearrange("p a b -> p (a b)"))
                dve.wait_ge(cs_ps, 1)
                nc.vector.tensor_copy(cs[:], m.ps[0:HPO, 5, 0:P])

            @block.scalar
            def _(act):
                act.wait_ge(lg_ready, 1)
                nc.scalar.activation(lg[:], lg[:], ACT.Exp).then_inc(e_ready, 1)

        with nc.Block() as block:
            @block.tensor
            def _(pe):
                for h in range(2):
                    nc.tensor.matmul(m.ps[:, 2 + h, :], zx[0][0:HPO, HPO:HPO + P], idxT[:, 0:HALF], start=True, stop=False)
                with pe.Fori(0, HPO) as k:
                    for h in range(2):
                        nc.tensor.matmul(m.ps[:, h, :], sel[:, bass.ds(k, 1), :].rearrange("p a b -> p (a b)"),
                                         idxT[:, h * HALF:(h + 1) * HALF], start=True, stop=True).then_inc(bc, 1)
                    for h in range(2):
                        pe.wait_ge(oh, k * 2 + h + 1)
                        for s in range(3):
                            ins = nc.tensor.matmul(m.ps[:, 2 + h, :], zx[s][:, bass.ds(k, P)],
                                                   hot[:, h, :], start=False, stop=False)
                        ins.then_inc(gsum, 1)
                for h in range(2):
                    nc.tensor.matmul(m.ps[:, 2 + h, :], zx[0][0:HPO, HPO:HPO + P], idxT[:, 0:HALF],
                                     start=False, stop=True).then_inc(gsum, 1)
                pe.wait_ge(gw_ready, 1)
                for t in range(TT):
                    o = m.ps[:, 4 + t // 4, (t % 4) * P:(t % 4 + 1) * P]
                    nc.tensor.matmul(o, gw[:, t * P:(t + 1) * P], cs[:], start=True, stop=False)
                    nc.tensor.matmul(o, m.ones_row[0:1, 0:P], bout[:], start=False, stop=True)

            @block.vector
            def _(dve):
                with dve.Fori(0, HPO) as k:
                    for h in range(2):
                        dve.wait_ge(bc, k * 2 + h + 1)
                        nc.vector.tensor_scalar(hot[:, h, :], m.ps[:, h, :], iota[:, 0:1], None, ALU.is_equal).then_inc(oh, 1)
                dve.wait_ge(gsum, 2 * HPO + 2)
                nc.vector.tensor_tensor(gw[:], m.ps[0:HPO, 2:4, :].rearrange("p a b -> p (a b)"), wT[:], ALU.mult).then_inc(gw_ready, 1)
        layernorm(m, "ln0", m.ps[:, 4:6, :].rearrange("p a (b c) -> p (a b) c", c=P))


def split3(m, dve, src, p1, p2, p3, rest, done):
    nc = m.nc
    m.dve(dve, nc.vector.tensor_copy(p1, src))
    m.dve(dve, nc.vector.tensor_tensor(rest, src, p1, ALU.subtract))
    m.dve(dve, nc.vector.tensor_copy(p2, rest))
    nc.vector.tensor_tensor(p3, rest, p2, ALU.subtract).then_inc(done, 1)


def cross_attention(m):
    nc, a = m.nc, m.a
    with ExitStack() as ctx:
        def sb(name, shape, dt=F32, c=ctx):
            return m.sb("ca_" + name, shape, dt, c)

        sem = {n: m.sem("ca_" + n) for n in (
            "loaded", "k_ps", "k_sb", "k_parts", "k_stored0", "k_stored1", "v_ps", "v_sb", "ones", "k_stacked", "q_ps", "q_sb", "q_parts",
            "q_stored", "q_stacked", "cleared")}
        ao = sb("ao", [P, NPAIR, HALF])
        c0 = ctx.enter_context(ExitStack())
        ks = sb("ks", [P, NPAIR * KP], BF16, c0)
        vs = sb("vs", [P, KT, NH, HD + 1], F32, c0)
        qs = sb("qs", [P, NPAIR * NT], BF16, c0)
        kd = nc.dram_tensor("k_parts", (3, P, KP), BF16, kind="Internal").ap()
        qd = nc.dram_tensor("q_parts", (3, P, NT), BF16, kind="Internal").ap()
        chunks = [(c * HALF, min(HALF, KP - c * HALF)) for c in range(-(-KP // HALF))]

        with ExitStack() as c1:
            ctxT = sb("ctxT", [CD + 1, KP], F32, c1)
            wk = sb("wk", [CD + 1, P], F32, c1)
            wv = sb("wv", [CD + 1, P], F32, c1)
            wq = sb("wq", [P, P], F32, c1)
            bq = sb("bq", [P, 1], F32, c1)
            k32 = ao[:, 0:2, :]
            rest = ao[:, 2, :]
            kp = ao[:, 3:6, :].rearrange("p a b -> p (a b)").bitcast(BF16).rearrange("p (i s n) -> p i s n", i=2, s=3)
            block = c1.enter_context(nc.Block())
            n_k = len(chunks)

            @block.sync
            def _(sp):
                sp.dma_start(ctxT[0:CD, 0:KV], a["ctx_T"]).then_inc(sem["loaded"], 16)
                sp.dma_start(ctxT[0:CD, KV:KP], a["ctx_T"][:, 0:KP - KV]).then_inc(sem["loaded"], 16)
                for dst, src in ((wk, "ca_wk"), (wv, "ca_wv"), (wq, "ca_wq"), (bq, "ca_bq")):
                    sp.dma_start(dst[:], a[src]).then_inc(sem["loaded"], 16)
                for i, (c, n) in enumerate(chunks):
                    sp.wait_ge(sem["k_parts"], i + 1)
                    sp.dma_start(kd[:, :, c:c + n].rearrange("s p n -> p s n"), kp[:, i % 2, :, 0:n]).then_inc(sem[f"k_stored{i % 2}"], 16)
                for i in range(2):
                    sp.wait_ge(sem["k_parts"], n_k + i + 1)
                    sp.dma_start(qd[:, :, i * HALF:(i + 1) * HALF].rearrange("s p n -> p s n"),
                                 kp[:, (n_k + i) % 2, :, :]).then_inc(sem[f"k_stored{(n_k + i) % 2}"], 16)
                sp.wait_ge(sem["k_stored0"], 16 * ((n_k + 3) // 2))
                sp.wait_ge(sem["k_stored1"], 16 * ((n_k + 2) // 2))
                sp.wait_ge(sem["cleared"], 2)
                for part in range(len(Q_PART)):
                    for h in range(2):
                        r = 64 * h + HD * part
                        sp.dma_start(ks[r:r + HD, :].rearrange("p (g n) -> p g n", g=NPAIR),
                                     kd[K_PART[part]].rearrange("(g h d) n -> h d g n", h=2, d=HD)[h]).then_inc(sem["k_stacked"], 16)
                        sp.dma_start(qs[r:r + HD, :].rearrange("p (g n) -> p g n", g=NPAIR),
                                     qd[Q_PART[part]].rearrange("(g h d) n -> h d g n", h=2, d=HD)[h]).then_inc(sem["q_stacked"], 16)
                sp.wait_ge(sem["k_stacked"], 16 * 12)
                sp.wait_ge(sem["q_stacked"], 16 * 12)

            @block.tensor
            def _(pe):
                pe.wait_ge(sem["loaded"], 96)
                pe.wait_ge(sem["ones"], 1)
                for i, (c, n) in enumerate(chunks):
                    if i >= 2:
                        pe.wait_ge(sem["k_sb"], i - 1)
                    nc.tensor.matmul(m.ps[:, i % 2, 0:n], wk[:], ctxT[:, c:c + n], start=True, stop=True).then_inc(sem["k_ps"], 1)
                for h in range(2):
                    i = n_k + h
                    pe.wait_ge(sem["k_sb"], i - 1)
                    nc.tensor.matmul(m.ps[:, i % 2, :], wq[:], m.xT[:, h * HALF:(h + 1) * HALF],
                                     start=True, stop=True).then_inc(sem["k_ps"], 1)
                for t in range(KT):
                    if t % 4 == 0 and t >= 8:
                        pe.wait_ge(sem["v_sb"], t // 4 - 1)
                    ins = nc.tensor.matmul(m.ps[:, 2 + t // 4 % 2, (t % 4) * P:(t % 4 + 1) * P], ctxT[:, t * P:(t + 1) * P], wv[:],
                                           start=True, stop=True)
                    if t % 4 == 3 or t == KT - 1:
                        ins.then_inc(sem["v_ps"], 1)

            @block.scalar
            def _(act):
                act.wait_ge(sem["loaded"], 96)
                for i, (c, n) in enumerate(chunks + [(0, HALF), (HALF, HALF)]):
                    act.wait_ge(sem["k_ps"], i + 1)
                    if i >= 2:
                        act.wait_ge(sem["k_parts"], i - 1)
                    if i < n_k:
                        nc.scalar.activation(k32[:, i % 2, 0:n], m.ps[:, i % 2, 0:n], ACT.Identity).then_inc(sem["k_sb"], 1)
                    else:
                        nc.scalar.activation(k32[:, i % 2, :], m.ps[:, i % 2, :], ACT.Identity, bias=bq[:, 0:1]).then_inc(sem["k_sb"], 1)
                for g in range(-(-KT // 4)):
                    n = min(4, KT - 4 * g)
                    act.wait_ge(sem["v_ps"], g + 1)
                    ins = nc.scalar.activation(vs[:, 4 * g:4 * g + n, :, 0:HD],
                                               m.ps[:, 2 + g % 2, 0:n * P].rearrange("p (t h d) -> p t h d", h=NH, d=HD), ACT.Copy)
                    ins.then_inc(sem["v_sb"], 1)

            @block.vector
            def _(dve):
                nc.vector.memset(ctxT[CD:CD + 1, :], 1.0).then_inc(sem["ones"], 1)
                nc.vector.memset(qs[:], 0.0).then_inc(sem["cleared"], 1)
                for i, (c, n) in enumerate(chunks + [(0, HALF), (HALF, HALF)]):
                    dve.wait_ge(sem["k_sb"], i + 1)
                    if i >= 2:
                        dve.wait_ge(sem[f"k_stored{i % 2}"], 16 * (i // 2))
                    split3(m, dve, k32[:, i % 2, 0:n], kp[:, i % 2, 0, 0:n], kp[:, i % 2, 1, 0:n], kp[:, i % 2, 2, 0:n],
                           rest[:, 0:n], sem["k_parts"])
                    dve.wait_ge(sem["k_parts"], i + 1)
                dve.wait_ge(sem["v_sb"], -(-KT // 4))
                m.dve(dve, nc.vector.memset(vs[:, :, :, HD:HD + 1], 1.0))
                nc.vector.tensor_scalar(vs[:, KT - 1, :, :], vs[:, KT - 1, :, :], m.padm[:, 0:1], None, ALU.mult)

            @block.gpsimd
            def _(pool):
                nc.gpsimd.memset(ks[:], 1.0).then_inc(sem["cleared"], 1)

        attention_loop(m, c0, ks, vs, qs, ao)
        c0.close()

        with ExitStack() as c2:
            rec = sb("rec", [P, 2, 16], F32, c2)
            att = sb("att", [P, TT, P], F32, c2)
            attT = sb("attT", [P, NT], F32, c2)
            wo = sb("wo", [P, P], F32, c2)
            bo = sb("bo", [1, P], F32, c2)
            tr, nrm, atr, acp, ld = (m.sem("ca_" + s) for s in ("o_tr", "o_nrm", "o_atr", "o_acp", "o_loaded"))
            block = c2.enter_context(nc.Block())

            @block.sync
            def _(sp):
                sp.dma_start(wo[:], a["ca_wo"]).then_inc(ld, 16)
                sp.dma_start(bo[:], a["ca_bo"]).then_inc(ld, 16)

            @block.tensor
            def _(pe):
                for g in range(NPAIR):
                    if g >= 2:
                        pe.wait_ge(nrm, 2 * (g - 1))
                    for c in range(4):
                        ins = nc.tensor.transpose(m.ps[:, g % 2, c * P:(c + 1) * P], ao[:, g, c * P:(c + 1) * P], m.ident[:])
                    ins.then_inc(tr, 1)
                pe.wait_ge(nrm, 2 * NPAIR)
                for t in range(TT):
                    ins = nc.tensor.transpose(m.ps[:, 2 + t // 4, (t % 4) * P:(t % 4 + 1) * P], att[:, t, :], m.ident[:])
                ins.then_inc(atr, 1)
                pe.wait_ge(acp, 2)
                pe.wait_ge(ld, 32)
                for t in range(TT):
                    o = m.ps[:, 4 + t // 4, (t % 4) * P:(t % 4 + 1) * P]
                    nc.tensor.matmul(o, attT[:, t * P:(t + 1) * P], wo[:], start=True, stop=False)
                    nc.tensor.matmul(o, m.ones_row[0:1, 0:P], bo[:], start=False, stop=True)

            @block.vector
            def _(dve):
                for g in range(NPAIR):
                    dve.wait_ge(tr, g + 1)
                    t = m.ps[:, g % 2, :].rearrange("p (c k r) -> p c k r", c=4, k=4)
                    r = rec[:, g % 2, :].rearrange("p (c k) -> p c k", c=4)
                    m.dve(dve, nc.vector.reciprocal(r.unsqueeze(3), t[:, :, :, HD:HD + 1]))
                    for h in range(2):
                        o = att[:, :, (2 * g + h) * HD:(2 * g + h + 1) * HD].rearrange("p (a c) d -> p c a d", a=2)
                        nc.vector.tensor_tensor(o, t[:, :, 2 * h:2 * h + 2, 0:HD],
                                                r[:, :, 2 * h:2 * h + 2].unsqueeze(3).to_broadcast([P, 4, 2, HD]),
                                                ALU.mult).then_inc(nrm, 1)
                dve.wait_ge(atr, 1)
                nc.vector.tensor_copy(attT[:, 0:HALF], m.ps[:, 2, :]).then_inc(acp, 1)

            @block.scalar
            def _(act):
                act.wait_ge(atr, 1)
                nc.scalar.activation(attT[:, HALF:NT], m.ps[:, 3, :], ACT.Copy).then_inc(acp, 1)
    layernorm(m, "ln1", m.ps[:, 4:6, :].rearrange("p a (b c) -> p (a b) c", c=P))


def attention_loop(m, ctx, ks, vs, qs, ao):
    nc = m.nc

    def sb(name, shape, dt=F32):
        return m.sb("at_" + name, shape, dt, ctx)

    def sem(name):
        return m.sem("at_" + name)

    kb = [sb(f"kb{t}", [P, P], BF16) for t in range(TPB)]
    vb = [sb(f"vb{t}", [P, 2, 32]) for t in range(TPB)]
    ka = [sb(f"ka{j}", [P, SUB], BF16) for j in range(2)]
    qa, qb = sb("qa", [P, NT], BF16), sb("qb", [P, NT], BF16)
    prob = sb("prob", [P, 12, HALF])
    zero = sb("zero", [P, HALF], BF16)
    mx = sb("mx", [P, 16, 2 * NB])
    top = sb("top", [P, 16])
    hl = sb("hl", [P, 2, 2, TT], BF16)
    mt = sb("mt", [32, P], BF16)
    (ready0, kb_ready, ka_ready, qa_ready, qb_ready, scores, probs, b_used, a_scores, a_maxed, pv_done, pv_free,
     fin, hl_ready, mt_ps, mt_ready, mrow) = (sem(n) for n in (
         "init", "kb_ready", "ka_ready", "qa_ready", "qb_ready", "scores", "probs", "b_used", "a_scores", "a_maxed",
         "pv_done", "pv_free", "fin", "hl_ready", "mt_ps", "mt_ready", "mrow"))
    S = [m.ps[:, i, :] for i in range(3)]
    A = [m.ps[:, 3 + 2 * u:5 + 2 * u, :].rearrange("p a (b c) -> p (a b) c", b=2)[:, :, 0:SUB] for u in range(2)]
    PV = m.ps[:, 7, :]
    mt_bank = m.ps[0:32, 3, 0:P // 2].bitcast(BF16)
    FREE_S, FREE_B, FREE_A, FREE_K = 3, TPB, 2, 5
    scale = float(np.float32(1.0) / np.sqrt(np.float32(HD)))
    block = ctx.enter_context(nc.Block())

    @block.tensor
    def _(pe):
        def score_step(ib, i):
            t, h, half = i // 4, i // 2 % 2, i % 2
            r = 64 * h
            if i % 4 == 0:
                pe.wait_ge(kb_ready, ib * (2 * TPB) + 2 * t + 2)
            pe.wait_ge(probs, ib * 12 + i + 1)
            nc.tensor.matmul(S[i % 3], kb[t][r:r + SCORE_ROWS, :], qb[r:r + SCORE_ROWS, half * HALF:(half + 1) * HALF],
                             start=True, stop=True).then_inc(scores, 1)

        def value_step(ib, t):
            pe.wait_ge(probs, ib * 12 + 4 * t + 4 + FREE_S)
            for k in range(4):
                ins = nc.tensor.matmul(PV[32 * k:32 * k + 32, :], vb[t][:, k // 2, :], prob[:, 4 * t + k, :],
                                       start=False, stop=False)
            ins.then_inc(b_used, 1)

        def max_step(ia, u):
            if u % 4 == 0:
                pe.wait_ge(ka_ready, ia * 2 + u // 4 + 1)
            pe.wait_ge(a_maxed, ia * 8 + u + 1)
            for n in range(4):
                q = 4 * (u % 4) + n
                r = 64 * (q // TT)
                ins = nc.tensor.matmul(A[u % 2][:, n, :], qa[r:r + SPLIT_ROWS, q % TT * P:(q % TT + 1) * P],
                                       ka[u // 4][r:r + SPLIT_ROWS, :], start=True, stop=True)
            ins.then_inc(a_scores, 1)

        def both(ib, ia):
            for kind, i in (("s", 0), ("s", 1), ("s", 2), ("m", 0), ("s", 3), ("m", 1), ("s", 4), ("s", 5), ("v", 0),
                            ("s", 6), ("m", 2), ("s", 7), ("m", 3), ("s", 8), ("m", 4), ("s", 9), ("v", 1), ("s", 10),
                            ("m", 5), ("s", 11), ("m", 6), ("m", 7), ("v", 2)):
                if kind == "s":
                    score_step(ib, i)
                elif kind == "v":
                    value_step(ib, i)
                elif ia is not None:
                    max_step(ia, i)

        def open_pair(g):
            pe.wait_ge(qb_ready, g + 1)
            pe.wait_ge(pv_free, g + 1)
            for k in range(4):
                nc.tensor.matmul(PV[32 * k:32 * k + 32, :], zero[:, 0:32], zero[:], start=True, stop=False)

        def close_pair():
            for k in range(4):
                ins = nc.tensor.matmul(PV[32 * k:32 * k + 32, :], zero[:, 0:32], zero[:], start=False, stop=True)
            ins.then_inc(pv_done, 1)

        def flip_maximum(ga):
            pe.wait_ge(hl_ready, ga + 1)
            nc.tensor.transpose(mt_bank, hl[:].rearrange("p a b c -> p (a b c)"), m.identb[:]).then_inc(mt_ps, 1)

        pe.wait_ge(ready0, 4)
        pe.sem_inc(b_used, FREE_B)
        pe.sem_inc(a_scores, FREE_K)
        pe.wait_ge(qa_ready, 1)
        with pe.Fori(0, NB) as c:
            for u in range(8):
                max_step(c, u)
        flip_maximum(0)
        with pe.Fori(0, NPAIR - 1) as g:
            pe.wait_ge(qa_ready, g + 2)
            pe.wait_ge(mt_ready, g + 1)
            open_pair(g)
            with pe.Fori(0, NB) as c:
                both(g * NB + c, g * NB + c + NB)
            close_pair()
            flip_maximum(g + 1)
        open_pair(NPAIR - 1)
        with pe.Fori(0, NB) as c:
            both(c + (NPAIR - 1) * NB, None)
        close_pair()

    @block.scalar
    def _(act):
        act.sem_inc(probs, FREE_S)
        act.sem_inc(pv_free, 1)
        with act.Fori(0, NPAIR) as g:
            with act.Fori(0, NB) as c:
                ib = g * NB + c
                for i in range(12):
                    if i % 4 == 0:
                        act.wait_ge(b_used, ib * TPB + i // 4 + 1)
                    act.wait_ge(scores, ib * 12 + i + 1)
                    nc.scalar.activation(prob[:, i, :], S[i % 3], ACT.Exp, scale=scale).then_inc(probs, 1)
            act.wait_ge(pv_done, g + 1)
            nc.scalar.activation(ao[:, bass.ds(g, 1), :].rearrange("p a b -> p (a b)"), PV, ACT.Copy).then_inc(pv_free, 1)

    @block.vector
    def _(dve):
        def reduce_steps(ia, c):
            for u in range(8):
                dve.wait_ge(a_scores, ia * 8 + u + 1 + FREE_K)
                nc.vector.tensor_reduce(mx[:, 4 * (u % 4):4 * (u % 4) + 4, bass.ds(c * 2 + u // 4, 1)], A[u % 2],
                                        AX.X, ALU.max).then_inc(a_maxed, 1)

        def finish_maximum(ga):
            dve.wait_ge(a_maxed, ga * (8 * NB) + 8 * NB + FREE_A)
            nc.vector.tensor_reduce(top[:], mx[:], AX.X, ALU.max).then_inc(fin, 1)
            t2 = top[:].rearrange("p (h q) -> p h q", h=2)
            dve.wait_ge(fin, ga * 2 + 1)
            nc.vector.tensor_scalar(hl[:, :, 0, :], t2, -1.0, None, ALU.mult).then_inc(fin, 1)
            dve.wait_ge(fin, ga * 2 + 2)
            nc.vector.scalar_tensor_tensor(hl[:, :, 1, :], t2, -1.0, hl[:, :, 0, :], ALU.mult, ALU.subtract).then_inc(hl_ready, 1)
            dve.wait_ge(mt_ps, ga + 1)
            if not isinstance(ga, int):
                dve.wait_ge(mrow, ga * 32)
            nc.vector.tensor_copy(mt[:], mt_bank).then_inc(mt_ready, 1)

        for z in vb:
            nc.vector.memset(z[:], 0.0).then_inc(ready0, 1)
        nc.vector.memset(zero[:], 0.0).then_inc(ready0, 1)
        dve.sem_inc(a_maxed, FREE_A)
        with dve.Fori(0, NB) as c:
            reduce_steps(c, c)
        finish_maximum(0)
        with dve.Fori(0, NPAIR - 1) as g:
            with dve.Fori(0, NB) as c:
                reduce_steps(g * NB + c + NB, c)
            finish_maximum(g + 1)

    @block.gpsimd
    def _(pool):
        def stage_queries_max(ga):
            pool.wait_ge(a_scores, ga * (8 * NB) + FREE_K)
            nc.gpsimd.tensor_copy(qa[:], qs[:, bass.ds(ga * NT, NT)]).then_inc(qa_ready, 1)

        def stage_queries(g):
            pool.wait_ge(mrow, g * 32 + 32)
            pool.wait_ge(b_used, g * (TPB * NB) + FREE_B)
            nc.gpsimd.tensor_copy(qb[:], qs[:, bass.ds(g * NT, NT)]).then_inc(qb_ready, 1)

        def stage_tile(g, c, ib, t):
            pool.wait_ge(b_used, ib * TPB + t + 1)
            nc.gpsimd.tensor_copy(kb[t][:], ks[:, bass.ds(g * KP + c * BLK + t * P, P)]).then_inc(kb_ready, 1)
            nc.gpsimd.tensor_copy(vb[t][:, :, 0:HD + 1],
                                  vs[:].rearrange("p t h d -> p (t h) d")[:, bass.ds(c * (TPB * NH) + g * 2 + t * NH, 2), :]).then_inc(kb_ready, 1)

        def stage_sub(ga, c, ia, j):
            pool.wait_ge(a_scores, ia * 8 + 4 * j + 1)
            nc.gpsimd.tensor_copy(ka[j][:], ks[:, bass.ds(ga * KP + c * BLK + j * SUB, SUB)]).then_inc(ka_ready, 1)

        pool.wait_ge(ready0, 4)
        stage_queries_max(0)
        with pool.Fori(0, NB) as c:
            for j in range(2):
                stage_sub(0, c, c, j)
        with pool.Fori(0, NPAIR - 1) as g:
            stage_queries_max(g + 1)
            stage_queries(g)
            with pool.Fori(0, NB) as c:
                ib = g * NB + c
                stage_tile(g, c, ib, 0)
                stage_sub(g + 1, c, ib + NB, 0)
                stage_tile(g, c, ib, 1)
                stage_sub(g + 1, c, ib + NB, 1)
                stage_tile(g, c, ib, 2)
        stage_queries(NPAIR - 1)
        with pool.Fori(0, NB) as c:
            for t in range(TPB):
                stage_tile(NPAIR - 1, c, c + (NPAIR - 1) * NB, t)

    @block.sync
    def _(sp):
        with sp.Fori(0, NPAIR) as ga:
            sp.wait_ge(mt_ready, ga + 1)
            for h in range(2):
                r = 64 * h + SPLIT_ROWS
                sp.dma_start(qs[r:r + 2, bass.ds(ga * NT, NT)], mt[16 * h:16 * h + 16, :]).then_inc(mrow, 16)
        sp.wait_ge(mrow, 32 * NPAIR)


def first_mask(m, dve, src, top, rev, tmp, tmp_top, mask):
    nc = m.nc

    def wide(t):
        return t[:].unsqueeze(2).to_broadcast([P, TT, NE])

    m.dve(dve, nc.vector.tensor_tensor(tmp[:], src[:], wide(top), ALU.is_equal))
    m.dve(dve, nc.vector.tensor_tensor(tmp[:], tmp[:], rev[:].unsqueeze(1).to_broadcast([P, TT, NE]), ALU.mult))
    m.dve(dve, nc.vector.tensor_reduce(tmp_top[:], tmp[:], AX.X, ALU.max))
    m.dve(dve, nc.vector.tensor_tensor(mask[:], tmp[:], wide(tmp_top), ALU.is_equal))


def route(m, name, gate_key, top_k, wide_w):
    nc, a = m.nc, m.a
    with ExitStack() as ctx:
        def sb(n, shape):
            return m.sb(f"{name}_{n}", shape, F32, ctx)

        gate, rev, sel = sb("gate", [P, NE]), sb("rev", [P, NE]), sb("sel", [NE, NE, P])
        lg, ex, tmp, mask, mask2, w = (sb(n, [P, TT, NE]) for n in ("lg", "ex", "tmp", "mask", "mask2", "w"))
        top, top2, t1, t2, t3 = (sb(n, [P, TT]) for n in ("top", "top2", "t1", "t2", "t3"))
        wT = sb("wT", [NE, NT])
        loaded, logits, ex_in, ex_out, w_ready, w_ps, w_rows, wide_ps, wide_sb = (
            m.sem(f"{name}_{s}") for s in ("loaded", "logits", "exin", "exout", "w", "wps", "wrows", "wideps", "widesb"))
        lp = m.ps[:, 0, 0:TT * NE].rearrange("p (t e) -> p t e", e=NE)

        def wide(t):
            return t[:].unsqueeze(2).to_broadcast([P, TT, NE])

        block = ctx.enter_context(nc.Block())

        @block.sync
        def _(sp):
            sp.dma_start(gate[:], a[gate_key]).then_inc(loaded, 16)
            sp.dma_start(rev[:], a["c_rev"]).then_inc(loaded, 16)

        @block.tensor
        def _(pe):
            pe.wait_ge(loaded, 32)
            for t in range(TT):
                ins = nc.tensor.matmul(lp[:, t, :], m.xT[:, t * P:(t + 1) * P], gate[:], start=True, stop=True)
            ins.then_inc(logits, 1)
            pe.wait_ge(w_ready, 1)
            for t in range(TT):
                ins = nc.tensor.transpose(m.ps[0:NE, 1 + t // 4, t % 4 * P:(t % 4 + 1) * P], w[:, t, :], m.ident[:])
            ins.then_inc(w_ps, 1)
            pe.wait_ge(w_rows, 2)
            for i in range(2 * NE):
                e, h = i // 2, i % 2
                if i >= 4:
                    pe.wait_ge(wide_sb, i - 3)
                nc.tensor.matmul(m.ps[:, 4 + i % 4, :], sel[:, e, :], wT[:, h * HALF:(h + 1) * HALF],
                                 start=True, stop=True).then_inc(wide_ps, 1)

        @block.vector
        def _(dve):
            def own(ins):
                m.dve(dve, ins)

            nc.vector.tensor_copy(sel[:], m.ident[0:NE, 0:NE].unsqueeze(2).to_broadcast([NE, NE, P])).then_inc(w_rows, 1)
            dve.wait_ge(loaded, 32)
            dve.wait_ge(logits, 1)
            own(nc.vector.tensor_copy(lg[:], lp))
            own(nc.vector.tensor_reduce(top[:], lg[:], AX.X, ALU.max))
            if top_k == 1:
                first_mask(m, dve, lg, top, rev, tmp, t1, mask)
                nc.vector.tensor_tensor(ex[:], lg[:], wide(top), ALU.subtract).then_inc(ex_in, 1)
                dve.wait_ge(ex_out, 1)
                own(nc.vector.tensor_reduce(t2[:], ex[:], AX.X, ALU.add))
                own(nc.vector.reciprocal(t3[:], t2[:]))
                nc.vector.tensor_tensor(w[:], mask[:], wide(t3), ALU.mult).then_inc(w_ready, 1)
            else:
                first_mask(m, dve, lg, top, rev, tmp, t1, mask)
                own(nc.vector.scalar_tensor_tensor(lg[:], mask[:], -BIG, lg[:], ALU.mult, ALU.add))
                own(nc.vector.tensor_reduce(top2[:], lg[:], AX.X, ALU.max))
                first_mask(m, dve, lg, top2, rev, tmp, t1, mask2)
                nc.vector.tensor_tensor(t2[:], top2[:], top[:], ALU.subtract).then_inc(ex_in, 1)
                dve.wait_ge(ex_out, 1)
                own(nc.vector.tensor_scalar(t1[:], t3[:], 1.0, None, ALU.add))
                own(nc.vector.reciprocal(t1[:], t1[:]))
                own(nc.vector.tensor_tensor(t2[:], t3[:], t1[:], ALU.mult))
                own(nc.vector.tensor_tensor(mask[:], mask[:], wide(t1), ALU.mult))
                own(nc.vector.tensor_tensor(mask2[:], mask2[:], wide(t2), ALU.mult))
                nc.vector.tensor_tensor(w[:], mask[:], mask2[:], ALU.add).then_inc(w_ready, 1)
            dve.wait_ge(w_ps, 1)
            nc.vector.tensor_copy(wT[:], m.ps[0:NE, 1:3, :].rearrange("p a b -> p (a b)")).then_inc(w_rows, 1)

        @block.scalar
        def _(act):
            act.wait_ge(ex_in, 1)
            if top_k == 1:
                nc.scalar.activation(ex[:], ex[:], ACT.Exp).then_inc(ex_out, 1)
            else:
                nc.scalar.activation(t3[:], t2[:], ACT.Exp).then_inc(ex_out, 1)
            for i in range(2 * NE):
                act.wait_ge(wide_ps, i + 1)
                nc.scalar.activation(wide_w[:, i // 2, i % 2 * HALF:(i % 2 + 1) * HALF], m.ps[:, 4 + i % 4, :],
                                     ACT.Copy).then_inc(wide_sb, 1)


def to_token_tiles(m, name, acc):
    nc = m.nc
    with nc.Block() as block:
        @block.tensor
        def _(pe):
            for t in range(TT):
                nc.tensor.transpose(m.ps[:, 4 + t // 4, t % 4 * P:(t % 4 + 1) * P], acc[:, t * P:(t + 1) * P], m.ident[:])


def experts_gelu(m):
    nc, a = m.nc, m.a
    FC = FF0 // P
    with ExitStack() as ctx:
        def sb(n, shape):
            return m.sb("m0_" + n, shape, F32, ctx)

        ww = sb("ww", [P, NE, NT])
        acc = sb("acc", [P, NT])
        route(m, "m0r", "m0_gate", 1, ww)
        w1 = [sb(f"w1_{i}", [P, FF0]) for i in range(2)]
        w2 = [sb(f"w2_{i}", [P, FC, P]) for i in range(2)]
        b1 = [sb(f"b1_{i}", [P, FC]) for i in range(2)]
        b2 = sb("b2", [P, NE])
        hid = sb("hid", [P, 2, FC, NT])
        part = sb("part", [P, 2, 2, HALF])
        loaded, cleared, up_ps, gelu, y_ps, y_read, added = (
            m.sem("m0_" + s) for s in ("loaded", "cleared", "up", "gelu", "y", "yread", "added"))
        w_in = [m.sem(f"m0_w{i}") for i in range(2)]
        c3 = ctx.enter_context(ExitStack())
        block = c3.enter_context(nc.Block())

        @block.sync
        def _(sp):
            sp.dma_start(b2[:], a["m0_b2"]).then_inc(loaded, 16)
            with sp.Fori(0, NE // 2) as e2:
                for i in range(2):
                    e = e2 * 2 + i
                    sp.wait_ge(y_ps, e * 2 + 2)
                    sp.dma_start(b1[i][:], a["m0_b1"][bass.ds(e, 1)].rearrange("e p f -> p (e f)")).then_inc(w_in[i], 16)
                    sp.dma_start(w1[i][:], a["m0_w1"][bass.ds(e, 1)].rearrange("e p f -> p (e f)")).then_inc(w_in[i], 16)
                    sp.dma_start(w2[i][:], a["m0_w2"][bass.ds(e, 1)].rearrange("e (c p) d -> p (e c) d", p=P)).then_inc(w_in[i], 16)

        @block.tensor
        def _(pe):
            pe.sem_inc(y_ps, 4)
            with pe.Fori(0, NE // 2) as e2:
                for par in range(2):
                    e = e2 * 2 + par
                    pe.wait_ge(w_in[par], e2 * 48 + 48)
                    for i in range(2 * FC):
                        c, h = i // 2, i % 2
                        pe.wait_ge(gelu, e * 8 + i + 1)
                        nc.tensor.matmul(m.ps[:, i % 4, :], w1[par][:, c * P:(c + 1) * P], m.xT[:, h * HALF:(h + 1) * HALF],
                                         start=True, stop=True).then_inc(up_ps, 1)
                    for i in range(2 * FC):
                        c, h = i // 2, i % 2
                        pe.wait_ge(gelu, e * 8 + i + 1 + 4)
                        if c == 0:
                            pe.wait_ge(y_read, e * 2 + h + 1)
                        ins = nc.tensor.matmul(m.ps[:, 4 + 2 * par + h, :], w2[par][:, c, :],
                                               hid[:, par, c, h * HALF:(h + 1) * HALF], start=c == 0, stop=c == FC - 1)
                        if c == FC - 1:
                            ins.then_inc(y_ps, 1)

        @block.scalar
        def _(act):
            act.sem_inc(gelu, 4)
            with act.Fori(0, NE // 2) as e2:
                for par in range(2):
                    e = e2 * 2 + par
                    act.wait_ge(y_ps, e * 2 + 2)
                    act.wait_ge(w_in[par], e2 * 48 + 48)
                    for i in range(2 * FC):
                        c, h = i // 2, i % 2
                        act.wait_ge(up_ps, e * 8 + i + 1)
                        nc.scalar.activation(hid[:, par, c, h * HALF:(h + 1) * HALF], m.ps[:, i % 4, :], ACT.Gelu,
                                             bias=b1[par][:, c:c + 1]).then_inc(gelu, 1)

        @block.vector
        def _(dve):
            nc.vector.memset(acc[:], 0.0).then_inc(cleared, 1)
            dve.sem_inc(y_read, 4)
            dve.wait_ge(loaded, 16)
            with dve.Fori(0, NE // 2) as e2:
                for par in range(2):
                    e = e2 * 2 + par
                    for h in range(2):
                        dve.wait_ge(y_ps, e * 2 + h + 1 + 4)
                        dve.wait_ge(added, e * 2 + h + 1)
                        nc.vector.scalar_tensor_tensor(
                            part[:, par, h, :], m.ps[:, 4 + 2 * par + h, :], b2[:, bass.ds(e, 1)],
                            ww[:, bass.ds(e, 1), h * HALF:(h + 1) * HALF].rearrange("p a b -> p (a b)"),
                            ALU.add, ALU.mult).then_inc(y_read, 1)

        @block.gpsimd
        def _(pool):
            pool.sem_inc(added, 4)
            pool.wait_ge(cleared, 1)
            with pool.Fori(0, NE // 2) as e2:
                for par in range(2):
                    e = e2 * 2 + par
                    for h in range(2):
                        pool.wait_ge(y_read, e * 2 + h + 1 + 4)
                        pool.wait_ge(added, e * 2 + h + 1 + 2)
                        o = acc[:, h * HALF:(h + 1) * HALF]
                        nc.gpsimd.tensor_tensor(o, o, part[:, par, h, :], ALU.add).then_inc(added, 1)

        c3.close()
        to_token_tiles(m, "m0", acc)
    layernorm(m, "ln2", m.ps[:, 4:6, :].rearrange("p a (b c) -> p (a b) c", c=P))


def experts_silu(m):
    nc, a = m.nc, m.a
    FC = FF1 // P
    with ExitStack() as ctx:
        def sb(n, shape):
            return m.sb("m1_" + n, shape, F32, ctx)

        ww = sb("ww", [P, NE, NT])
        acc = sb("acc", [P, NT])
        route(m, "m1r", "m1_gate", 2, ww)
        wg = [sb(f"wg_{i}", [P, FF1]) for i in range(2)]
        wu = [sb(f"wu_{i}", [P, FF1]) for i in range(2)]
        wd = [sb(f"wd_{i}", [P, FC, P]) for i in range(2)]
        sil = sb("sil", [P, 4, HALF])
        hid = sb("hid", [P, 2, FC, NT])
        part = sb("part", [P, 2, 2, HALF])
        cleared, g_ps, u_ps, silu, h_ready, y_ps, y_read, added = (
            m.sem("m1_" + s) for s in ("cleared", "g", "u", "silu", "h", "y", "yread", "added"))
        w_in = [m.sem(f"m1_w{i}") for i in range(2)]
        c3 = ctx.enter_context(ExitStack())
        block = c3.enter_context(nc.Block())

        @block.sync
        def _(sp):
            with sp.Fori(0, NE // 2) as e2:
                for i in range(2):
                    e = e2 * 2 + i
                    sp.wait_ge(y_ps, e * 2 + 2)
                    sp.dma_start(wg[i][:], a["m1_wg"][bass.ds(e, 1)].rearrange("e p f -> p (e f)")).then_inc(w_in[i], 16)
                    sp.dma_start(wu[i][:], a["m1_wu"][bass.ds(e, 1)].rearrange("e p f -> p (e f)")).then_inc(w_in[i], 16)
                    sp.dma_start(wd[i][:], a["m1_wd"][bass.ds(e, 1)].rearrange("e (c p) d -> p (e c) d", p=P)).then_inc(w_in[i], 16)

        @block.tensor
        def _(pe):
            pe.sem_inc(y_ps, 4)
            with pe.Fori(0, NE // 2) as e2:
                for par in range(2):
                    e = e2 * 2 + par
                    pe.wait_ge(w_in[par], e2 * 48 + 48)
                    for i in range(2 * FC):
                        c, h = i // 2, i % 2
                        x = m.xT[:, h * HALF:(h + 1) * HALF]
                        pe.wait_ge(h_ready, e * 4 + i + 3)
                        nc.tensor.matmul(m.ps[:, i % 2, :], wg[par][:, c * P:(c + 1) * P], x, start=True, stop=True).then_inc(g_ps, 1)
                        nc.tensor.matmul(m.ps[:, 2 + i % 2, :], wu[par][:, c * P:(c + 1) * P], x, start=True, stop=True).then_inc(u_ps, 1)
                    for i in range(2 * FC):
                        c, h = i // 2, i % 2
                        pe.wait_ge(h_ready, e * 4 + i + 1 + 4)
                        if c == 0:
                            pe.wait_ge(y_read, e * 2 + h + 1)
                        ins = nc.tensor.matmul(m.ps[:, 4 + 2 * par + h, :], wd[par][:, c, :],
                                               hid[:, par, c, h * HALF:(h + 1) * HALF], start=c == 0, stop=c == FC - 1)
                        if c == FC - 1:
                            ins.then_inc(y_ps, 1)

        @block.scalar
        def _(act):
            with act.Fori(0, NE) as e:
                for i in range(4):
                    act.wait_ge(g_ps, e * 4 + i + 1)
                    act.wait_ge(h_ready, e * 4 + i + 1)
                    nc.scalar.activation(sil[:, i, :], m.ps[:, i % 2, :], ACT.Silu).then_inc(silu, 1)

        @block.vector
        def _(dve):
            nc.vector.memset(acc[:], 0.0).then_inc(cleared, 1)
            dve.sem_inc(y_read, 4)
            dve.sem_inc(h_ready, 4)
            with dve.Fori(0, NE // 2) as e2:
                for par in range(2):
                    e = e2 * 2 + par
                    dve.wait_ge(y_ps, e * 2 + 2)
                    for i in range(4):
                        c, h = i // 2, i % 2
                        dve.wait_ge(silu, e * 4 + i + 1)
                        dve.wait_ge(u_ps, e * 4 + i + 1)
                        nc.vector.tensor_tensor(hid[:, par, c, h * HALF:(h + 1) * HALF], m.ps[:, 2 + i % 2, :], sil[:, i, :],
                                                ALU.mult).then_inc(h_ready, 1)
                    for h in range(2):
                        dve.wait_ge(y_ps, e * 2 + h + 1 + 4)
                        dve.wait_ge(added, e * 2 + h + 1)
                        nc.vector.tensor_tensor(
                            part[:, par, h, :], m.ps[:, 4 + 2 * par + h, :],
                            ww[:, bass.ds(e, 1), h * HALF:(h + 1) * HALF].rearrange("p a b -> p (a b)"), ALU.mult).then_inc(y_read, 1)

        @block.gpsimd
        def _(pool):
            pool.sem_inc(added, 4)
            pool.wait_ge(cleared, 1)
            with pool.Fori(0, NE // 2) as e2:
                for par in range(2):
                    e = e2 * 2 + par
                    for h in range(2):
                        pool.wait_ge(y_read, e * 2 + h + 1 + 4)
                        pool.wait_ge(added, e * 2 + h + 1 + 2)
                        o = acc[:, h * HALF:(h + 1) * HALF]
                        nc.gpsimd.tensor_tensor(o, o, part[:, par, h, :], ALU.add).then_inc(added, 1)

        c3.close()
        to_token_tiles(m, "m1", acc)
    layernorm(m, "ln5", m.ps[:, 4:6, :].rearrange("p a (b c) -> p (a b) c", c=P), out=m.out)


def s4_kernel(m, kern):
    nc, a = m.nc, m.a
    with ExitStack() as ctx:
        def sb(n, shape):
            return m.sb("sk_" + n, shape, F32, ctx)

        cc = sb("cc", [P, 8])
        b_steps, a_steps = sb("bsteps", [P, 32]), sb("asteps", [P, 32])
        logs, turns, red, ex = (sb(n, [P, 2, P]) for n in ("logs", "turns", "red", "ex"))
        power = m.sb("sk_power", [P, 2, P], mybir.dt.int32, ctx)
        aim, cre, cim = (sb(n, [P, P]) for n in ("aim", "cre", "cim"))
        dr, wi, er, ei, t1, t2, t3, nr, ni, alpha, beta = (
            sb(n, [P, P]) for n in ("dr", "wi", "er", "ei", "t1", "t2", "t3", "nr", "ni", "alpha", "beta"))
        big = [P, P, 32]
        th, rn, e2, g1, g2 = (sb(n, big) for n in ("th", "rn", "e2", "g1", "g2"))
        loaded, act_in, act_out, tables, k_ps = (m.sem("sk_" + s) for s in ("loaded", "actin", "actout", "tables", "kps"))
        n_act = [0]

        with nc.Block() as block:
            requests = []

            @block.sync
            def _(sp):
                for dst, src in ((cc, "c_s4"), (b_steps, "c_bsteps"), (a_steps, "c_asteps"), (aim, "s4_aim"), (cre, "s4_cre"), (cim, "s4_cim")):
                    sp.dma_start(dst[:], a[src]).then_inc(loaded, 16)
                sp.dma_start(logs[:, 0, :], a["s4_ldt"]).then_inc(loaded, 16)
                sp.dma_start(logs[:, 1, :], a["s4_arl"]).then_inc(loaded, 16)

            @block.vector
            def _(dve):
                def own(ins):
                    m.dve(dve, ins)

                def ready_for_act():
                    n_act[0] += 1
                    dve.wait_ge(act_out, n_act[0])

                def give(ins):
                    ins.then_inc(act_in, 1)
                    ready_for_act()

                def reduced_angle(out, angle, turn, rad, tmp, last=give):
                    own(nc.vector.tensor_scalar(tmp, angle, 1.0 / TWO_PI, turn, ALU.mult, ALU.add))
                    own(nc.vector.tensor_scalar(tmp, tmp, MAGIC, MAGIC, ALU.add, ALU.subtract))
                    own(nc.vector.scalar_tensor_tensor(out, tmp, -TWO_PI_HI, angle, ALU.mult, ALU.add))
                    own(nc.vector.scalar_tensor_tensor(out, tmp, -TWO_PI_LO, out, ALU.mult, ALU.add))
                    own(nc.vector.tensor_scalar(out, out, rad, PI_BELOW, ALU.add, ALU.min))
                    last(nc.vector.tensor_scalar(out, out, -PI_BELOW, None, ALU.max))

                tt, ts, stt = nc.vector.tensor_tensor, nc.vector.tensor_scalar, nc.vector.scalar_tensor_tensor
                dve.wait_ge(loaded, 16 * 8)
                own(ts(turns[:], logs[:], 1.0 / LN2, MAGIC, ALU.mult, ALU.add))
                own(ts(turns[:], turns[:], MAGIC, None, ALU.subtract))
                own(ts(turns[:], turns[:], -126.0, 127.0, ALU.max, ALU.min))
                own(stt(red[:], turns[:], -LN2_HI, logs[:], ALU.mult, ALU.add))
                give(stt(red[:], turns[:], -LN2_LO, red[:], ALU.mult, ALU.add))
                own(ts(power[:], turns[:], 127.0, 8388608.0, ALU.add, ALU.mult))
                own(ts(ex[:], red[:], -1.0, 1.0, ALU.mult, ALU.add))
                own(nc.vector.reciprocal(ex[:], ex[:]))
                own(stt(ex[:], red[:], 1.0, ex[:], ALU.add, ALU.mult))
                own(tt(ex[:], ex[:], power[:].bitcast(F32), ALU.mult))
                dt, are = ex[:, 0, :], ex[:, 1, :]
                own(stt(dr[:], dt, -1.0, are, ALU.mult, ALU.mult))
                own(tt(wi[:], dt, aim[:], ALU.mult))
                reduced_angle(er[:], wi[:], 0.25, TWO_PI / 4, t1[:])
                reduced_angle(ei[:], wi[:], 0.0, 0.0, t1[:])
                own(ts(t2[:], wi[:], 0.5, None, ALU.mult))
                reduced_angle(nr[:], t2[:], 0.0, 0.0, t1[:])
                give(ts(t3[:], dr[:], 1.0, None, ALU.mult))
                own(ts(t1[:], t3[:], -1.0, 1.0, ALU.mult, ALU.add))
                own(nc.vector.reciprocal(t1[:], t1[:]))
                own(stt(t3[:], t3[:], 2.0, t1[:], ALU.mult, ALU.mult))
                own(tt(er[:], er[:], t3[:], ALU.mult))
                own(stt(nr[:], nr[:], 2.0, nr[:], ALU.mult, ALU.mult))
                own(tt(er[:], er[:], nr[:], ALU.subtract))
                own(stt(ei[:], t3[:], 1.0, ei[:], ALU.add, ALU.mult))
                own(tt(nr[:], cre[:], er[:], ALU.mult))
                own(tt(t1[:], cim[:], ei[:], ALU.mult))
                own(tt(nr[:], nr[:], t1[:], ALU.subtract))
                own(tt(ni[:], cre[:], ei[:], ALU.mult))
                own(tt(t1[:], cim[:], er[:], ALU.mult))
                own(tt(ni[:], ni[:], t1[:], ALU.add))
                own(tt(t1[:], are, are, ALU.mult))
                own(tt(t2[:], aim[:], aim[:], ALU.mult))
                own(tt(t1[:], t1[:], t2[:], ALU.add))
                own(nc.vector.reciprocal(t1[:], t1[:]))
                own(tt(t2[:], ni[:], aim[:], ALU.mult))
                own(tt(t3[:], nr[:], are, ALU.mult))
                own(tt(alpha[:], t2[:], t3[:], ALU.subtract))
                own(tt(alpha[:], alpha[:], t1[:], ALU.mult))
                own(ts(alpha[:], alpha[:], cc[:, 4:5], None, ALU.mult))
                own(tt(t2[:], ni[:], are, ALU.mult))
                own(tt(t3[:], nr[:], aim[:], ALU.mult))
                own(tt(beta[:], t2[:], t3[:], ALU.add))
                own(stt(beta[:], beta[:], 2.0, t1[:], ALU.mult, ALU.mult))
                wide = [P, P, 32]

                def steps(out, rate, which):
                    return tt(out, rate[:].unsqueeze(2).to_broadcast(wide), which[:].unsqueeze(1).to_broadcast(wide), ALU.mult)

                def exp_from_tanh(t):
                    own(ts(t, t, -1.0, 1.0, ALU.mult, ALU.add))
                    own(nc.vector.reciprocal(t, t))
                    own(ts(t, t, 2.0, 1.0, ALU.mult, ALU.subtract))

                own(steps(th[:], wi, b_steps))
                reduced_angle(e2[:], th[:], cc[:, 0:1], cc[:, 1:2], rn[:])
                give(steps(th[:], dr, b_steps))
                exp_from_tanh(th[:])
                own(tt(e2[:], e2[:], th[:], ALU.mult))
                own(steps(th[:], wi, a_steps))
                reduced_angle(g1[:], th[:], cc[:, 0:1], cc[:, 1:2], rn[:])
                reduced_angle(g2[:], th[:], cc[:, 2:3], cc[:, 3:4], rn[:])
                give(steps(th[:], dr, a_steps))
                exp_from_tanh(th[:])
                own(tt(g1[:], g1[:], alpha[:].unsqueeze(2).to_broadcast(wide), ALU.mult))
                own(tt(g2[:], g2[:], beta[:].unsqueeze(2).to_broadcast(wide), ALU.mult))
                own(tt(g1[:], g1[:], g2[:], ALU.add))
                tt(g1[:], g1[:], th[:], ALU.mult).then_inc(tables, 1)
                dve.wait_ge(k_ps, 1)
                nc.vector.tensor_copy(kern[:], m.ps[:, 0:2, :].rearrange("p a b -> p (a b)").rearrange("p (h c) -> p c h", c=TT))

            @block.scalar
            def _(act):
                act.wait_ge(loaded, 16 * 8)
                for i, (buf, f) in enumerate(((red, ACT.Tanh), (er, ACT.Sin), (ei, ACT.Sin), (nr, ACT.Sin), (t3, ACT.Tanh), (e2, ACT.Sin),
                                              (th, ACT.Tanh), (g1, ACT.Sin), (g2, ACT.Sin), (th, ACT.Tanh))):
                    act.wait_ge(act_in, i + 1)
                    nc.scalar.activation(buf[:], buf[:], f, scale=0.5 if f == ACT.Tanh else 1.0).then_inc(act_out, 1)

            @block.tensor
            def _(pe):
                pe.wait_ge(tables, 1)
                kp = m.ps[:, 0:2, :].rearrange("p a b -> p (a b)").rearrange("p (h c) -> p h c", c=TT)
                g1v = g1[:].rearrange("p h (c k) -> p h k c", k=4)
                for h in range(P):
                    for k in range(4):
                        ins = nc.tensor.matmul(kp[32 * k:32 * k + 32, h, :], e2[:, h, :], g1v[:, h, k, :], start=True, stop=True)
                ins.then_inc(k_ps, 1)


def s4_layer(m):
    nc, a = m.nc, m.a
    with ExitStack() as ctx:
        def sb(n, shape, c=ctx):
            return m.sb("s4_" + n, shape, F32, c)

        kern = sb("kern", [P, TT, P])
        s4_kernel(m, kern)
        dft = sb("dft", [P, TT, 2 * NF])
        altc, altr = sb("altc", [P, 1]), sb("altr", [1, NT])
        dcol, wout, bout = sb("dcol", [P, 1]), sb("wout", [P, 2 * P]), sb("bout", [1, 2 * P])
        kh, yh, t1 = sb("kh", [P, 2, NF]), sb("yh", [P, 2, NF]), sb("t1", [P, NF])
        khn, yhn, yrow = sb("khn", [P, 1]), sb("yhn", [P, 1]), sb("yrow", [1, P])
        yT = sb("yT", [P, 2 * TT, P])
        u, gT, sig, yb = sb("u", [P, NT]), sb("gT", [P, NT]), sb("sig", [P, TT, P]), sb("yb", [P, TT, P])
        (loaded, k_ps, k_sb, x_ps, y_sb, t_ps, t_sb, inv_ps, u_sb, g_sb, z_ps, s_sb) = (
            m.sem("s4_" + s) for s in ("loaded", "kps", "ksb", "xps", "ysb", "tps", "tsb", "invps", "usb", "gsb", "zps", "ssb"))
        spec = m.ps[:, 4:8, :].rearrange("p (a b) c -> p a (b c)", a=2)
        scale = 1.0 / NF
        zp = m.ps[:, 0:4, :].rearrange("p a (b c) -> p (a b) c", c=2 * P)
        with nc.Block() as block:
            @block.sync
            def _(sp):
                for t in range(TT):
                    sp.dma_start(dft[:, t, :], a["c_dft"][t * P:(t + 1) * P, :]).then_inc(loaded, 16)
                for dst, src in ((altc, "c_altc"), (altr, "c_altr"), (dcol, "s4_d"), (wout, "s4_wout"), (bout, "s4_bout")):
                    sp.dma_start(dst[:], a[src]).then_inc(loaded, 16)

            @block.tensor
            def _(pe):
                def forward(src, nyq, done):
                    for j in range(4):
                        for c in range(TT):
                            ins = nc.tensor.matmul(m.ps[:, 4 + j, :], src[:, c, :], dft[:, c, j * 512:(j + 1) * 512],
                                                   start=c == 0, stop=c == TT - 1)
                        ins.then_inc(done, 1)
                    for c in range(TT):
                        ins = nc.tensor.matmul(nyq, src[:, c, :], altc[:], start=c == 0, stop=c == TT - 1)
                    ins.then_inc(done, 1)

                pe.wait_ge(loaded, 16 * 13)
                forward(kern, m.ps[:, 0, 0:1], k_ps)
                pe.wait_ge(k_sb, 3)
                forward(m.xtok, m.ps[:, 1, 0:1], x_ps)
                pe.wait_ge(y_sb, 1)
                nc.tensor.matmul(m.ps[0:1, 2, 0:P], yhn[:], m.ident[:], start=True, stop=True).then_inc(t_ps, 1)
                for j in range(4):
                    pe.wait_ge(y_sb, 2 + j // 2)
                    if j == 2:
                        pe.wait_ge(t_sb, 1)
                    for c in range(4):
                        f = 4 * j + c
                        ins = nc.tensor.transpose(m.ps[:, (0, 1, 2, 3)[j], c * P:(c + 1) * P],
                                                  yh[:, f // TT, f % TT * P:(f % TT + 1) * P], m.ident[:])
                    ins.then_inc(t_ps, 1)
                pe.wait_ge(t_sb, 5)
                for h in range(2):
                    for f in range(2 * TT):
                        nc.tensor.matmul(m.ps[:, 4 + h, :], yT[:, f, :],
                                         dft[:, f % TT, f // TT * NF + h * HALF:f // TT * NF + (h + 1) * HALF],
                                         start=f == 0, stop=False)
                    nc.tensor.matmul(m.ps[:, 4 + h, :], yrow[:], altr[:, h * HALF:(h + 1) * HALF], start=False,
                                     stop=True).then_inc(inv_ps, 1)
                for t in range(TT):
                    pe.wait_ge(g_sb, 1 + t // 4)
                    nc.tensor.matmul(zp[:, t, :], gT[:, t * P:(t + 1) * P], wout[:], start=True, stop=False)
                    nc.tensor.matmul(zp[:, t, :], m.ones_row[0:1, 0:P], bout[:], start=False, stop=True).then_inc(z_ps, 1)

            @block.vector
            def _(dve):
                def own(ins):
                    m.dve(dve, ins)

                tt, ts = nc.vector.tensor_tensor, nc.vector.tensor_scalar
                dve.wait_ge(loaded, 16 * 13)
                dve.wait_ge(k_ps, 5)
                for s in range(2):
                    own(ts(kh[:, s, :], spec[:, s, :], scale, None, ALU.mult))
                    ts(kh[:, s, 0:1], kh[:, s, 0:1], 0.5, None, ALU.mult).then_inc(k_sb, 1)
                ts(khn[:], m.ps[:, 0, 0:1], 0.5 * scale, None, ALU.mult).then_inc(k_sb, 1)
                dve.wait_ge(k_sb, 3)
                dve.wait_ge(x_ps, 5)
                tt(yhn[:], khn[:], m.ps[:, 1, 0:1], ALU.mult).then_inc(y_sb, 1)
                own(tt(yh[:, 0, :], kh[:, 0, :], spec[:, 0, :], ALU.mult))
                own(tt(t1[:], kh[:, 1, :], spec[:, 1, :], ALU.mult))
                tt(yh[:, 0, :], yh[:, 0, :], t1[:], ALU.subtract).then_inc(y_sb, 1)
                dve.wait_ge(y_sb, 2)
                own(tt(yh[:, 1, :], kh[:, 1, :], spec[:, 0, :], ALU.mult))
                own(tt(t1[:], kh[:, 0, :], spec[:, 1, :], ALU.mult))
                tt(yh[:, 1, :], yh[:, 1, :], t1[:], ALU.add).then_inc(y_sb, 1)
                dve.wait_ge(t_ps, 1)
                nc.vector.tensor_copy(yrow[:], m.ps[0:1, 2, 0:P]).then_inc(t_sb, 1)
                for j in range(4):
                    dve.wait_ge(t_ps, 2 + j)
                    nc.vector.tensor_copy(yT[:, 4 * j:4 * j + 4, :].rearrange("p a b -> p (a b)"), m.ps[:, j, :]).then_inc(t_sb, 1)
                for h in range(2):
                    dve.wait_ge(inv_ps, h + 1)
                    nc.vector.scalar_tensor_tensor(u[:, h * HALF:(h + 1) * HALF], m.xT[:, h * HALF:(h + 1) * HALF], dcol[:, 0:1],
                                                   m.ps[:, 4 + h, :], ALU.mult, ALU.add).then_inc(u_sb, 1)
                for g in range(4):
                    dve.wait_ge(s_sb, g + 1)
                    tt(yb[:, 2 * g:2 * g + 2, :], zp[:, 2 * g:2 * g + 2, 0:P], sig[:, 2 * g:2 * g + 2, :], ALU.mult)

            @block.scalar
            def _(act):
                for h in range(2):
                    act.wait_ge(u_sb, h + 1)
                    nc.scalar.activation(gT[:, h * HALF:(h + 1) * HALF], u[:, h * HALF:(h + 1) * HALF],
                                         ACT.Gelu_apprx_tanh).then_inc(g_sb, 1)
                for g in range(4):
                    act.wait_ge(z_ps, 2 * g + 2)
                    nc.scalar.activation(sig[:, 2 * g:2 * g + 2, :], zp[:, 2 * g:2 * g + 2, P:2 * P], ACT.Sigmoid).then_inc(s_sb, 1)
        layernorm(m, "ln3", yb)


W_D2V, W_IMG, W_TXT, W_ATT0, W_ATT1, W_F1, W_F2 = range(7)


def all_partitions(m, name, col, out, op):
    with m.nc.Block() as block:
        @block.gpsimd
        def _(pool):
            m.nc.gpsimd.partition_all_reduce(out, col, P, op)


def input_scale(m, top, weight_scale, inv, product, step):
    nc = m.nc
    with nc.Block() as block:
        @block.vector
        def _(dve):
            m.dve(dve, nc.vector.tensor_scalar(step, top, 1e-8, 1.0 / 127.0, ALU.max, ALU.mult))
            m.dve(dve, nc.vector.reciprocal(inv, step))
            for w, p in zip(weight_scale, product):
                nc.vector.tensor_tensor(p, step, w, ALU.mult)


def bit_layer(m, name, src, k, n, inv, quant, weight, out, scale, bias, max_out, sum_out=None, real=None):
    nc = m.nc
    real = real or n
    chunks = [(c, min(HALF, n - c)) for c in range(0, n, HALF)]
    with ExitStack() as ctx:
        tmp = m.sb(name + "_tmp", [P, 2, HALF], F32, ctx)
        tops = m.sb(name + "_tops", [P, len(chunks)], F32, ctx)
        q, mm, ev = (m.sem(f"{name}_{s}") for s in ("quant", "mm", "out"))
        block = ctx.enter_context(nc.Block())

        @block.vector
        def _(dve):
            for i, (c, w) in enumerate(chunks):
                m.dve(dve, nc.vector.tensor_scalar(tmp[0:k, i % 2, 0:w], src[0:k, c:c + w], inv[0:k, :], MAGIC, ALU.mult, ALU.add))
                nc.vector.tensor_scalar(quant[0:k, c:c + w], tmp[0:k, i % 2, 0:w], MAGIC, 127.0, ALU.subtract, ALU.min).then_inc(q, 1)
            for i, (c, w) in enumerate(chunks):
                dve.wait_ge(ev, i + 1)
                w = min(w, real - c)
                last = nc.vector.tensor_reduce(tops[:, i:i + 1], out[:, c:c + w], AX.X, ALU.max, apply_absolute_value=True)
            m.dve(dve, last)
            nc.vector.tensor_reduce(max_out, tops[:], AX.X, ALU.max)
            if sum_out is not None:
                nc.vector.tensor_reduce(sum_out, out[:, 0:real], AX.X, ALU.add)

        @block.tensor
        def _(pe):
            for i, (c, w) in enumerate(chunks):
                pe.wait_ge(q, i + 1)
                if i >= 4:
                    pe.wait_ge(ev, i - 3)
                nc.tensor.matmul(m.ps[:, i % 4, 0:w], weight, quant[0:k, c:c + w], start=True, stop=True).then_inc(mm, 1)

        @block.scalar
        def _(act):
            for i, (c, w) in enumerate(chunks):
                act.wait_ge(mm, i + 1)
                nc.scalar.activation(out[:, c:c + w], m.ps[:, i % 4, 0:w], ACT.Identity, scale=scale, bias=bias).then_inc(ev, 1)


def vision_attention(m):
    nc, a = m.nc, m.a
    with ExitStack() as ctx:
        def sb(n, shape, dt=F32, c=ctx):
            return m.sb("va_" + n, shape, dt, c)

        qimg = sb("qimg", [P, KP], BF16)
        fT = sb("fT", [P, NT])
        shapes = {W_D2V: (CD, P), W_IMG: (P, P), W_TXT: (P, P), W_ATT0: (P, 64), W_ATT1: (P, 64), W_F1: (P, 2 * FF0), W_F2: (P, 4 * P)}
        tern = {w: sb(f"tern{w}", list(shapes[w]), BF16) for w in shapes}
        tern_out = [sb(f"ternout{i}", [P, P]) for i in range(2)]
        bias = sb("bias", [P, 3])
        batt = [sb(f"batt{i}", [P, 64]) for i in range(2)]
        bf1, bf2 = sb("bf1", [P, 4]), sb("bf2", [P, P])
        wsc = sb("wsc", [P, 7])
        avg = sb("avg", [P, 1])
        step_img = sb("step_img", [P, 1])
        satt = sb("satt", [P, 2])
        with ExitStack() as c1:
            raw = {w: sb(f"raw{w}", list(shapes[w]), F32, c1) for w in shapes}
            raw_out = [sb(f"rawout{i}", [P, P], F32, c1) for i in range(2)]
            inv_n, sums, thr, nthr = (sb(n, [P, 7], F32, c1) for n in ("invn", "sums", "thr", "nthr"))
            tmp = sb("tmp", [P, 2 * FF0], F32, c1)
            tmpb = sb("tmpb", [P, P], F32, c1)
            tops, top = sb("tops", [P, 4], F32, c1), sb("top", [P, 4], F32, c1)
            vec, vis = sb("vec", [P, KP], F32, c1), sb("vis", [P, KP], F32, c1)
            qtmp = sb("qtmp", [P, KP], BF16, c1)
            loaded, ab = m.sem("va_loaded"), m.sem("va_abs")
            with nc.Block() as block:
                @block.sync
                def _(sp):
                    n = 0
                    for dst, src in [(raw[w], f"va_w{w}") for w in shapes] + [(raw_out[0], "va_wo0"), (raw_out[1], "va_wo1"),
                                     (inv_n, "c_inv"), (bias, "va_bias"), (batt[0], "va_batt0"), (batt[1], "va_batt1"),
                                     (bf1, "va_bf1"), (bf2, "va_bf2")]:
                        sp.dma_start(dst[:], a[src]).then_inc(loaded, 16)
                    sp.dma_start(vec[0:CD, 0:KV], a["ctx_T"]).then_inc(loaded, 16)
                    sp.dma_start(vec[0:CD, KV:KP], a["ctx_T"][:, 0:KP - KV]).then_inc(loaded, 16)

                @block.vector
                def _(dve):
                    m.dve(dve, nc.vector.memset(sums[:], 0.0))
                    m.dve(dve, nc.vector.memset(tops[:], 0.0))
                    dve.wait_ge(loaded, 16 * 17)
                    for w, (k, _) in shapes.items():
                        nc.vector.tensor_reduce(sums[0:k, w:w + 1], raw[w][:], AX.X, ALU.add, apply_absolute_value=True)
                    nc.vector.tensor_reduce(tops[0:CD, 0:1], vec[0:CD, 0:KV], AX.X, ALU.max, apply_absolute_value=True)
                    nc.vector.tensor_reduce(tops[:, 1:2], m.xT[:], AX.X, ALU.max, apply_absolute_value=True)
            all_partitions(m, "w", sums[:], wsc[:], RADD)
            all_partitions(m, "x", tops[:], top[:], RMAX)
            with nc.Block() as block:
                @block.vector
                def _(dve):
                    def own(ins):
                        m.dve(dve, ins)

                    own(nc.vector.tensor_tensor(wsc[:], wsc[:], inv_n[:], ALU.mult))
                    own(nc.vector.tensor_scalar(wsc[:], wsc[:], 1e-5, None, ALU.max))
                    own(nc.vector.tensor_scalar(thr[:], wsc[:], 0.5, None, ALU.mult))
                    own(nc.vector.tensor_scalar(nthr[:], wsc[:], -0.5, None, ALU.mult))

                    def ternary(dst, src, k, w, t):
                        own(nc.vector.tensor_scalar(t, src[:], nthr[0:k, w:w + 1], None, ALU.is_lt))
                        own(nc.vector.scalar_tensor_tensor(dst[:], src[:], thr[0:k, w:w + 1], t, ALU.is_gt, ALU.subtract))

                    for w, (k, n) in shapes.items():
                        ternary(tern[w], raw[w], k, w, tmp[0:k, 0:n])
                    for i in range(2):
                        ternary(tern_out[i], raw_out[i], P, W_ATT0 + i, tmpb[:])
            sc = {n: sb("s_" + n, [P, 1], F32, c1) for n in ("inv_x", "p_x", "inv_c", "p_c", "inv_v", "p_v", "step", "max_v", "max_i", "top_v", "top_i",
                                         "inv_i", "max_f")}
            input_scale(m, top[:, 0:1], [wsc[:, W_D2V:W_D2V + 1]], sc["inv_c"][:], [sc["p_c"][:]], sc["step"][:])
            bit_layer(m, "va_d2v", vec, CD, KP, sc["inv_c"], qtmp, tern[W_D2V][:], vis, sc["p_c"][:, 0:1], bias[:, 0:1],
                      sc["max_v"][:], real=KV)
            all_partitions(m, "v", sc["max_v"][:], sc["top_v"][:], RMAX)
            input_scale(m, sc["top_v"][:], [wsc[:, W_IMG:W_IMG + 1]], sc["inv_v"][:], [sc["p_v"][:]], sc["step"][:])
            bit_layer(m, "va_img", vis, P, KP, sc["inv_v"], qtmp, tern[W_IMG][:], vec, sc["p_v"][:, 0:1], bias[:, 1:2],
                      sc["max_i"][:], avg[:], real=KV)
            all_partitions(m, "i", sc["max_i"][:], sc["top_i"][:], RMAX)
            input_scale(m, sc["top_i"][:], [wsc[:, W_ATT0 + i:W_ATT0 + i + 1] for i in range(2)], sc["inv_i"][:],
                        [satt[:, i:i + 1] for i in range(2)], step_img[:])
            input_scale(m, top[:, 1:2], [wsc[:, W_TXT:W_TXT + 1]], sc["inv_x"][:], [sc["p_x"][:]], sc["step"][:])
            with nc.Block() as block:
                @block.vector
                def _(dve):
                    nc.vector.tensor_scalar(avg[:], avg[:], 1.0 / KV, None, ALU.mult)
                    m.dve(dve, nc.vector.tensor_scalar(vis[:], vec[:], sc["inv_i"][:], MAGIC, ALU.mult, ALU.add))
                    nc.vector.tensor_scalar(qimg[:], vis[:], MAGIC, 127.0, ALU.subtract, ALU.min)
            bit_layer(m, "va_txt", m.xT, P, NT, sc["inv_x"], qtmp, tern[W_TXT][:], fT, sc["p_x"][:, 0:1], bias[:, 2:3],
                      sc["max_f"][:])

        for layer in range(2):
            one_head_attention(m, f"v{layer}", qimg, fT, tern[W_ATT0 + layer], tern_out[layer], satt[:, layer:layer + 1], batt[layer])
        vision_mlp(m, fT, avg, wsc, tern, bf1, bf2)


def one_head_attention(m, name, qimg, fT, wT, w_out, scale, b_row):
    nc = m.nc
    with ExitStack() as ctx:
        def sb(n, shape, dt=F32):
            return m.sb(f"{name}_{n}", shape, dt, ctx)

        kv = sb("kv", [P, KT, P])
        g32, rest = sb("g32", [P, NT]), sb("rest", [P, NT])
        gp = [sb(f"g{i}", [P, NT], BF16) for i in range(3)]
        mx, top = sb("mx", [P, TT, NB]), sb("top", [P, TT])
        hl, mt, neg = sb("hl", [P, 2, TT], BF16), sb("mt", [2 * TT, P], BF16), sb("neg", [2, NT], BF16)
        one2 = sb("one2", [2, P], BF16)
        kvs = [sb(f"kvs{t}", [P, P]) for t in range(TPB)]
        prob = sb("prob", [P, 6, HALF])
        zero = sb("zero", [1, HALF], BF16)
        rec, o = sb("rec", [P, HALF]), sb("o", [P, HALF])
        odup = sb("odup", [P, NT])
        (kv_ps, kv_sb, g_ps, g_sb, g_parts, init, a_scores, a_maxed, hl_ready, mt_ps, mt_ready, neg_ready, kvs_ready, scores,
         probs, used, pv_done, o_ready, o_in) = (m.sem(f"{name}_{s}") for s in (
             "kvps", "kvsb", "gps", "gsb", "gparts", "init", "ascores", "amaxed", "hl", "mtps", "mt", "neg", "kvs", "scores",
             "probs", "used", "pvdone", "o", "oin"))
        groups = [(g * TT, min(TT, KT - g * TT)) for g in range(-(-KT // TT))]
        with nc.Block() as block:
            @block.tensor
            def _(pe):
                for h in range(2):
                    nc.tensor.matmul(m.ps[:, 4 + h, :], w_out[:], fT[:, h * HALF:(h + 1) * HALF], start=True, stop=True).then_inc(g_ps, 1)
                for i, (t0, n) in enumerate(groups):
                    if i >= 2:
                        pe.wait_ge(kv_sb, i - 1)
                    for t in range(n):
                        ins = nc.tensor.matmul(m.ps[:, i % 2, t * 64:(t + 1) * 64], qimg[:, (t0 + t) * P:(t0 + t + 1) * P], wT[:],
                                               start=True, stop=True)
                    ins.then_inc(kv_ps, 1)

            @block.scalar
            def _(act):
                for h in range(2):
                    act.wait_ge(g_ps, h + 1)
                    nc.scalar.activation(g32[:, h * HALF:(h + 1) * HALF], m.ps[:, 4 + h, :], ACT.Copy, scale=scale).then_inc(g_sb, 1)

            @block.vector
            def _(dve):
                m.dve(dve, nc.vector.memset(kv[:, :, 64:P], 1.0))
                dve.wait_ge(g_sb, 2)
                split3(m, dve, g32[:], gp[0][:], gp[1][:], gp[2][:], rest[:], g_parts)
                for i, (t0, n) in enumerate(groups):
                    dve.wait_ge(kv_ps, i + 1)
                    nc.vector.scalar_tensor_tensor(kv[:, t0:t0 + n, 0:64],
                                                   m.ps[:, i % 2, 0:n * 64].rearrange("p (t c) -> p t c", c=64), scale,
                                                   b_row[:].unsqueeze(1).to_broadcast([P, n, 64]), ALU.mult, ALU.add).then_inc(kv_sb, 1)
                dve.wait_ge(kv_sb, len(groups))
                nc.vector.tensor_scalar(kv[:, KT - 1, :], kv[:, KT - 1, :], m.padm[:, 0:1], None, ALU.mult)
                nc.vector.memset(one2[:], 1.0)
                nc.vector.memset(zero[:], 0.0)

        with nc.Block() as block:
            @block.tensor
            def _(pe):
                with pe.Fori(0, NB) as c:
                    for u in range(4):
                        pe.wait_ge(a_maxed, c * 4 + u + 1)
                        for j in range(2):
                            q = (2 * u + j) * P
                            for i in range(2):
                                ins = nc.tensor.matmul(m.ps[:, 2 * u + j, 0:BLK], gp[i][:, q:q + P],
                                                       qimg[:, bass.ds(c * BLK, BLK)], start=i == 0, stop=i == 1)
                        ins.then_inc(a_scores, 1)
                pe.wait_ge(hl_ready, 1)
                nc.tensor.transpose(m.ps[0:2 * TT, 0, 0:P // 2].bitcast(BF16), hl[:].rearrange("p a b -> p (a b)"),
                                    m.identb[:]).then_inc(mt_ps, 1)

            @block.vector
            def _(dve):
                dve.sem_inc(a_maxed, 4)
                with dve.Fori(0, NB) as c:
                    for u in range(4):
                        dve.wait_ge(a_scores, c * 4 + u + 1)
                        nc.vector.tensor_reduce(mx[:, 2 * u:2 * u + 2, bass.ds(c, 1)], m.ps[:, 2 * u:2 * u + 2, 0:BLK],
                                                AX.X, ALU.max).then_inc(a_maxed, 1)
                dve.wait_ge(a_maxed, 4 * NB + 4)
                m.dve(dve, nc.vector.tensor_reduce(top[:], mx[:], AX.X, ALU.max))
                m.dve(dve, nc.vector.tensor_scalar(hl[:, 0, :], top[:], -1.0, None, ALU.mult))
                nc.vector.scalar_tensor_tensor(hl[:, 1, :], top[:], -1.0, hl[:, 0, :], ALU.mult, ALU.subtract).then_inc(hl_ready, 1)
                dve.wait_ge(mt_ps, 1)
                nc.vector.tensor_copy(mt[:], m.ps[0:2 * TT, 0, 0:P // 2].bitcast(BF16)).then_inc(mt_ready, 1)

            @block.sync
            def _(sp):
                sp.wait_ge(mt_ready, 1)
                sp.dma_start(neg[:], mt[:]).then_inc(neg_ready, 16)
                sp.wait_ge(neg_ready, 16)

        O, D = m.ps[:, 6, :], m.ps[:, 7, :]
        with nc.Block() as block:
            @block.tensor
            def _(pe):
                def value_step(c, t):
                    pe.wait_ge(kvs_ready, c * TPB + t + 1)
                    pe.wait_ge(probs, c * 6 + 2 * t + 2 + 3)
                    for h in range(2):
                        for bank, w in ((O, kvs[t][:, 0:64]), (D, kvs[t][:, 64:P])):
                            ins = nc.tensor.matmul(bank[64 * h:64 * h + 64, :], w, prob[:, 2 * t + h, :], start=False, stop=False)
                    ins.then_inc(used, 1)

                for h in range(2):
                    for bank in (O, D):
                        nc.tensor.matmul(bank[64 * h:64 * h + 64, :], zero[0:1, 0:64], zero[0:1, :], start=True, stop=False)
                pe.sem_inc(used, 3)
                with pe.Fori(0, NB) as c:
                    for i in range(6):
                        t, h = i // 2, i % 2
                        pe.wait_ge(probs, c * 6 + i + 1)
                        x = slice(h * HALF, (h + 1) * HALF)
                        for j in range(3):
                            nc.tensor.matmul(m.ps[:, i % 3, :], qimg[:, bass.ds(c * BLK + t * P, P)], gp[j][:, x],
                                             start=j == 0, stop=False)
                        nc.tensor.matmul(m.ps[:, i % 3, :], one2[:], neg[:, x], start=False, stop=True).then_inc(scores, 1)
                        if i in (3, 5):
                            value_step(c, i // 2 - 1)
                    value_step(c, 2)
                for h in range(2):
                    for bank in (O, D):
                        ins = nc.tensor.matmul(bank[64 * h:64 * h + 64, :], zero[0:1, 0:64], zero[0:1, :], start=False, stop=True)
                ins.then_inc(pv_done, 1)

            @block.scalar
            def _(act):
                act.sem_inc(probs, 3)
                with act.Fori(0, NB) as c:
                    for i in range(6):
                        if i % 2 == 0:
                            act.wait_ge(used, c * TPB + i // 2 + 1)
                        act.wait_ge(scores, c * 6 + i + 1)
                        nc.scalar.activation(prob[:, i, :], m.ps[:, i % 3, :], ACT.Exp, scale=1.0 / float(np.sqrt(P))).then_inc(probs, 1)

            @block.gpsimd
            def _(pool):
                with pool.Fori(0, NB) as c:
                    for t in range(TPB):
                        pool.wait_ge(used, c * TPB + t + 1)
                        nc.gpsimd.tensor_copy(kvs[t][:], kv[:, bass.ds(c * TPB + t, 1), :].rearrange("p a b -> p (a b)")).then_inc(kvs_ready, 1)

            @block.vector
            def _(dve):
                dve.wait_ge(pv_done, 1)
                m.dve(dve, nc.vector.reciprocal(rec[:], D))
                nc.vector.scalar_tensor_tensor(o[:], O, 0.1, rec[:], ALU.mult, ALU.mult).then_inc(o_ready, 1)
                dve.wait_ge(o_in, 64)
                nc.vector.tensor_tensor(fT[:], fT[:], odup[:], ALU.add)

            @block.sync
            def _(sp):
                sp.wait_ge(o_ready, 1)
                for h in range(2):
                    for d in range(2):
                        sp.dma_start(odup[64 * d:64 * d + 64, h * HALF:(h + 1) * HALF], o[64 * h:64 * h + 64, :]).then_inc(o_in, 16)


def vision_mlp(m, fT, avg, wsc, tern, bf1, bf2):
    nc = m.nc
    with ExitStack() as ctx:
        def sb(n, shape, dt=F32):
            return m.sb("vm_" + n, shape, dt, ctx)

        tops, top = sb("tops", [P, 2]), sb("top", [P, 2])
        big, inv, prod, step, inv2, prod2, hmax, htop = (
            sb(n, [P, 1]) for n in ("big", "inv", "prod", "step", "inv2", "prod2", "hmax", "htop"))
        tmp, qf = sb("tmp", [P, NT]), sb("qf", [P, NT], BF16)
        tav, qav = sb("tav", [P, 1]), sb("qav", [P, HALF], BF16)
        hid, qh = sb("hid", [P, 4, NT]), sb("qh", [P, 4, NT], BF16)
        htops = sb("htops", [P, 8])
        yb = sb("yb", [P, TT, P])
        mm, ev, q2, y_ps = (m.sem("vm_" + n) for n in ("mm", "ev", "q2", "y"))
        with nc.Block() as block:
            @block.vector
            def _(dve):
                nc.vector.tensor_reduce(tops[:, 0:1], fT[:], AX.X, ALU.max, apply_absolute_value=True)
                nc.vector.tensor_reduce(tops[:, 1:2], avg[:], AX.X, ALU.max, apply_absolute_value=True)
        all_partitions(m, "f", tops[:], top[:], RMAX)
        with nc.Block() as block:
            @block.vector
            def _(dve):
                nc.vector.tensor_tensor(big[:], top[:, 0:1], top[:, 1:2], ALU.max)
        input_scale(m, big[:], [wsc[:, W_F1:W_F1 + 1]], inv[:], [prod[:]], step[:])
        with nc.Block() as block:
            @block.vector
            def _(dve):
                q = m.sem("vm_q")
                m.dve(dve, nc.vector.tensor_scalar(tmp[:], fT[:], inv[:], MAGIC, ALU.mult, ALU.add))
                m.dve(dve, nc.vector.tensor_scalar(tav[:], avg[:], inv[:], MAGIC, ALU.mult, ALU.add))
                nc.vector.tensor_scalar(qav[:], tav[:].to_broadcast([P, HALF]), MAGIC, 127.0, ALU.subtract, ALU.min).then_inc(q2, 1)
                nc.vector.tensor_scalar(qf[:], tmp[:], MAGIC, 127.0, ALU.subtract, ALU.min).then_inc(q2, 1)
                for i in range(8):
                    dve.wait_ge(ev, i + 1)
                    ins = nc.vector.tensor_reduce(htops[:, i:i + 1], hid[:, i // 2, i % 2 * HALF:(i % 2 + 1) * HALF], AX.X, ALU.max)
                m.dve(dve, ins)
                nc.vector.tensor_reduce(hmax[:], htops[:], AX.X, ALU.max)

            @block.tensor
            def _(pe):
                pe.wait_ge(q2, 2)
                for i in range(8):
                    c, h = i // 2, i % 2
                    if i >= 4:
                        pe.wait_ge(ev, i - 3)
                    nc.tensor.matmul(m.ps[:, i % 4, :], tern[W_F1][:, c * P:(c + 1) * P], qf[:, h * HALF:(h + 1) * HALF], start=True, stop=False)
                    nc.tensor.matmul(m.ps[:, i % 4, :], tern[W_F1][:, FF0 + c * P:FF0 + (c + 1) * P], qav[:], start=False,
                                     stop=True).then_inc(mm, 1)

            @block.scalar
            def _(act):
                for i in range(8):
                    act.wait_ge(mm, i + 1)
                    nc.scalar.activation(hid[:, i // 2, i % 2 * HALF:(i % 2 + 1) * HALF], m.ps[:, i % 4, :], ACT.Relu,
                                         scale=prod[:, 0:1], bias=bf1[:, i // 2:i // 2 + 1]).then_inc(ev, 1)
        all_partitions(m, "h", hmax[:], htop[:], RMAX)
        input_scale(m, htop[:], [wsc[:, W_F2:W_F2 + 1]], inv2[:], [prod2[:]], step[:])
        with nc.Block() as block:
            @block.vector
            def _(dve):
                q = 0
                for c in range(4):
                    m.dve(dve, nc.vector.tensor_scalar(hid[:, c, :], hid[:, c, :], inv2[:], MAGIC, ALU.mult, ALU.add))
                    ins = nc.vector.tensor_scalar(qh[:, c, :], hid[:, c, :], MAGIC, 127.0, ALU.subtract, ALU.min)
                ins.then_inc(y_ps, 1)
                dve.wait_ge(y_ps, 2)
                yp = m.ps[:, 4:6, :].rearrange("p a (b c) -> p (a b) c", c=P)
                nc.vector.scalar_tensor_tensor(yb[:], yp, prod2[:, 0:1], bf2[:].unsqueeze(1).to_broadcast([P, TT, P]), ALU.mult, ALU.add)

            @block.tensor
            def _(pe):
                pe.wait_ge(y_ps, 1)
                for t in range(TT):
                    for c in range(4):
                        ins = nc.tensor.matmul(m.ps[:, 4 + t // 4, t % 4 * P:(t % 4 + 1) * P], qh[:, c, t * P:(t + 1) * P],
                                               tern[W_F2][:, c * P:(c + 1) * P], start=c == 0, stop=c == 3)
                ins.then_inc(y_ps, 1)
        layernorm(m, "ln4", yb)


STAGES = [deform_attention, cross_attention, experts_gelu, s4_layer, vision_attention, experts_silu]


def decoder_kernel(nc, a, out, first=0, last=6):
    with ExitStack() as ctx:
        m = Machine(nc, ctx, a)
        m.out = out
        setup(m)
        for s in STAGES[first:last]:
            s(m)
            m.end_stage()
        if last < 6:
            done = m.sem("dbg")
            with nc.Block() as block:
                @block.sync
                def _(sp):
                    sp.dma_start(out.rearrange("(t p) d -> p t d", p=P), m.xtok[:]).then_inc(done, 16)
                    sp.wait_ge(done, 16)


def layout(i):
    f = np.float32

    def row(v):
        return np.reshape(v, (1, -1))

    def col(v):
        return np.reshape(v, (-1, 1))

    def both(v):
        return np.concatenate([v.T, v.T], 0)

    x = i["x"][0]
    re = (np.arange(P) < NS).astype(f)
    l = np.arange(NT)
    turn = np.outer(l, l) % (2 * NF) * (np.pi / NF)
    alt = (1 - 2 * (l % 2)).astype(f)
    quarter, zero = np.full(P, 0.25, f), np.zeros(P, f)
    a = {
        "c_ident": np.eye(P, dtype=f), "c_iota": np.arange(P, dtype=f).reshape(P, 1),
        "c_pad": (np.arange(P) < LASTV).astype(f).reshape(P, 1),
        "c_flip": np.eye(HPO, dtype=f)[::-1],
        "x_tok": x, "x_T": x.T, "ctx_T": i["ctx_768"][0].T,
        "da_w": np.concatenate([i["L0_attn_W_off"][:, 0::2], i["L0_attn_W_attn"]], 1),
        "da_b": row(np.concatenate([i["L0_attn_b_off"][0::2], i["L0_attn_b_attn"]])),
        "da_wout": i["L0_attn_W_out"], "da_bout": row(i["L0_attn_b_out"]),
        "ca_wk": np.concatenate([i["L0_xattn_wk"].T, row(i["L0_xattn_bk"])], 0),
        "ca_wv": np.concatenate([i["L0_xattn_wv"].T, row(i["L0_xattn_bv"])], 0),
        "ca_wq": i["L0_xattn_wq"].T, "ca_bq": col(i["L0_xattn_bq"]),
        "c_rev": np.tile(np.arange(NE, 0, -1, dtype=f), (P, 1)),
        "m0_gate": i["L0_ffn_gate_w"], "m0_w1": i["L0_ffn_w1"], "m0_w2": i["L0_ffn_w2"],
        "m0_b1": i["L0_ffn_b1"].reshape(NE, FF0 // P, P).transpose(0, 2, 1), "m0_b2": i["L0_ffn_b2"].T,
        "m1_gate": i["L1_ffn_gate_w"].T, "m1_wg": i["L1_ffn_w_gate"], "m1_wu": i["L1_ffn_w_up"], "m1_wd": i["L1_ffn_w_down"],
        "c_s4": np.stack([quarter * re, np.pi / 2 * re, quarter * (1 - re), np.pi / 2 * (1 - re), 4 * re - 2, zero, zero, zero],
                         1).astype(f),
        "c_bsteps": np.tile(np.arange(32, dtype=f), (P, 1)), "c_asteps": np.tile(np.arange(0, NT, 32, dtype=f), (P, 1)),
        "c_dft": np.concatenate([np.cos(turn), np.sin(turn)], 1).astype(f), "c_altc": alt[0:P].reshape(P, 1), "c_altr": row(alt),
        "s4_ldt": np.broadcast_to(i["L1_attn_log_dt"], (P, P)), "s4_arl": both(i["L1_attn_A_real_log"]),
        "s4_aim": both(i["L1_attn_A_imag"]), "s4_cre": both(i["L1_attn_C_real"]), "s4_cim": both(i["L1_attn_C_imag"]),
        "s4_d": col(i["L1_attn_D"]), "s4_wout": i["L1_attn_W_out"], "s4_bout": row(i["L1_attn_b_out"]),
        "va_w0": i["L1_xattn_W_d2v"].T, "va_w1": i["L1_xattn_W_img"].T, "va_w2": i["L1_xattn_W_txt"].T,
        "va_w3": i["L1_xattn_W_att0"].T, "va_w4": i["L1_xattn_W_att1"].T,
        "va_w5": i["L1_xattn_W_f1"].T.reshape(2, P, FF0).transpose(1, 0, 2).reshape(P, 2 * FF0),
        "va_w6": i["L1_xattn_W_f2"].T.reshape(4, P, P).transpose(1, 0, 2).reshape(P, 4 * P),
        "va_wo0": np.concatenate([i["L1_xattn_W_att0"]] * 2, 0), "va_wo1": np.concatenate([i["L1_xattn_W_att1"]] * 2, 0),
        "c_inv": np.tile(np.array([1 / (CD * P), 1 / (P * P), 1 / (P * P), 1 / (64 * P), 1 / (64 * P), 1 / (2 * P * FF0), 1 / (P * FF0)], f), (P, 1)),
        "va_bias": np.stack([i["L1_xattn_b_d2v"], i["L1_xattn_b_img"], i["L1_xattn_b_txt"]], 1),
        "va_batt0": np.broadcast_to(i["L1_xattn_b_att0"], (P, 64)), "va_batt1": np.broadcast_to(i["L1_xattn_b_att1"], (P, 64)),
        "va_bf1": i["L1_xattn_b_f1"].reshape(4, P).T, "va_bf2": np.broadcast_to(i["L1_xattn_b_f2"], (P, P)),
        "ca_wo": i["L0_xattn_wo"].T, "ca_bo": row(i["L0_xattn_bo"]),
    }
    return {k: np.ascontiguousarray(v) for k, v in a.items()}


def kernel(**inputs):
    import concourse.bacc as bacc
    from concourse.bass_utils import run_bass_kernel_spmd

    arrays = layout({k: np.asarray(v) for k, v in inputs.items()})
    nc = bacc.Bacc("TRN2", target_bir_lowering=False, num_devices=1)
    a = {k: nc.dram_tensor(k, v.shape, mybir.dt.from_np(v.dtype), kind="ExternalInput").ap() for k, v in arrays.items()}
    out = nc.dram_tensor("out", (NT, P), F32, kind="ExternalOutput").ap()
    decoder_kernel(nc, a, out)
    r = run_bass_kernel_spmd(nc, [arrays], core_ids=[0])
    return np.reshape(r.results[0]["out"], (1, NT, P))
```

```python
from contextlib import ExitStack

import numpy as np

import concourse.bass as bass
from concourse import mybir

F32 = mybir.dt.float32
BF16 = mybir.dt.bfloat16
ALU = mybir.AluOpType
ACT = mybir.ActivationFunctionType
AX = mybir.AxisListType
RADD = bass.bass_isa.ReduceOp.add
RMAX = bass.bass_isa.ReduceOp.max

P = 128
NT = 1024
TT = NT // P
HALF = 512
KV = 6404
KT = -(-KV // P)
KP = KT * P
CD = 96
TPB = 3
NB = KT // TPB
BLK = TPB * P
LASTV = KV - (KT - 1) * P
NH, HD = 16, 8
NPAIR = NH // 2
HPO = 32
NE = 8
FF0, FF1 = 512, 256
NF = 1024
NS = 64
MAGIC = 12582912.0
TWO_PI = 6.283185307179586
TWO_PI_HI = 6.28125
TWO_PI_LO = TWO_PI - TWO_PI_HI
PI_BELOW = 3.1415925
LN2 = 0.6931471805599453
LN2_HI = 0.693359375
LN2_LO = LN2 - LN2_HI
EPS = 1e-5
BIG = 1.0e38
Q_PART = (0, 0, 1, 1, 0, 2)
K_PART = (0, 1, 0, 1, 2, 0)
SPLIT_ROWS = len(Q_PART) * HD
ATTENTION_STEP = "s0 s1 m0 s2 m1 v2 m2 s3 s4 s5 m3 s6 m4 v0 m5 s7 s8 s9 m6 s10 m7 v1 s11"


class Chain:

    def __init__(self, sem):
        self.sem, self.n = sem, 0

    def __call__(self, eng, ins):
        self.n += 1
        ins.then_inc(self.sem, 1)
        eng.wait_ge(self.sem, self.n)


class Machine:

    def __init__(self, nc, ctx, a):
        self.nc, self.ctx, self.a = nc, ctx, a
        self.stage_sems = []
        self.ps = ctx.enter_context(nc.psum_tensor("ps", [P, 8, 512], F32))
        self.ident = self.sb("ident", [P, P])
        self.identb = self.sb("identb", [P, P], BF16)
        self.ones_row = self.sb("ones_row", [1, HALF])
        self.eps = self.sb("eps", [P, 1])
        self.xtok = self.sb("xtok", [P, TT, P])
        self.xT = self.sb("xT", [P, NT])
        self.padm = self.sb("padm", [P, 1])
        self.dve = Chain(self.sem("dve_own"))
        self.act = Chain(self.sem("act_own"))
        self.pool = Chain(self.sem("pool_own"))
        self.stage_sems = []

    def sb(self, name, shape, dt=F32, ctx=None):
        return (ctx or self.ctx).enter_context(self.nc.sbuf_tensor(name + "_sb", shape, dt))

    def sem(self, name):
        self.stage_sems.append(self.nc.alloc_semaphore(name))
        return self.stage_sems[-1]

    def end_stage(self):
        self.nc.clear_and_free_semaphores(self.stage_sems)
        self.nc.all_engine_barrier()
        self.stage_sems = []


def setup(m):
    nc, a = m.nc, m.a
    loaded = m.sem("setup_loaded")
    with nc.Block() as block:
        @block.sync
        def _(sp):
            sp.dma_start(m.ident[:], a["c_ident"]).then_inc(loaded, 16)
            sp.dma_start(m.padm[:], a["c_pad"]).then_inc(loaded, 16)
            sp.dma_start(m.xtok[:], a["x_tok"].rearrange("(t p) d -> p t d", p=P)).then_inc(loaded, 16)
            sp.dma_start(m.xT[:], a["x_T"]).then_inc(loaded, 16)

        @block.vector
        def _(dve):
            nc.vector.memset(m.ones_row[:], 1.0)
            nc.vector.memset(m.eps[:], EPS)
            dve.wait_ge(loaded, 64)
            nc.vector.tensor_copy(m.identb[:], m.ident[:])


def layernorm(m, name, y, out=None):
    nc = m.nc
    with ExitStack() as ctx:
        res = m.sb(name + "_res", [P, TT, P], ctx=ctx)
        stats = m.sb(name + "_stats", [P, TT, 6], ctx=ctx)
        mv = m.sb(name + "_mv", [P, TT, 2], ctx=ctx)
        std = m.sb(name + "_std", [P, TT], ctx=ctx)
        rstd = m.sb(name + "_rstd", [P, TT], ctx=ctx)
        var_ready, std_ready, x_ready, xt_ps, stored = (
            m.sem(f"{name}_{s}") for s in ("var", "std", "x", "xt", "stored"))
        block = ctx.enter_context(nc.Block())

        @block.vector
        def _(dve):
            for g in range(2):
                m.dve(dve, nc.vector.tensor_tensor(res[:, 4 * g:4 * g + 4, :], y[:, 4 * g:4 * g + 4, :],
                                                   m.xtok[:, 4 * g:4 * g + 4, :], ALU.add))
            for t in range(TT):
                m.dve(dve, nc.vector.bn_stats(stats[:, t, :], res[:, t, :]))
            for t in range(TT):
                last = nc.vector.bn_aggr(mv[:, t, :], stats[:, t, :])
                last.then_inc(var_ready, 1)
            dve.wait_ge(std_ready, 1)
            m.dve(dve, nc.vector.reciprocal(rstd[:], std[:]))
            for t in range(TT):
                nc.vector.tensor_scalar(m.xtok[:, t, :], res[:, t, :], mv[:, t, 0:1], rstd[:, t:t + 1],
                                        ALU.subtract, ALU.mult).then_inc(x_ready, 1)
            if out is None:
                dve.wait_ge(xt_ps, 1)
                nc.vector.tensor_copy(m.xT[:, 0:HALF], m.ps[:, 6, :])

        @block.scalar
        def _(act):
            act.wait_ge(var_ready, TT)
            nc.scalar.activation(std[:], mv[:, :, 1], ACT.Sqrt, bias=m.eps[:, 0:1]).then_inc(std_ready, 1)
            if out is None:
                act.wait_ge(xt_ps, 2)
                nc.scalar.activation(m.xT[:, HALF:NT], m.ps[:, 7, :], ACT.Copy)

        @block.tensor
        def _(pe):
            if out is None:
                for t in range(TT):
                    pe.wait_ge(x_ready, t + 1)
                    ins = nc.tensor.transpose(m.ps[:, 6 + t // 4, (t % 4) * P:(t % 4 + 1) * P], m.xtok[:, t, :], m.ident[:])
                    if t % 4 == 3:
                        ins.then_inc(xt_ps, 1)

        @block.sync
        def _(sp):
            if out is not None:
                sp.wait_ge(x_ready, TT)
                sp.dma_start(out.rearrange("(t p) d -> p t d", p=P), m.xtok[:]).then_inc(stored, 16)
                sp.wait_ge(stored, 16)


def deform_attention(m):
    nc, a = m.nc, m.a
    with ExitStack() as ctx:
        def sb(name, shape, dt=F32):
            return m.sb("da_" + name, shape, dt, ctx)

        w = sb("w", [P, 2 * HPO])
        b = sb("b", [1, 2 * HPO])
        wout = sb("wout", [P, P])
        bout = sb("bout", [1, P])
        iota = sb("iota", [P, 1])
        ones = sb("ones", [P, HPO])
        sh = [P, TT, HPO]
        lg, off, mag, fl, gt, sg, neg, idx, prob = (sb(n, sh) for n in ("lg", "off", "mag", "fl", "gt", "sg", "neg", "idx", "prob"))
        mx, den = sb("mx", [P, TT * 8]), sb("den", [P, TT * 8])
        x0r = sb("x0r", [P, 1])
        zx = [sb(f"zx{s}", [P, P + HPO], BF16) for s in range(3)]
        flip = sb("flip", [HPO, HPO])
        sel = sb("sel", [HPO, HPO, P], BF16)
        idxT = sb("idxT", [HPO, NT], BF16)
        wT = sb("wT", [HPO, NT])
        hot = sb("hot", [P, 2, HALF], BF16)
        gw = sb("gw", [HPO, NT])
        cs = sb("cs", [HPO, P])
        loaded, proj, lg_ready, e_ready, t_ready, tps, oh_in, bc, oh, cs_ps, gsum, gw_ready = (
            m.sem("da_" + s) for s in ("loaded", "proj", "lg", "exp", "tok", "tps", "ohin", "bcast", "onehot", "cs", "gsum", "gw"))
        op = m.ps[:, 0, :].rearrange("p (t c) -> p t c", t=TT)

        def g4(t):
            return t[:].rearrange("p t (h q) -> p (t h) q", q=4)

        def b4(t):
            return t[:].unsqueeze(2).to_broadcast([P, TT * 8, 4])

        with nc.Block() as block:
            @block.sync
            def _(sp):
                for dst, src in ((w, "da_w"), (b, "da_b"), (wout, "da_wout"), (bout, "da_bout"), (iota, "c_iota"),
                                 (flip, "c_flip")):
                    sp.dma_start(dst[:], a[src]).then_inc(loaded, 16)

            @block.tensor
            def _(pe):
                pe.wait_ge(loaded, 96)
                for t in range(TT):
                    nc.tensor.matmul(op[:, t, :], m.xT[:, t * P:(t + 1) * P], w[:], start=True, stop=False)
                    nc.tensor.matmul(op[:, t, :], m.ones_row[0:1, 0:P], b[:], start=False, stop=True).then_inc(proj, 1)
                pe.wait_ge(t_ready, 2)
                for t in range(TT):
                    c = slice((t % 4) * P, (t % 4 + 1) * P)
                    nc.tensor.transpose(m.ps[0:HPO, 1 + t // 4, c], idx[:, t, :], m.ident[:])
                    nc.tensor.transpose(m.ps[0:HPO, 3 + t // 4, c], prob[:, t, :], m.ident[:]).then_inc(tps, 1)
                pe.wait_ge(oh_in, 1)
                nc.tensor.matmul(m.ps[0:HPO, 5, 0:P], ones[:], wout[:], start=True, stop=True).then_inc(cs_ps, 1)

            @block.vector
            def _(dve):
                def own(ins):
                    m.dve(dve, ins)

                nc.vector.memset(ones[:], 1.0).then_inc(oh_in, 1)
                for z in zx:
                    own(nc.vector.memset(z[:], 0.0))
                own(nc.vector.tensor_copy(zx[0][:, HPO - 1:HPO], m.xT[:, 0:1]))
                own(nc.vector.tensor_tensor(x0r[:], m.xT[:, 0:1], zx[0][:, HPO - 1:HPO], ALU.subtract))
                own(nc.vector.tensor_copy(zx[1][:, HPO - 1:HPO], x0r[:]))
                own(nc.vector.tensor_tensor(zx[2][:, HPO - 1:HPO], x0r[:], zx[1][:, HPO - 1:HPO], ALU.subtract))
                dve.wait_ge(loaded, 96)
                own(nc.vector.tensor_copy(sel[:], flip[:].unsqueeze(2).to_broadcast([HPO, HPO, P])))
                dve.wait_ge(proj, TT)
                own(nc.vector.tensor_copy(lg[:], op[:, :, HPO:2 * HPO]))
                own(nc.vector.tensor_reduce(mx[:], g4(lg), AX.X, ALU.max))
                nc.vector.tensor_tensor(g4(lg), g4(lg), b4(mx), ALU.subtract).then_inc(lg_ready, 1)
                own(nc.vector.tensor_copy(off[:], op[:, :, 0:HPO]))
                own(nc.vector.scalar_tensor_tensor(mag[:], off[:], -1.0, off[:], ALU.mult, ALU.max))
                own(nc.vector.tensor_scalar(mag[:], mag[:], 1000.0, None, ALU.min))
                own(nc.vector.tensor_scalar(fl[:], mag[:], MAGIC, MAGIC, ALU.add, ALU.subtract))
                own(nc.vector.tensor_tensor(gt[:], fl[:], mag[:], ALU.is_gt))
                own(nc.vector.tensor_tensor(fl[:], fl[:], gt[:], ALU.subtract))
                own(nc.vector.tensor_scalar(sg[:], off[:], 0.0, -2.0, ALU.is_lt, ALU.mult))
                own(nc.vector.tensor_scalar(sg[:], sg[:], 1.0, None, ALU.add))
                own(nc.vector.tensor_tensor(fl[:], fl[:], sg[:], ALU.mult))
                own(nc.vector.tensor_scalar(neg[:], fl[:], 0.0, float(P), ALU.is_lt, ALU.mult))
                own(nc.vector.tensor_tensor(fl[:], fl[:], neg[:], ALU.add))
                nc.vector.tensor_scalar(idx[:], fl[:], 0.0, float(P - 1), ALU.max, ALU.min).then_inc(t_ready, 1)
                dve.wait_ge(e_ready, 1)
                own(nc.vector.tensor_reduce(den[:], g4(lg), AX.X, ALU.add))
                own(nc.vector.reciprocal(den[:], den[:]))
                nc.vector.tensor_tensor(g4(prob), g4(lg), b4(den), ALU.mult).then_inc(t_ready, 1)
                dve.wait_ge(tps, TT)
                nc.vector.tensor_copy(idxT[:], m.ps[0:HPO, 1:3, :].rearrange("p a b -> p (a b)"))
                nc.vector.tensor_copy(wT[:], m.ps[0:HPO, 3:5, :].rearrange("p a b -> p (a b)"))
                dve.wait_ge(cs_ps, 1)
                nc.vector.tensor_copy(cs[:], m.ps[0:HPO, 5, 0:P])

            @block.scalar
            def _(act):
                act.wait_ge(lg_ready, 1)
                nc.scalar.activation(lg[:], lg[:], ACT.Exp).then_inc(e_ready, 1)

        with nc.Block() as block:
            @block.tensor
            def _(pe):
                for h in range(2):
                    nc.tensor.matmul(m.ps[:, 2 + h, :], zx[0][0:HPO, HPO:HPO + P], idxT[:, 0:HALF], start=True, stop=False)
                with pe.Fori(0, HPO) as k:
                    for h in range(2):
                        nc.tensor.matmul(m.ps[:, h, :], sel[:, bass.ds(k, 1), :].rearrange("p a b -> p (a b)"),
                                         idxT[:, h * HALF:(h + 1) * HALF], start=True, stop=True).then_inc(bc, 1)
                    for h in range(2):
                        pe.wait_ge(oh, k * 2 + h + 1)
                        for s in range(3):
                            ins = nc.tensor.matmul(m.ps[:, 2 + h, :], zx[s][:, bass.ds(k, P)],
                                                   hot[:, h, :], start=False, stop=False)
                        ins.then_inc(gsum, 1)
                for h in range(2):
                    nc.tensor.matmul(m.ps[:, 2 + h, :], zx[0][0:HPO, HPO:HPO + P], idxT[:, 0:HALF],
                                     start=False, stop=True).then_inc(gsum, 1)
                pe.wait_ge(gw_ready, 1)
                for t in range(TT):
                    o = m.ps[:, 4 + t // 4, (t % 4) * P:(t % 4 + 1) * P]
                    nc.tensor.matmul(o, gw[:, t * P:(t + 1) * P], cs[:], start=True, stop=False)
                    nc.tensor.matmul(o, m.ones_row[0:1, 0:P], bout[:], start=False, stop=True)

            @block.vector
            def _(dve):
                with dve.Fori(0, HPO) as k:
                    for h in range(2):
                        dve.wait_ge(bc, k * 2 + h + 1)
                        nc.vector.tensor_scalar(hot[:, h, :], m.ps[:, h, :], iota[:, 0:1], None, ALU.is_equal).then_inc(oh, 1)
                dve.wait_ge(gsum, 2 * HPO + 2)
                nc.vector.tensor_tensor(gw[:], m.ps[0:HPO, 2:4, :].rearrange("p a b -> p (a b)"), wT[:], ALU.mult).then_inc(gw_ready, 1)
        layernorm(m, "ln0", m.ps[:, 4:6, :].rearrange("p a (b c) -> p (a b) c", c=P))


def split3(m, dve, src, p1, p2, p3, rest, done):
    nc = m.nc
    m.dve(dve, nc.vector.tensor_copy(p1, src))
    m.dve(dve, nc.vector.tensor_tensor(rest, src, p1, ALU.subtract))
    m.dve(dve, nc.vector.tensor_copy(p2, rest))
    nc.vector.tensor_tensor(p3, rest, p2, ALU.subtract).then_inc(done, 1)


def cross_attention(m):
    nc, a = m.nc, m.a
    with ExitStack() as ctx:
        def sb(name, shape, dt=F32, c=ctx):
            return m.sb("ca_" + name, shape, dt, c)

        sem = {n: m.sem("ca_" + n) for n in (
            "loaded", "k_ps", "k_sb", "k_parts", "k_stored0", "k_stored1", "v_ps", "v_sb", "ones", "k_stacked", "q_ps", "q_sb", "q_parts",
            "q_stored", "q_stacked", "cleared", "ks_filled")}
        c0 = ctx.enter_context(ExitStack())
        ks = sb("ks", [P, NPAIR * KP], BF16, c0)
        vs = sb("vs", [P, KT, NH, HD + 1], F32, c0)
        q_stack = sb("qs", [P, 2, NPAIR * NT], BF16, c0)
        qs = [q_stack[:, h, :] for h in range(2)]
        prob = sb("prob", [P, 12, HALF], F32, c0)
        kd = nc.dram_tensor("k_parts", (3, P, KP), BF16, kind="Internal").ap()
        qd = nc.dram_tensor("q_parts", (3, P, NT), BF16, kind="Internal").ap()
        od = nc.dram_tensor("pair_sums", (P, NPAIR * HALF), F32, kind="Internal").ap()
        chunks = [(c * HALF, min(HALF, KP - c * HALF)) for c in range(-(-KP // HALF))]

        with ExitStack() as c1:
            ctxT = q_stack[:].rearrange("p h n -> p (h n)").bitcast(F32)[0:CD + 1, 0:KP]
            wk = sb("wk", [CD + 1, P], F32, c1)
            wv = sb("wv", [CD + 1, P], F32, c1)
            wq = sb("wq", [P, P], F32, c1)
            bq = sb("bq", [P, 1], F32, c1)
            table_warm = sb("table_warm", [P, 1], F32, c1)
            k32 = prob[:, 0:2, :]
            rest = prob[:, 2, :]
            kp = prob[:, 3:6, :].rearrange("p a b -> p (a b)").bitcast(BF16).rearrange("p (i s n) -> p i s n", i=2, s=3)
            block = c1.enter_context(nc.Block())
            n_k = len(chunks)

            @block.sync
            def _(sp):
                sp.dma_start(ctxT[0:CD, 0:KV], a["ctx_T"]).then_inc(sem["loaded"], 16)
                sp.dma_start(ctxT[0:CD, KV:KP], a["ctx_T"][:, 0:KP - KV]).then_inc(sem["loaded"], 16)
                for dst, src in ((wk, "ca_wk"), (wv, "ca_wv"), (wq, "ca_wq"), (bq, "ca_bq")):
                    sp.dma_start(dst[:], a[src]).then_inc(sem["loaded"], 16)
                for i, (c, n) in enumerate(chunks):
                    sp.wait_ge(sem["k_parts"], i + 1)
                    sp.dma_start(kd[:, :, c:c + n].rearrange("s p n -> p s n"), kp[:, i % 2, :, 0:n]).then_inc(sem[f"k_stored{i % 2}"], 16)
                for i in range(2):
                    sp.wait_ge(sem["k_parts"], n_k + i + 1)
                    sp.dma_start(qd[:, :, i * HALF:(i + 1) * HALF].rearrange("s p n -> p s n"),
                                 kp[:, (n_k + i) % 2, :, :]).then_inc(sem[f"k_stored{(n_k + i) % 2}"], 16)
                sp.wait_ge(sem["k_stored0"], 16 * ((n_k + 3) // 2))
                sp.wait_ge(sem["k_stored1"], 16 * ((n_k + 2) // 2))
                sp.wait_ge(sem["ks_filled"], 1)
                for part in range(len(Q_PART)):
                    for h in range(2):
                        r = 64 * h + HD * part
                        sp.dma_start(ks[r:r + HD, :].rearrange("p (g n) -> p g n", g=NPAIR),
                                     kd[K_PART[part]].rearrange("(g h d) n -> h d g n", h=2, d=HD)[h]).then_inc(sem["k_stacked"], 16)
                sp.wait_ge(sem["cleared"], 2)
                for part in range(len(Q_PART)):
                    for h in range(2):
                        r = 64 * h + HD * part
                        sp.dma_start(qs[h][r:r + HD, :].rearrange("p (g n) -> p g n", g=NPAIR),
                                     qd[Q_PART[part]].rearrange("(g h d) n -> h d g n", h=2, d=HD)[h]).then_inc(sem["q_stacked"], 16)
                sp.wait_ge(sem["k_stacked"], 16 * 12)
                sp.wait_ge(sem["q_stacked"], 16 * 12)

            @block.tensor
            def _(pe):
                pe.wait_ge(sem["loaded"], 96)
                pe.wait_ge(sem["ones"], 1)
                for i, (c, n) in enumerate(chunks):
                    if i >= 2:
                        pe.wait_ge(sem["k_sb"], i - 1)
                    nc.tensor.matmul(m.ps[:, i % 2, 0:n], wk[:], ctxT[:, c:c + n], start=True, stop=True).then_inc(sem["k_ps"], 1)
                for h in range(2):
                    i = n_k + h
                    pe.wait_ge(sem["k_sb"], i - 1)
                    nc.tensor.matmul(m.ps[:, i % 2, :], wq[:], m.xT[:, h * HALF:(h + 1) * HALF],
                                     start=True, stop=True).then_inc(sem["k_ps"], 1)
                for t in range(KT):
                    if t % 4 == 0 and t >= 8:
                        pe.wait_ge(sem["v_sb"], t // 4 - 1)
                    ins = nc.tensor.matmul(m.ps[:, 2 + t // 4 % 2, (t % 4) * P:(t % 4 + 1) * P], ctxT[:, t * P:(t + 1) * P], wv[:],
                                           start=True, stop=True)
                    if t % 4 == 3 or t == KT - 1:
                        ins.then_inc(sem["v_ps"], 1)

            @block.scalar
            def _(act):
                nc.scalar.activation(table_warm[:], m.eps[:], ACT.Exp)
                act.wait_ge(sem["loaded"], 96)
                for i, (c, n) in enumerate(chunks + [(0, HALF), (HALF, HALF)]):
                    act.wait_ge(sem["k_ps"], i + 1)
                    if i >= 2:
                        act.wait_ge(sem["k_parts"], i - 1)
                    if i < n_k:
                        nc.scalar.activation(k32[:, i % 2, 0:n], m.ps[:, i % 2, 0:n], ACT.Identity).then_inc(sem["k_sb"], 1)
                    else:
                        nc.scalar.activation(k32[:, i % 2, :], m.ps[:, i % 2, :], ACT.Identity, bias=bq[:, 0:1]).then_inc(sem["k_sb"], 1)
                for g in range(-(-KT // 4)):
                    n = min(4, KT - 4 * g)
                    act.wait_ge(sem["v_ps"], g + 1)
                    ins = nc.scalar.activation(vs[:, 4 * g:4 * g + n, :, 0:HD],
                                               m.ps[:, 2 + g % 2, 0:n * P].rearrange("p (t h d) -> p t h d", h=NH, d=HD), ACT.Copy)
                    ins.then_inc(sem["v_sb"], 1)

            @block.vector
            def _(dve):
                nc.vector.memset(ctxT[CD:CD + 1, :], 1.0).then_inc(sem["ones"], 1)
                for i, (c, n) in enumerate(chunks + [(0, HALF), (HALF, HALF)]):
                    dve.wait_ge(sem["k_sb"], i + 1)
                    if i >= 2:
                        dve.wait_ge(sem[f"k_stored{i % 2}"], 16 * (i // 2))
                    split3(m, dve, k32[:, i % 2, 0:n], kp[:, i % 2, 0, 0:n], kp[:, i % 2, 1, 0:n], kp[:, i % 2, 2, 0:n],
                           rest[:, 0:n], sem["k_parts"])
                    dve.wait_ge(sem["k_parts"], i + 1)
                dve.wait_ge(sem["v_ps"], -(-KT // 4))
                dve.wait_ge(sem["k_ps"], n_k + 2)
                for h in range(2):
                    nc.vector.memset(qs[h], 0.0).then_inc(sem["cleared"], 1)
                dve.wait_ge(sem["v_sb"], -(-KT // 4))
                m.dve(dve, nc.vector.memset(vs[:, :, :, HD:HD + 1], 1.0))
                nc.vector.tensor_scalar(vs[:, KT - 1, :, :], vs[:, KT - 1, :, :], m.padm[:, 0:1], None, ALU.mult)

            @block.gpsimd
            def _(pool):
                nc.gpsimd.memset(ks[:], 1.0).then_inc(sem["ks_filled"], 1)

        attention_loop(m, c0, ks, vs, qs, prob, od)
        c0.close()

        with ExitStack() as c2:
            ao = sb("ao", [P, NPAIR, HALF], F32, c2)
            rec = sb("rec", [P, 2, 16], F32, c2)
            att = sb("att", [P, TT, P], F32, c2)
            attT = sb("attT", [P, NT], F32, c2)
            wo = sb("wo", [P, P], F32, c2)
            bo = sb("bo", [1, P], F32, c2)
            tr, nrm, atr, acp, ld, back = (m.sem("ca_" + s) for s in ("o_tr", "o_nrm", "o_atr", "o_acp", "o_loaded", "o_back"))
            block = c2.enter_context(nc.Block())

            @block.sync
            def _(sp):
                sp.dma_start(ao[:], od.rearrange("p (g n) -> p g n", g=NPAIR)).then_inc(back, 16)
                sp.dma_start(wo[:], a["ca_wo"]).then_inc(ld, 16)
                sp.dma_start(bo[:], a["ca_bo"]).then_inc(ld, 16)

            @block.tensor
            def _(pe):
                pe.wait_ge(back, 16)
                for g in range(NPAIR):
                    if g >= 2:
                        pe.wait_ge(nrm, 2 * (g - 1))
                    for c in range(4):
                        ins = nc.tensor.transpose(m.ps[:, g % 2, c * P:(c + 1) * P], ao[:, g, c * P:(c + 1) * P], m.ident[:])
                    ins.then_inc(tr, 1)
                pe.wait_ge(nrm, 2 * NPAIR)
                for t in range(TT):
                    ins = nc.tensor.transpose(m.ps[:, 2 + t // 4, (t % 4) * P:(t % 4 + 1) * P], att[:, t, :], m.ident[:])
                ins.then_inc(atr, 1)
                pe.wait_ge(acp, 2)
                pe.wait_ge(ld, 32)
                for t in range(TT):
                    o = m.ps[:, 4 + t // 4, (t % 4) * P:(t % 4 + 1) * P]
                    nc.tensor.matmul(o, attT[:, t * P:(t + 1) * P], wo[:], start=True, stop=False)
                    nc.tensor.matmul(o, m.ones_row[0:1, 0:P], bo[:], start=False, stop=True)

            @block.vector
            def _(dve):
                for g in range(NPAIR):
                    dve.wait_ge(tr, g + 1)
                    t = m.ps[:, g % 2, :].rearrange("p (c k r) -> p c k r", c=4, k=4)
                    r = rec[:, g % 2, :].rearrange("p (c k) -> p c k", c=4)
                    m.dve(dve, nc.vector.reciprocal(r.unsqueeze(3), t[:, :, :, HD:HD + 1]))
                    for h in range(2):
                        o = att[:, :, (2 * g + h) * HD:(2 * g + h + 1) * HD].rearrange("p (a c) d -> p c a d", a=2)
                        nc.vector.tensor_tensor(o, t[:, :, 2 * h:2 * h + 2, 0:HD],
                                                r[:, :, 2 * h:2 * h + 2].unsqueeze(3).to_broadcast([P, 4, 2, HD]),
                                                ALU.mult).then_inc(nrm, 1)
                dve.wait_ge(atr, 1)
                nc.vector.tensor_copy(attT[:, 0:HALF], m.ps[:, 2, :]).then_inc(acp, 1)

            @block.scalar
            def _(act):
                act.wait_ge(atr, 1)
                nc.scalar.activation(attT[:, HALF:NT], m.ps[:, 3, :], ACT.Copy).then_inc(acp, 1)
    layernorm(m, "ln1", m.ps[:, 4:6, :].rearrange("p a (b c) -> p (a b) c", c=P))


def attention_loop(m, ctx, ks, vs, qs, prob, od):
    nc = m.nc

    def sb(name, shape, dt=F32):
        return m.sb("at_" + name, shape, dt, ctx)

    def sem(name):
        return m.sem("at_" + name)

    vb = [sb(f"vb{t}", [P, 2, 32]) for t in range(TPB)]
    zero = sb("zero", [P, HALF], BF16)
    mx = sb("mx", [P, 16, NB])
    top = sb("top", [P, 16])
    hl = sb("hl", [P, 2, 2, TT], BF16)
    mt = sb("mt", [32, P], BF16)
    sums = sb("sums", [P, HALF])
    (ready0, v_ready, scores, probs, v_used, a_scores, a_maxed, pv_done, pv_free, sums_stored, fin, hl_ready, mt_ps,
     mt_ready, mrow) = (sem(n) for n in (
         "init", "v_ready", "scores", "probs", "v_used", "a_scores", "a_maxed", "pv_done", "pv_free", "sums_stored", "fin",
         "hl_ready", "mt_ps", "mt_ready", "mrow"))
    S = [m.ps[:, i, :] for i in range(3)]
    A = [m.ps[:, 3 + 2 * u:5 + 2 * u, 0:BLK] for u in range(2)]
    PV = m.ps[:, 7, :]
    mt_bank = m.ps[0:32, 3, 0:P // 2].bitcast(BF16)
    FREE_S, FREE_V, FREE_A = 3, TPB, 2
    scale = float(np.float32(1.0) / np.sqrt(np.float32(HD)))
    block = ctx.enter_context(nc.Block())

    @block.tensor
    def _(pe):
        def score_step(g, c, ib, i):
            t, h, half = i // 4, i // 2 % 2, i % 2
            pe.wait_ge(probs, ib * 12 + i + 1)
            nc.tensor.matmul(S[i % 3], ks[:, bass.ds(g * KP + c * BLK + t * P, P)], qs[h][:, bass.ds(g * NT + half * HALF, HALF)],
                             start=True, stop=True).then_inc(scores, 1)

        def value_step(ib, t):
            pe.wait_ge(v_ready, ib * TPB + t + 1)
            pe.wait_ge(probs, ib * 12 + 4 * t + 4 + FREE_S)
            for k in range(4):
                ins = nc.tensor.matmul(PV[32 * k:32 * k + 32, :], vb[t][:, k // 2, :], prob[:, 4 * t + k, :],
                                       start=False, stop=False)
            ins.then_inc(v_used, 1)

        def max_step(ga, c, ia, u):
            pe.wait_ge(a_maxed, ia * 8 + u + 1)
            for n in range(2):
                h, t = (2 * u + n) // TT, (2 * u + n) % TT
                ins = nc.tensor.matmul(A[u % 2][:, n, :], qs[h][:, bass.ds(ga * NT + t * P, P)], ks[:, bass.ds(ga * KP + c * BLK, BLK)],
                                       start=True, stop=True)
            ins.then_inc(a_scores, 1)

        def open_pair(g):
            pe.wait_ge(mrow, g * 32 + 32)
            pe.wait_ge(pv_free, g + 1)
            for k in range(4):
                nc.tensor.matmul(PV[32 * k:32 * k + 32, :], zero[:, 0:32], zero[:], start=True, stop=False)

        def close_pair():
            for k in range(4):
                ins = nc.tensor.matmul(PV[32 * k:32 * k + 32, :], zero[:, 0:32], zero[:], start=False, stop=True)
            ins.then_inc(pv_done, 1)

        def flip_maximum(ga):
            pe.wait_ge(hl_ready, ga + 1)
            nc.tensor.transpose(mt_bank, hl[:].rearrange("p a b c -> p (a b c)"), m.identb[:]).then_inc(mt_ps, 1)

        def attend(g, c, first=False, with_maximum=True):
            ib = g * NB + c
            for step in ATTENTION_STEP.split():
                kind, i = step[0], int(step[1:])
                if kind == "s":
                    score_step(g, c, ib, i)
                elif kind == "v" and i == TPB - 1:
                    if not first:
                        value_step(ib - 1, i)
                elif kind == "v":
                    value_step(ib, i)
                elif with_maximum:
                    max_step(g + 1, c + 1, ib + NB + 1, i)

        pe.wait_ge(ready0, 4)
        with pe.Fori(0, NB) as c:
            for u in range(8):
                max_step(0, c, c, u)
        flip_maximum(0)
        pe.sem_inc(v_used, FREE_V)
        with pe.Fori(0, NPAIR - 1) as g:
            pe.wait_ge(mt_ready, g + 1)
            for u in range(8):
                max_step(g + 1, 0, g * NB + NB, u)
            open_pair(g)
            attend(g, 0, first=True)
            with pe.Fori(0, NB - 2) as c:
                attend(g, c + 1)
            attend(g, NB - 1, with_maximum=False)
            value_step(g * NB + NB - 1, TPB - 1)
            close_pair()
            flip_maximum(g + 1)
        last = NPAIR - 1
        open_pair(last)
        attend(last, 0, first=True, with_maximum=False)
        with pe.Fori(0, NB - 1) as c:
            attend(last, c + 1, with_maximum=False)
        value_step(last * NB + NB - 1, TPB - 1)
        close_pair()

    @block.scalar
    def _(act):
        act.sem_inc(probs, FREE_S)
        with act.Fori(0, NPAIR) as g:
            with act.Fori(0, NB) as c:
                ib = g * NB + c
                for i in range(12):
                    if i % 4 == 0:
                        act.wait_ge(v_used, ib * TPB + i // 4 + 1)
                    act.wait_ge(scores, ib * 12 + i + 1)
                    nc.scalar.activation(prob[:, i, :], S[i % 3], ACT.Exp, scale=scale).then_inc(probs, 1)

    @block.vector
    def _(dve):
        def reduce_steps(ia, c):
            for u in range(8):
                dve.wait_ge(a_scores, ia * 8 + u + 1)
                nc.vector.tensor_reduce(mx[:, 2 * u:2 * u + 2, bass.ds(c, 1)], A[u % 2], AX.X, ALU.max).then_inc(a_maxed, 1)

        def finish_maximum(ga, rows_delivered):
            dve.wait_ge(a_maxed, ga * (8 * NB) + 8 * NB + FREE_A)
            nc.vector.tensor_reduce(top[:], mx[:], AX.X, ALU.max).then_inc(fin, 1)
            t2 = top[:].rearrange("p (h q) -> p h q", h=2)
            dve.wait_ge(fin, ga * 2 + 1)
            nc.vector.tensor_scalar(hl[:, :, 0, :], t2, -1.0, None, ALU.mult).then_inc(fin, 1)
            dve.wait_ge(fin, ga * 2 + 2)
            nc.vector.scalar_tensor_tensor(hl[:, :, 1, :], t2, -1.0, hl[:, :, 0, :], ALU.mult, ALU.subtract).then_inc(hl_ready, 1)
            dve.wait_ge(mt_ps, ga + 1)
            if rows_delivered is not None:
                dve.wait_ge(mrow, rows_delivered)
            nc.vector.tensor_copy(mt[:], mt_bank).then_inc(mt_ready, 1)

        def copy_sums(g):
            dve.wait_ge(pv_done, g + 1)
            dve.wait_ge(sums_stored, g * 16 + 16)
            nc.vector.tensor_copy(sums[:], PV).then_inc(pv_free, 1)

        for z in vb:
            nc.vector.memset(z[:], 0.0).then_inc(ready0, 1)
        nc.vector.memset(zero[:], 0.0).then_inc(ready0, 1)
        dve.sem_inc(a_maxed, FREE_A)
        dve.sem_inc(pv_free, 1)
        with dve.Fori(0, NB) as c:
            reduce_steps(c, c)
        finish_maximum(0, None)
        with dve.Fori(0, NPAIR - 1) as g:
            with dve.Fori(0, NB) as c:
                reduce_steps(g * NB + c + NB, c)
            finish_maximum(g + 1, g * 32 + 32)
            copy_sums(g)
        copy_sums(NPAIR - 1)

    @block.gpsimd
    def _(pool):
        pool.wait_ge(ready0, 4)
        with pool.Fori(0, NPAIR) as g:
            with pool.Fori(0, NB) as c:
                for t in range(TPB):
                    pool.wait_ge(v_used, g * (NB * TPB) + c * TPB + t + 1)
                    nc.gpsimd.tensor_copy(vb[t][:, :, 0:HD + 1],
                                          vs[:].rearrange("p t h d -> p (t h) d")[:, bass.ds(c * (TPB * NH) + g * 2 + t * NH, 2), :]).then_inc(v_ready, 1)

    @block.sync
    def _(sp):
        def deliver_maxima(ga):
            sp.wait_ge(mt_ready, ga + 1)
            for h in range(2):
                r = 64 * h + SPLIT_ROWS
                sp.dma_start(qs[h][r:r + 2, bass.ds(ga * NT, NT)], mt[16 * h:16 * h + 16, :]).then_inc(mrow, 16)

        def store_sums(g):
            sp.wait_ge(pv_free, g + 2)
            sp.dma_start(od[:, bass.ds(g * HALF, HALF)], sums[:]).then_inc(sums_stored, 16)

        sp.sem_inc(sums_stored, 16)
        deliver_maxima(0)
        with sp.Fori(0, NPAIR - 1) as g:
            deliver_maxima(g + 1)
            store_sums(g)
        store_sums(NPAIR - 1)
        sp.wait_ge(mrow, 32 * NPAIR)
        sp.wait_ge(sums_stored, 16 * (NPAIR + 1))


def first_mask(m, dve, src, top, rev, tmp, tmp_top, mask):
    nc = m.nc

    def wide(t):
        return t[:].unsqueeze(2).to_broadcast([P, TT, NE])

    m.dve(dve, nc.vector.tensor_tensor(tmp[:], src[:], wide(top), ALU.is_equal))
    m.dve(dve, nc.vector.tensor_tensor(tmp[:], tmp[:], rev[:].unsqueeze(1).to_broadcast([P, TT, NE]), ALU.mult))
    m.dve(dve, nc.vector.tensor_reduce(tmp_top[:], tmp[:], AX.X, ALU.max))
    m.dve(dve, nc.vector.tensor_tensor(mask[:], tmp[:], wide(tmp_top), ALU.is_equal))


def route(m, name, gate_key, top_k, wide_w):
    nc, a = m.nc, m.a
    with ExitStack() as ctx:
        def sb(n, shape):
            return m.sb(f"{name}_{n}", shape, F32, ctx)

        gate, rev, sel = sb("gate", [P, NE]), sb("rev", [P, NE]), sb("sel", [NE, NE, P])
        lg, ex, tmp, mask, mask2, w = (sb(n, [P, TT, NE]) for n in ("lg", "ex", "tmp", "mask", "mask2", "w"))
        top, top2, t1, t2, t3 = (sb(n, [P, TT]) for n in ("top", "top2", "t1", "t2", "t3"))
        wT = sb("wT", [NE, NT])
        loaded, logits, ex_in, ex_out, w_ready, w_ps, w_rows, wide_ps, wide_sb = (
            m.sem(f"{name}_{s}") for s in ("loaded", "logits", "exin", "exout", "w", "wps", "wrows", "wideps", "widesb"))
        lp = m.ps[:, 0, 0:TT * NE].rearrange("p (t e) -> p t e", e=NE)

        def wide(t):
            return t[:].unsqueeze(2).to_broadcast([P, TT, NE])

        block = ctx.enter_context(nc.Block())

        @block.sync
        def _(sp):
            sp.dma_start(gate[:], a[gate_key]).then_inc(loaded, 16)
            sp.dma_start(rev[:], a["c_rev"]).then_inc(loaded, 16)

        @block.tensor
        def _(pe):
            pe.wait_ge(loaded, 32)
            for t in range(TT):
                ins = nc.tensor.matmul(lp[:, t, :], m.xT[:, t * P:(t + 1) * P], gate[:], start=True, stop=True)
            ins.then_inc(logits, 1)
            pe.wait_ge(w_ready, 1)
            for t in range(TT):
                ins = nc.tensor.transpose(m.ps[0:NE, 1 + t // 4, t % 4 * P:(t % 4 + 1) * P], w[:, t, :], m.ident[:])
            ins.then_inc(w_ps, 1)
            pe.wait_ge(w_rows, 2)
            for i in range(2 * NE):
                e, h = i // 2, i % 2
                if i >= 4:
                    pe.wait_ge(wide_sb, i - 3)
                nc.tensor.matmul(m.ps[:, 4 + i % 4, :], sel[:, e, :], wT[:, h * HALF:(h + 1) * HALF],
                                 start=True, stop=True).then_inc(wide_ps, 1)

        @block.vector
        def _(dve):
            def own(ins):
                m.dve(dve, ins)

            nc.vector.tensor_copy(sel[:], m.ident[0:NE, 0:NE].unsqueeze(2).to_broadcast([NE, NE, P])).then_inc(w_rows, 1)
            dve.wait_ge(loaded, 32)
            dve.wait_ge(logits, 1)
            own(nc.vector.tensor_copy(lg[:], lp))
            own(nc.vector.tensor_reduce(top[:], lg[:], AX.X, ALU.max))
            if top_k == 1:
                first_mask(m, dve, lg, top, rev, tmp, t1, mask)
                nc.vector.tensor_tensor(ex[:], lg[:], wide(top), ALU.subtract).then_inc(ex_in, 1)
                dve.wait_ge(ex_out, 1)
                own(nc.vector.tensor_reduce(t2[:], ex[:], AX.X, ALU.add))
                own(nc.vector.reciprocal(t3[:], t2[:]))
                nc.vector.tensor_tensor(w[:], mask[:], wide(t3), ALU.mult).then_inc(w_ready, 1)
            else:
                first_mask(m, dve, lg, top, rev, tmp, t1, mask)
                own(nc.vector.scalar_tensor_tensor(lg[:], mask[:], -BIG, lg[:], ALU.mult, ALU.add))
                own(nc.vector.tensor_reduce(top2[:], lg[:], AX.X, ALU.max))
                first_mask(m, dve, lg, top2, rev, tmp, t1, mask2)
                nc.vector.tensor_tensor(t2[:], top2[:], top[:], ALU.subtract).then_inc(ex_in, 1)
                dve.wait_ge(ex_out, 1)
                own(nc.vector.tensor_scalar(t1[:], t3[:], 1.0, None, ALU.add))
                own(nc.vector.reciprocal(t1[:], t1[:]))
                own(nc.vector.tensor_tensor(t2[:], t3[:], t1[:], ALU.mult))
                own(nc.vector.tensor_tensor(mask[:], mask[:], wide(t1), ALU.mult))
                own(nc.vector.tensor_tensor(mask2[:], mask2[:], wide(t2), ALU.mult))
                nc.vector.tensor_tensor(w[:], mask[:], mask2[:], ALU.add).then_inc(w_ready, 1)
            dve.wait_ge(w_ps, 1)
            nc.vector.tensor_copy(wT[:], m.ps[0:NE, 1:3, :].rearrange("p a b -> p (a b)")).then_inc(w_rows, 1)

        @block.scalar
        def _(act):
            act.wait_ge(ex_in, 1)
            if top_k == 1:
                nc.scalar.activation(ex[:], ex[:], ACT.Exp).then_inc(ex_out, 1)
            else:
                nc.scalar.activation(t3[:], t2[:], ACT.Exp).then_inc(ex_out, 1)
            for i in range(2 * NE):
                act.wait_ge(wide_ps, i + 1)
                nc.scalar.activation(wide_w[:, i // 2, i % 2 * HALF:(i % 2 + 1) * HALF], m.ps[:, 4 + i % 4, :],
                                     ACT.Copy).then_inc(wide_sb, 1)


def to_token_tiles(m, name, acc):
    nc = m.nc
    with nc.Block() as block:
        @block.tensor
        def _(pe):
            for t in range(TT):
                nc.tensor.transpose(m.ps[:, 4 + t // 4, t % 4 * P:(t % 4 + 1) * P], acc[:, t * P:(t + 1) * P], m.ident[:])


class S4Tables:

    def __init__(self, m, ctx):
        self.m = m

        def sb(n, shape, dt=F32):
            return m.sb("sk_" + n, shape, dt, ctx)

        self.cc = sb("cc", [P, 8])
        self.b_steps, self.a_steps = sb("bsteps", [P, 32]), sb("asteps", [P, 32])
        self.logs, self.turns, self.red, self.ex = (sb(n, [P, 2, P]) for n in ("logs", "turns", "red", "ex"))
        self.power = sb("power", [P, 2, P], mybir.dt.int32)
        self.aim, self.cre, self.cim = (sb(n, [P, P]) for n in ("aim", "cre", "cim"))
        self.small = [sb(n, [P, P]) for n in ("dr", "wi", "er", "ei", "t1", "t2", "t3", "nr", "ni", "alpha", "beta")]
        self.th, self.rn, self.e2, self.g1, self.g2 = (sb(n, [P, P, 32]) for n in ("th", "rn", "e2", "g1", "g2"))
        self.decay = sb("decay", [P, P, 24])
        self.weight = sb("weight", [P, 2, P, 4])
        self.loaded, self.asked, self.answered = (m.sem("sk_" + n) for n in ("loaded", "asked", "answered"))
        er, ei, t3, nr = self.small[2], self.small[3], self.small[6], self.small[7]
        self.functions = [(self.red, ACT.Tanh), (er, ACT.Sin), (ei, ACT.Sin), (nr, ACT.Sin), (t3, ACT.Tanh), (self.e2, ACT.Sin),
                          (self.decay, ACT.Tanh), (self.g1, ACT.Sin), (self.g2, ACT.Sin)]

    def load(self, sp):
        a = self.m.a
        for dst, src in ((self.cc, "c_s4"), (self.b_steps, "c_bsteps"), (self.a_steps, "c_asteps"), (self.aim, "s4_aim"),
                         (self.cre, "s4_cre"), (self.cim, "s4_cim")):
            sp.dma_start(dst[:], a[src]).then_inc(self.loaded, 16)
        sp.dma_start(self.logs[:, 0, :], a["s4_ldt"]).then_inc(self.loaded, 16)
        sp.dma_start(self.logs[:, 1, :], a["s4_arl"]).then_inc(self.loaded, 16)

    def answer(self, act, first, last):
        for i in range(first, last):
            buf, f = self.functions[i]
            act.wait_ge(self.asked, i + 1)
            self.m.nc.scalar.activation(buf[:], buf[:], f, scale=0.5 if f == ACT.Tanh else 1.0).then_inc(self.answered, 1)

    def compute(s, dve):
        m, nc = s.m, s.m.nc
        cc, red, ex, power, aim, cre, cim = s.cc, s.red, s.ex, s.power, s.aim, s.cre, s.cim
        dr, wi, er, ei, t1, t2, t3, nr, ni, alpha, beta = s.small
        th, rn, e2, g1, g2, decay, weight = s.th, s.rn, s.e2, s.g1, s.g2, s.decay, s.weight

        def own(ins):
            m.dve(dve, ins)

        def ask(ins):
            ins.then_inc(s.asked, 1)

        def take(n):
            dve.wait_ge(s.answered, n)

        def reduced_angle(out, angle, turn, rad, tmp):
            own(nc.vector.tensor_scalar(tmp, angle, 1.0 / TWO_PI, turn, ALU.mult, ALU.add))
            own(nc.vector.tensor_scalar(tmp, tmp, MAGIC, MAGIC, ALU.add, ALU.subtract))
            own(nc.vector.scalar_tensor_tensor(out, tmp, -TWO_PI_HI, angle, ALU.mult, ALU.add))
            own(nc.vector.scalar_tensor_tensor(out, tmp, -TWO_PI_LO, out, ALU.mult, ALU.add))
            own(nc.vector.tensor_scalar(out, out, rad, PI_BELOW, ALU.add, ALU.min))
            ask(nc.vector.tensor_scalar(out, out, -PI_BELOW, None, ALU.max))

        tt, ts, stt = nc.vector.tensor_tensor, nc.vector.tensor_scalar, nc.vector.scalar_tensor_tensor
        dve.wait_ge(s.loaded, 16 * 8)
        own(ts(s.turns[:], s.logs[:], 1.0 / LN2, MAGIC, ALU.mult, ALU.add))
        own(ts(s.turns[:], s.turns[:], MAGIC, None, ALU.subtract))
        own(ts(s.turns[:], s.turns[:], -126.0, 127.0, ALU.max, ALU.min))
        own(stt(red[:], s.turns[:], -LN2_HI, s.logs[:], ALU.mult, ALU.add))
        ask(stt(red[:], s.turns[:], -LN2_LO, red[:], ALU.mult, ALU.add))
        own(ts(power[:], s.turns[:], 127.0, 8388608.0, ALU.add, ALU.mult))
        take(1)
        own(ts(ex[:], red[:], -1.0, 1.0, ALU.mult, ALU.add))
        own(nc.vector.reciprocal(ex[:], ex[:]))
        own(stt(ex[:], red[:], 1.0, ex[:], ALU.add, ALU.mult))
        own(tt(ex[:], ex[:], power[:].bitcast(F32), ALU.mult))
        dt, are = ex[:, 0, :], ex[:, 1, :]
        own(stt(dr[:], dt, -1.0, are, ALU.mult, ALU.mult))
        own(tt(wi[:], dt, aim[:], ALU.mult))
        reduced_angle(er[:], wi[:], 0.25, TWO_PI / 4, t1[:])
        reduced_angle(ei[:], wi[:], 0.0, 0.0, t1[:])
        own(ts(t2[:], wi[:], 0.5, None, ALU.mult))
        reduced_angle(nr[:], t2[:], 0.0, 0.0, t1[:])
        ask(ts(t3[:], dr[:], 1.0, None, ALU.mult))
        wide = [P, P, 32]

        def steps(out, rate, which):
            n = which.shape[-1]
            return tt(out, rate[:].unsqueeze(2).to_broadcast([P, P, n]), which.unsqueeze(1).to_broadcast([P, P, n]), ALU.mult)

        own(steps(th[:], wi, s.b_steps[:]))
        reduced_angle(e2[:], th[:], cc[:, 0:1], cc[:, 1:2], rn[:])
        for at, which in ((0, s.b_steps[:, 0:8]), (8, s.b_steps[:, 0:32:8]), (12, s.a_steps[:, 0:8])):
            own(steps(decay[:, :, at:at + which.shape[-1]], dr, which))
        ask(steps(decay[:, :, 20:24], dr, s.a_steps[:, 0:32:8]))
        own(steps(th[:], wi, s.a_steps[:]))
        take(6)
        own(ts(t1[:], t3[:], -1.0, 1.0, ALU.mult, ALU.add))
        own(nc.vector.reciprocal(t1[:], t1[:]))
        own(stt(t3[:], t3[:], 2.0, t1[:], ALU.mult, ALU.mult))
        own(tt(er[:], er[:], t3[:], ALU.mult))
        own(stt(nr[:], nr[:], 2.0, nr[:], ALU.mult, ALU.mult))
        own(tt(er[:], er[:], nr[:], ALU.subtract))
        own(stt(ei[:], t3[:], 1.0, ei[:], ALU.add, ALU.mult))
        own(tt(nr[:], cre[:], er[:], ALU.mult))
        own(tt(t1[:], cim[:], ei[:], ALU.mult))
        own(tt(nr[:], nr[:], t1[:], ALU.subtract))
        own(tt(ni[:], cre[:], ei[:], ALU.mult))
        own(tt(t1[:], cim[:], er[:], ALU.mult))
        own(tt(ni[:], ni[:], t1[:], ALU.add))
        own(tt(t1[:], are, are, ALU.mult))
        own(tt(t2[:], aim[:], aim[:], ALU.mult))
        own(tt(t1[:], t1[:], t2[:], ALU.add))
        own(nc.vector.reciprocal(t1[:], t1[:]))
        own(tt(t2[:], ni[:], aim[:], ALU.mult))
        own(tt(t3[:], nr[:], are, ALU.mult))
        own(tt(alpha[:], t2[:], t3[:], ALU.subtract))
        own(tt(alpha[:], alpha[:], t1[:], ALU.mult))
        own(ts(alpha[:], alpha[:], cc[:, 4:5], None, ALU.mult))
        own(tt(t2[:], ni[:], are, ALU.mult))
        own(tt(t3[:], nr[:], aim[:], ALU.mult))
        own(tt(beta[:], t2[:], t3[:], ALU.add))
        own(stt(beta[:], beta[:], 2.0, t1[:], ALU.mult, ALU.mult))
        reduced_angle(g1[:], th[:], cc[:, 0:1], cc[:, 1:2], rn[:])
        reduced_angle(g2[:], th[:], cc[:, 2:3], cc[:, 3:4], rn[:])
        take(7)
        own(ts(decay[:], decay[:], -1.0, 1.0, ALU.mult, ALU.add))
        own(nc.vector.reciprocal(decay[:], decay[:]))
        own(ts(decay[:], decay[:], 2.0, 1.0, ALU.mult, ALU.subtract))
        split = [P, P, 4, 8]

        def by_step(t):
            return t[:].rearrange("p h (i j) -> p h i j", j=8)

        own(tt(by_step(e2), by_step(e2), decay[:, :, 0:8].unsqueeze(2).to_broadcast(split), ALU.mult))
        own(tt(by_step(e2), by_step(e2), decay[:, :, 8:12].unsqueeze(3).to_broadcast(split), ALU.mult))
        for i, rate in enumerate((alpha, beta)):
            own(tt(weight[:, i], decay[:, :, 20:24], rate[:].unsqueeze(2).to_broadcast([P, P, 4]), ALU.mult))
        take(9)
        for i, g in enumerate((g1, g2)):
            own(tt(by_step(g), by_step(g), weight[:, i].unsqueeze(3).to_broadcast(split), ALU.mult))
        own(tt(g1[:], g1[:], g2[:], ALU.add))
        tt(by_step(g1), by_step(g1), decay[:, :, 12:20].unsqueeze(2).to_broadcast(split), ALU.mult)

    def finish(s, kern, prefetch):
        m, nc = s.m, s.m.nc
        k_ps = m.sem("sk_kps")
        with nc.Block() as block:
            @block.sync
            def _(sp):
                prefetch(sp)

            @block.tensor
            def _(pe):
                kp = m.ps[:, 0:2, :].rearrange("p a b -> p (a b)").rearrange("p (h c) -> p h c", c=TT)
                g1v = s.g1[:].rearrange("p h (c k) -> p h k c", k=4)
                for h in range(P):
                    for k in range(4):
                        ins = nc.tensor.matmul(kp[32 * k:32 * k + 32, h, :], s.e2[:, h, :], g1v[:, h, k, :], start=True, stop=True)
                ins.then_inc(k_ps, 1)

            @block.vector
            def _(dve):
                dve.wait_ge(k_ps, 1)
                nc.vector.tensor_copy(kern[:], m.ps[:, 0:2, :].rearrange("p a b -> p (a b)").rearrange("p (h c) -> p c h", c=TT))


def experts_gelu(m):
    nc, a = m.nc, m.a
    FC = FF0 // P
    m.s4_ctx = m.ctx.enter_context(ExitStack())
    tables = m.s4_tables = S4Tables(m, m.s4_ctx)
    with ExitStack() as ctx:
        def sb(n, shape):
            return m.sb("m0_" + n, shape, F32, ctx)

        ww = sb("ww", [P, NE, NT])
        acc = sb("acc", [P, NT])
        route(m, "m0r", "m0_gate", 1, ww)
        w1 = [sb(f"w1_{i}", [P, FF0]) for i in range(2)]
        w2 = [sb(f"w2_{i}", [P, FC, P]) for i in range(2)]
        b1 = [sb(f"b1_{i}", [P, FC]) for i in range(2)]
        b2 = sb("b2", [P, NE])
        hid = sb("hid", [P, 2, FC, NT])
        part = sb("part", [P, 2, 2, HALF])
        loaded, cleared, up_ps, gelu, y_ps, y_read, weighted, added = (
            m.sem("m0_" + s) for s in ("loaded", "cleared", "up", "gelu", "y", "yread", "weighted", "added"))
        w_in = [m.sem(f"m0_w{i}") for i in range(2)]
        c3 = ctx.enter_context(ExitStack())
        block = c3.enter_context(nc.Block())

        @block.sync
        def _(sp):
            sp.dma_start(b2[:], a["m0_b2"]).then_inc(loaded, 16)
            tables.load(sp)
            with sp.Fori(0, NE // 2) as e2:
                for i in range(2):
                    e = e2 * 2 + i
                    sp.wait_ge(y_ps, e * 2 + 2)
                    sp.dma_start(b1[i][:], a["m0_b1"][bass.ds(e, 1)].rearrange("e p f -> p (e f)")).then_inc(w_in[i], 16)
                    sp.dma_start(w1[i][:], a["m0_w1"][bass.ds(e, 1)].rearrange("e p f -> p (e f)")).then_inc(w_in[i], 16)
                    sp.dma_start(w2[i][:], a["m0_w2"][bass.ds(e, 1)].rearrange("e (c p) d -> p (e c) d", p=P)).then_inc(w_in[i], 16)

        @block.tensor
        def _(pe):
            pe.sem_inc(y_ps, 4)
            with pe.Fori(0, NE // 2) as e2:
                for par in range(2):
                    e = e2 * 2 + par
                    pe.wait_ge(w_in[par], e2 * 48 + 48)
                    for i in range(2 * FC):
                        c, h = i // 2, i % 2
                        pe.wait_ge(gelu, e * 8 + i + 1)
                        nc.tensor.matmul(m.ps[:, i % 4, :], w1[par][:, c * P:(c + 1) * P], m.xT[:, h * HALF:(h + 1) * HALF],
                                         start=True, stop=True).then_inc(up_ps, 1)
                    for i in range(2 * FC):
                        c, h = i // 2, i % 2
                        pe.wait_ge(gelu, e * 8 + i + 1 + 4)
                        if c == 0:
                            pe.wait_ge(y_read, e * 2 + h + 1)
                        ins = nc.tensor.matmul(m.ps[:, 4 + 2 * par + h, :], w2[par][:, c, :],
                                               hid[:, par, c, h * HALF:(h + 1) * HALF], start=c == 0, stop=c == FC - 1)
                        if c == FC - 1:
                            ins.then_inc(y_ps, 1)

        @block.scalar
        def _(act):
            table_steps = ((0, 1), (1, 5), (5, 6), (6, 7), (7, 8), (8, 9), (9, 9), (9, 9))
            act.sem_inc(gelu, 4)
            act.wait_ge(loaded, 16)
            for e in range(NE):
                par = e % 2
                act.wait_ge(y_ps, e * 2 + 2)
                act.wait_ge(w_in[par], e // 2 * 48 + 48)
                for i in range(2 * FC):
                    c, h = i // 2, i % 2
                    act.wait_ge(up_ps, e * 8 + i + 1)
                    nc.scalar.activation(hid[:, par, c, h * HALF:(h + 1) * HALF], m.ps[:, i % 4, :], ACT.Gelu,
                                         bias=b1[par][:, c:c + 1]).then_inc(gelu, 1)
                tables.answer(act, *table_steps[e])
                for h in range(2):
                    act.wait_ge(y_ps, e * 2 + h + 1 + 4)
                    act.wait_ge(added, e * 2 + h + 1)
                    nc.scalar.activation(part[:, par, h, :], m.ps[:, 4 + 2 * par + h, :], ACT.Identity,
                                         bias=b2[:, e:e + 1]).then_inc(y_read, 1)

        @block.vector
        def _(dve):
            nc.vector.memset(acc[:], 0.0).then_inc(cleared, 1)
            tables.compute(dve)

        @block.gpsimd
        def _(pool):
            pool.sem_inc(added, 4)
            pool.sem_inc(y_read, 4)
            pool.wait_ge(cleared, 1)
            with pool.Fori(0, NE // 2) as e2:
                for par in range(2):
                    e = e2 * 2 + par
                    for h in range(2):
                        y = part[:, par, h, :]
                        pool.wait_ge(y_read, e * 2 + h + 1 + 4)
                        nc.gpsimd.tensor_tensor(y, y, ww[:, bass.ds(e, 1), h * HALF:(h + 1) * HALF].rearrange("p a b -> p (a b)"),
                                                ALU.mult).then_inc(weighted, 1)
                        pool.wait_ge(weighted, e * 2 + h + 1)
                        pool.wait_ge(added, e * 2 + h + 1 + 2)
                        o = acc[:, h * HALF:(h + 1) * HALF]
                        nc.gpsimd.tensor_tensor(o, o, y, ALU.add).then_inc(added, 1)

        c3.close()
        to_token_tiles(m, "m0", acc)
    layernorm(m, "ln2", m.ps[:, 4:6, :].rearrange("p a (b c) -> p (a b) c", c=P))


def experts_silu(m):
    nc, a = m.nc, m.a
    FC = FF1 // P
    with ExitStack() as ctx:
        def sb(n, shape):
            return m.sb("m1_" + n, shape, F32, ctx)

        ww = sb("ww", [P, NE, NT])
        acc = sb("acc", [P, NT])
        route(m, "m1r", "m1_gate", 2, ww)
        wg = [sb(f"wg_{i}", [P, FF1]) for i in range(2)]
        wu = [sb(f"wu_{i}", [P, FF1]) for i in range(2)]
        wd = [sb(f"wd_{i}", [P, FC, P]) for i in range(2)]
        sil = sb("sil", [P, 4, HALF])
        hid = sb("hid", [P, 2, FC, NT])
        part = sb("part", [P, 2, 2, HALF])
        cleared, g_ps, u_ps, silu, h_ready, y_ps, y_read, added = (
            m.sem("m1_" + s) for s in ("cleared", "g", "u", "silu", "h", "y", "yread", "added"))
        w_in = [m.sem(f"m1_w{i}") for i in range(2)]
        c3 = ctx.enter_context(ExitStack())
        block = c3.enter_context(nc.Block())

        @block.sync
        def _(sp):
            with sp.Fori(0, NE // 2) as e2:
                for i in range(2):
                    e = e2 * 2 + i
                    sp.wait_ge(y_ps, e * 2 + 2)
                    sp.dma_start(wg[i][:], a["m1_wg"][bass.ds(e, 1)].rearrange("e p f -> p (e f)")).then_inc(w_in[i], 16)
                    sp.dma_start(wu[i][:], a["m1_wu"][bass.ds(e, 1)].rearrange("e p f -> p (e f)")).then_inc(w_in[i], 16)
                    sp.dma_start(wd[i][:], a["m1_wd"][bass.ds(e, 1)].rearrange("e (c p) d -> p (e c) d", p=P)).then_inc(w_in[i], 16)

        @block.tensor
        def _(pe):
            pe.sem_inc(y_ps, 4)
            with pe.Fori(0, NE // 2) as e2:
                for par in range(2):
                    e = e2 * 2 + par
                    pe.wait_ge(w_in[par], e2 * 48 + 48)
                    for i in range(2 * FC):
                        c, h = i // 2, i % 2
                        x = m.xT[:, h * HALF:(h + 1) * HALF]
                        pe.wait_ge(h_ready, e * 4 + i + 3)
                        nc.tensor.matmul(m.ps[:, i % 2, :], wg[par][:, c * P:(c + 1) * P], x, start=True, stop=True).then_inc(g_ps, 1)
                        nc.tensor.matmul(m.ps[:, 2 + i % 2, :], wu[par][:, c * P:(c + 1) * P], x, start=True, stop=True).then_inc(u_ps, 1)
                    for i in range(2 * FC):
                        c, h = i // 2, i % 2
                        pe.wait_ge(h_ready, e * 4 + i + 1 + 4)
                        if c == 0:
                            pe.wait_ge(y_read, e * 2 + h + 1)
                        ins = nc.tensor.matmul(m.ps[:, 4 + 2 * par + h, :], wd[par][:, c, :],
                                               hid[:, par, c, h * HALF:(h + 1) * HALF], start=c == 0, stop=c == FC - 1)
                        if c == FC - 1:
                            ins.then_inc(y_ps, 1)

        @block.scalar
        def _(act):
            with act.Fori(0, NE) as e:
                for i in range(4):
                    act.wait_ge(g_ps, e * 4 + i + 1)
                    act.wait_ge(h_ready, e * 4 + i + 1)
                    nc.scalar.activation(sil[:, i, :], m.ps[:, i % 2, :], ACT.Silu).then_inc(silu, 1)

        @block.vector
        def _(dve):
            nc.vector.memset(acc[:], 0.0).then_inc(cleared, 1)
            dve.sem_inc(y_read, 4)
            dve.sem_inc(h_ready, 4)
            with dve.Fori(0, NE // 2) as e2:
                for par in range(2):
                    e = e2 * 2 + par
                    dve.wait_ge(y_ps, e * 2 + 2)
                    for i in range(4):
                        c, h = i // 2, i % 2
                        dve.wait_ge(silu, e * 4 + i + 1)
                        dve.wait_ge(u_ps, e * 4 + i + 1)
                        nc.vector.tensor_tensor(hid[:, par, c, h * HALF:(h + 1) * HALF], m.ps[:, 2 + i % 2, :], sil[:, i, :],
                                                ALU.mult).then_inc(h_ready, 1)
                    for h in range(2):
                        dve.wait_ge(y_ps, e * 2 + h + 1 + 4)
                        dve.wait_ge(added, e * 2 + h + 1)
                        nc.vector.tensor_tensor(
                            part[:, par, h, :], m.ps[:, 4 + 2 * par + h, :],
                            ww[:, bass.ds(e, 1), h * HALF:(h + 1) * HALF].rearrange("p a b -> p (a b)"), ALU.mult).then_inc(y_read, 1)

        @block.gpsimd
        def _(pool):
            pool.sem_inc(added, 4)
            pool.wait_ge(cleared, 1)
            with pool.Fori(0, NE // 2) as e2:
                for par in range(2):
                    e = e2 * 2 + par
                    for h in range(2):
                        pool.wait_ge(y_read, e * 2 + h + 1 + 4)
                        pool.wait_ge(added, e * 2 + h + 1 + 2)
                        o = acc[:, h * HALF:(h + 1) * HALF]
                        nc.gpsimd.tensor_tensor(o, o, part[:, par, h, :], ALU.add).then_inc(added, 1)

        c3.close()
        to_token_tiles(m, "m1", acc)
    layernorm(m, "ln5", m.ps[:, 4:6, :].rearrange("p a (b c) -> p (a b) c", c=P), out=m.out)


def s4_layer(m):
    nc, a = m.nc, m.a
    with ExitStack() as ctx:
        def sb(n, shape, c=ctx):
            return m.sb("s4_" + n, shape, F32, c)

        kern = sb("kern", [P, TT, P])
        dft = sb("dft", [P, TT, 2 * NF])
        altc, altr = sb("altc", [P, 1]), sb("altr", [1, NT])
        dcol, wout, bout = sb("dcol", [P, 1]), sb("wout", [P, 2 * P]), sb("bout", [1, 2 * P])
        loaded = m.sem("s4_loaded")

        def prefetch(sp):
            for t in range(TT):
                sp.dma_start(dft[:, t, :], a["c_dft"][t * P:(t + 1) * P, :]).then_inc(loaded, 16)
            for dst, src in ((altc, "c_altc"), (altr, "c_altr"), (dcol, "s4_d"), (wout, "s4_wout"), (bout, "s4_bout")):
                sp.dma_start(dst[:], a[src]).then_inc(loaded, 16)
            sp.wait_ge(loaded, 16 * 13)

        m.s4_tables.finish(kern, prefetch)
        spare = [t[:].rearrange("p h n -> p (h n)") for t in (m.s4_tables.th, m.s4_tables.rn, m.s4_tables.g2)]
        kh, yh = (spare[0][:, i * 2 * NF:(i + 1) * 2 * NF].rearrange("p (s f) -> p s f", s=2) for i in range(2))
        t1 = spare[1][:, 0:NF]
        yT = spare[1][:, NF:NF + 2 * TT * P].rearrange("p (f h) -> p f h", h=P)
        u, gT = spare[2][:, 0:NT], spare[2][:, NT:2 * NT]
        sig, yb = (spare[2][:, i * NT:(i + 1) * NT].rearrange("p (t h) -> p t h", h=P) for i in (2, 3))
        khn, yhn, yrow = sb("khn", [P, 1]), sb("yhn", [P, 1]), sb("yrow", [1, P])
        (k_ps, k_sb, x_ps, y_sb, t_ps, t_sb, inv_ps, u_sb, g_sb, z_ps, s_sb) = (
            m.sem("s4_" + s) for s in ("kps", "ksb", "xps", "ysb", "tps", "tsb", "invps", "usb", "gsb", "zps", "ssb"))
        spec = m.ps[:, 4:8, :].rearrange("p (a b) c -> p a (b c)", a=2)
        scale = 1.0 / NF
        zp = m.ps[:, 0:4, :].rearrange("p a (b c) -> p (a b) c", c=2 * P)
        with nc.Block() as block:
            @block.tensor
            def _(pe):
                def forward(src, nyq, done):
                    for j in range(4):
                        for c in range(TT):
                            ins = nc.tensor.matmul(m.ps[:, 4 + j, :], src[:, c, :], dft[:, c, j * 512:(j + 1) * 512],
                                                   start=c == 0, stop=c == TT - 1)
                        ins.then_inc(done, 1)
                    for c in range(TT):
                        ins = nc.tensor.matmul(nyq, src[:, c, :], altc[:], start=c == 0, stop=c == TT - 1)
                    ins.then_inc(done, 1)

                forward(kern, m.ps[:, 0, 0:1], k_ps)
                pe.wait_ge(k_sb, 3)
                forward(m.xtok, m.ps[:, 1, 0:1], x_ps)
                pe.wait_ge(y_sb, 1)
                nc.tensor.matmul(m.ps[0:1, 2, 0:P], yhn[:], m.ident[:], start=True, stop=True).then_inc(t_ps, 1)
                for j in range(4):
                    pe.wait_ge(y_sb, 2 + j // 2)
                    if j == 2:
                        pe.wait_ge(t_sb, 1)
                    for c in range(4):
                        f = 4 * j + c
                        ins = nc.tensor.transpose(m.ps[:, (0, 1, 2, 3)[j], c * P:(c + 1) * P],
                                                  yh[:, f // TT, f % TT * P:(f % TT + 1) * P], m.ident[:])
                    ins.then_inc(t_ps, 1)
                pe.wait_ge(t_sb, 5)
                for h in range(2):
                    for f in range(2 * TT):
                        nc.tensor.matmul(m.ps[:, 4 + h, :], yT[:, f, :],
                                         dft[:, f % TT, f // TT * NF + h * HALF:f // TT * NF + (h + 1) * HALF],
                                         start=f == 0, stop=False)
                    nc.tensor.matmul(m.ps[:, 4 + h, :], yrow[:], altr[:, h * HALF:(h + 1) * HALF], start=False,
                                     stop=True).then_inc(inv_ps, 1)
                for t in range(TT):
                    pe.wait_ge(g_sb, 1 + t // 4)
                    nc.tensor.matmul(zp[:, t, :], gT[:, t * P:(t + 1) * P], wout[:], start=True, stop=False)
                    nc.tensor.matmul(zp[:, t, :], m.ones_row[0:1, 0:P], bout[:], start=False, stop=True).then_inc(z_ps, 1)

            @block.vector
            def _(dve):
                def own(ins):
                    m.dve(dve, ins)

                tt, ts = nc.vector.tensor_tensor, nc.vector.tensor_scalar
                dve.wait_ge(k_ps, 5)
                for s in range(2):
                    own(ts(kh[:, s, :], spec[:, s, :], scale, None, ALU.mult))
                    ts(kh[:, s, 0:1], kh[:, s, 0:1], 0.5, None, ALU.mult).then_inc(k_sb, 1)
                ts(khn[:], m.ps[:, 0, 0:1], 0.5 * scale, None, ALU.mult).then_inc(k_sb, 1)
                dve.wait_ge(k_sb, 3)
                dve.wait_ge(x_ps, 5)
                tt(yhn[:], khn[:], m.ps[:, 1, 0:1], ALU.mult).then_inc(y_sb, 1)
                own(tt(yh[:, 0, :], kh[:, 0, :], spec[:, 0, :], ALU.mult))
                own(tt(t1[:], kh[:, 1, :], spec[:, 1, :], ALU.mult))
                tt(yh[:, 0, :], yh[:, 0, :], t1[:], ALU.subtract).then_inc(y_sb, 1)
                dve.wait_ge(y_sb, 2)
                own(tt(yh[:, 1, :], kh[:, 1, :], spec[:, 0, :], ALU.mult))
                own(tt(t1[:], kh[:, 0, :], spec[:, 1, :], ALU.mult))
                tt(yh[:, 1, :], yh[:, 1, :], t1[:], ALU.add).then_inc(y_sb, 1)
                dve.wait_ge(t_ps, 1)
                nc.vector.tensor_copy(yrow[:], m.ps[0:1, 2, 0:P]).then_inc(t_sb, 1)
                for j in range(4):
                    dve.wait_ge(t_ps, 2 + j)
                    nc.vector.tensor_copy(yT[:, 4 * j:4 * j + 4, :].rearrange("p a b -> p (a b)"), m.ps[:, j, :]).then_inc(t_sb, 1)
                for h in range(2):
                    dve.wait_ge(inv_ps, h + 1)
                    nc.vector.scalar_tensor_tensor(u[:, h * HALF:(h + 1) * HALF], m.xT[:, h * HALF:(h + 1) * HALF], dcol[:, 0:1],
                                                   m.ps[:, 4 + h, :], ALU.mult, ALU.add).then_inc(u_sb, 1)
                for g in range(4):
                    dve.wait_ge(s_sb, g + 1)
                    tt(yb[:, 2 * g:2 * g + 2, :], zp[:, 2 * g:2 * g + 2, 0:P], sig[:, 2 * g:2 * g + 2, :], ALU.mult)

            @block.scalar
            def _(act):
                for h in range(2):
                    act.wait_ge(u_sb, h + 1)
                    nc.scalar.activation(gT[:, h * HALF:(h + 1) * HALF], u[:, h * HALF:(h + 1) * HALF],
                                         ACT.Gelu_apprx_tanh).then_inc(g_sb, 1)
                for g in range(4):
                    act.wait_ge(z_ps, 2 * g + 2)
                    nc.scalar.activation(sig[:, 2 * g:2 * g + 2, :], zp[:, 2 * g:2 * g + 2, P:2 * P], ACT.Sigmoid).then_inc(s_sb, 1)
        layernorm(m, "ln3", yb)
    m.s4_ctx.close()


W_D2V, W_IMG, W_TXT, W_ATT0, W_ATT1, W_F1, W_F2 = range(7)


def all_partitions(m, name, col, out, op):
    with m.nc.Block() as block:
        @block.gpsimd
        def _(pool):
            m.nc.gpsimd.partition_all_reduce(out, col, P, op)


def input_scale(m, top, weight_scale, inv, product, step):
    nc = m.nc
    with nc.Block() as block:
        @block.vector
        def _(dve):
            m.dve(dve, nc.vector.tensor_scalar(step, top, 1e-8, 1.0 / 127.0, ALU.max, ALU.mult))
            m.dve(dve, nc.vector.reciprocal(inv, step))
            for w, p in zip(weight_scale, product):
                nc.vector.tensor_tensor(p, step, w, ALU.mult)


def bit_layer(m, name, src, k, n, inv, quant, weight, out, scale, bias, max_out, sum_out=None, real=None):
    nc = m.nc
    real = real or n
    chunks = [(c, min(HALF, n - c)) for c in range(0, n, HALF)]
    with ExitStack() as ctx:
        tmp = m.sb(name + "_tmp", [P, 2, HALF], F32, ctx)
        tops = m.sb(name + "_tops", [P, len(chunks)], F32, ctx)
        q, mm, ev = (m.sem(f"{name}_{s}") for s in ("quant", "mm", "out"))
        block = ctx.enter_context(nc.Block())

        @block.vector
        def _(dve):
            for i, (c, w) in enumerate(chunks):
                m.dve(dve, nc.vector.tensor_scalar(tmp[0:k, i % 2, 0:w], src[0:k, c:c + w], inv[0:k, :], MAGIC, ALU.mult, ALU.add))
                nc.vector.tensor_scalar(quant[0:k, c:c + w], tmp[0:k, i % 2, 0:w], MAGIC, 127.0, ALU.subtract, ALU.min).then_inc(q, 1)
            for i, (c, w) in enumerate(chunks):
                dve.wait_ge(ev, i + 1)
                w = min(w, real - c)
                last = nc.vector.tensor_reduce(tops[:, i:i + 1], out[:, c:c + w], AX.X, ALU.max, apply_absolute_value=True)
            m.dve(dve, last)
            nc.vector.tensor_reduce(max_out, tops[:], AX.X, ALU.max)
            if sum_out is not None:
                nc.vector.tensor_reduce(sum_out, out[:, 0:real], AX.X, ALU.add)

        @block.tensor
        def _(pe):
            for i, (c, w) in enumerate(chunks):
                pe.wait_ge(q, i + 1)
                if i >= 4:
                    pe.wait_ge(ev, i - 3)
                nc.tensor.matmul(m.ps[:, i % 4, 0:w], weight, quant[0:k, c:c + w], start=True, stop=True).then_inc(mm, 1)

        @block.scalar
        def _(act):
            for i, (c, w) in enumerate(chunks):
                act.wait_ge(mm, i + 1)
                nc.scalar.activation(out[:, c:c + w], m.ps[:, i % 4, 0:w], ACT.Identity, scale=scale, bias=bias).then_inc(ev, 1)


def vision_attention(m):
    nc, a = m.nc, m.a
    with ExitStack() as ctx:
        def sb(n, shape, dt=F32, c=ctx):
            return m.sb("va_" + n, shape, dt, c)

        qimg = sb("qimg", [P, KP], BF16)
        fT = sb("fT", [P, NT])
        shapes = {W_D2V: (CD, P), W_IMG: (P, P), W_TXT: (P, P), W_ATT0: (P, 64), W_ATT1: (P, 64), W_F1: (P, 2 * FF0), W_F2: (P, 4 * P)}
        tern = {w: sb(f"tern{w}", list(shapes[w]), BF16) for w in shapes}
        tern_out = [sb(f"ternout{i}", [P, P]) for i in range(2)]
        bias = sb("bias", [P, 3])
        batt = [sb(f"batt{i}", [P, 64]) for i in range(2)]
        bf1, bf2 = sb("bf1", [P, 4]), sb("bf2", [P, P])
        wsc = sb("wsc", [P, 7])
        avg = sb("avg", [P, 1])
        step_img = sb("step_img", [P, 1])
        satt = sb("satt", [P, 2])
        with ExitStack() as c1:
            raw = {w: sb(f"raw{w}", list(shapes[w]), F32, c1) for w in shapes}
            raw_out = [sb(f"rawout{i}", [P, P], F32, c1) for i in range(2)]
            inv_n, sums, thr, nthr = (sb(n, [P, 7], F32, c1) for n in ("invn", "sums", "thr", "nthr"))
            tmp = sb("tmp", [P, 2 * FF0], F32, c1)
            tmpb = sb("tmpb", [P, P], F32, c1)
            tops, top = sb("tops", [P, 4], F32, c1), sb("top", [P, 4], F32, c1)
            vec, vis = sb("vec", [P, KP], F32, c1), sb("vis", [P, KP], F32, c1)
            qtmp = sb("qtmp", [P, KP], BF16, c1)
            loaded, ab = m.sem("va_loaded"), m.sem("va_abs")
            with nc.Block() as block:
                @block.sync
                def _(sp):
                    n = 0
                    for dst, src in [(raw[w], f"va_w{w}") for w in shapes] + [(raw_out[0], "va_wo0"), (raw_out[1], "va_wo1"),
                                     (inv_n, "c_inv"), (bias, "va_bias"), (batt[0], "va_batt0"), (batt[1], "va_batt1"),
                                     (bf1, "va_bf1"), (bf2, "va_bf2")]:
                        sp.dma_start(dst[:], a[src]).then_inc(loaded, 16)
                    sp.dma_start(vec[0:CD, 0:KV], a["ctx_T"]).then_inc(loaded, 16)
                    sp.dma_start(vec[0:CD, KV:KP], a["ctx_T"][:, 0:KP - KV]).then_inc(loaded, 16)

                @block.vector
                def _(dve):
                    m.dve(dve, nc.vector.memset(sums[:], 0.0))
                    m.dve(dve, nc.vector.memset(tops[:], 0.0))
                    dve.wait_ge(loaded, 16 * 17)
                    for w, (k, _) in shapes.items():
                        nc.vector.tensor_reduce(sums[0:k, w:w + 1], raw[w][:], AX.X, ALU.add, apply_absolute_value=True)
                    nc.vector.tensor_reduce(tops[0:CD, 0:1], vec[0:CD, 0:KV], AX.X, ALU.max, apply_absolute_value=True)
                    nc.vector.tensor_reduce(tops[:, 1:2], m.xT[:], AX.X, ALU.max, apply_absolute_value=True)
            all_partitions(m, "w", sums[:], wsc[:], RADD)
            all_partitions(m, "x", tops[:], top[:], RMAX)
            with nc.Block() as block:
                @block.vector
                def _(dve):
                    def own(ins):
                        m.dve(dve, ins)

                    own(nc.vector.tensor_tensor(wsc[:], wsc[:], inv_n[:], ALU.mult))
                    own(nc.vector.tensor_scalar(wsc[:], wsc[:], 1e-5, None, ALU.max))
                    own(nc.vector.tensor_scalar(thr[:], wsc[:], 0.5, None, ALU.mult))
                    own(nc.vector.tensor_scalar(nthr[:], wsc[:], -0.5, None, ALU.mult))

                    def ternary(dst, src, k, w, t):
                        own(nc.vector.tensor_scalar(t, src[:], nthr[0:k, w:w + 1], None, ALU.is_lt))
                        own(nc.vector.scalar_tensor_tensor(dst[:], src[:], thr[0:k, w:w + 1], t, ALU.is_gt, ALU.subtract))

                    for w, (k, n) in shapes.items():
                        ternary(tern[w], raw[w], k, w, tmp[0:k, 0:n])
                    for i in range(2):
                        ternary(tern_out[i], raw_out[i], P, W_ATT0 + i, tmpb[:])
            sc = {n: sb("s_" + n, [P, 1], F32, c1) for n in ("inv_x", "p_x", "inv_c", "p_c", "inv_v", "p_v", "step", "max_v", "max_i", "top_v", "top_i",
                                         "inv_i", "max_f")}
            input_scale(m, top[:, 0:1], [wsc[:, W_D2V:W_D2V + 1]], sc["inv_c"][:], [sc["p_c"][:]], sc["step"][:])
            bit_layer(m, "va_d2v", vec, CD, KP, sc["inv_c"], qtmp, tern[W_D2V][:], vis, sc["p_c"][:, 0:1], bias[:, 0:1],
                      sc["max_v"][:], real=KV)
            all_partitions(m, "v", sc["max_v"][:], sc["top_v"][:], RMAX)
            input_scale(m, sc["top_v"][:], [wsc[:, W_IMG:W_IMG + 1]], sc["inv_v"][:], [sc["p_v"][:]], sc["step"][:])
            bit_layer(m, "va_img", vis, P, KP, sc["inv_v"], qtmp, tern[W_IMG][:], vec, sc["p_v"][:, 0:1], bias[:, 1:2],
                      sc["max_i"][:], avg[:], real=KV)
            all_partitions(m, "i", sc["max_i"][:], sc["top_i"][:], RMAX)
            input_scale(m, sc["top_i"][:], [wsc[:, W_ATT0 + i:W_ATT0 + i + 1] for i in range(2)], sc["inv_i"][:],
                        [satt[:, i:i + 1] for i in range(2)], step_img[:])
            input_scale(m, top[:, 1:2], [wsc[:, W_TXT:W_TXT + 1]], sc["inv_x"][:], [sc["p_x"][:]], sc["step"][:])
            with nc.Block() as block:
                @block.vector
                def _(dve):
                    nc.vector.tensor_scalar(avg[:], avg[:], 1.0 / KV, None, ALU.mult)
                    m.dve(dve, nc.vector.tensor_scalar(vis[:], vec[:], sc["inv_i"][:], MAGIC, ALU.mult, ALU.add))
                    nc.vector.tensor_scalar(qimg[:], vis[:], MAGIC, 127.0, ALU.subtract, ALU.min)
            bit_layer(m, "va_txt", m.xT, P, NT, sc["inv_x"], qtmp, tern[W_TXT][:], fT, sc["p_x"][:, 0:1], bias[:, 2:3],
                      sc["max_f"][:])

        for layer in range(2):
            one_head_attention(m, f"v{layer}", qimg, fT, tern[W_ATT0 + layer], tern_out[layer], satt[:, layer:layer + 1], batt[layer])
        vision_mlp(m, fT, avg, wsc, tern, bf1, bf2)


def one_head_attention(m, name, qimg, fT, wT, w_out, scale, b_row):
    nc = m.nc
    with ExitStack() as ctx:
        def sb(n, shape, dt=F32):
            return m.sb(f"{name}_{n}", shape, dt, ctx)

        kv = sb("kv", [P, KT, 64])
        g32, rest = sb("g32", [P, NT]), sb("rest", [P, NT])
        gp = [sb(f"g{i}", [P, NT], BF16) for i in range(3)]
        mx, top = sb("mx", [P, TT, NB]), sb("top", [P, TT])
        hl, mt, neg = sb("hl", [P, 2, TT], BF16), sb("mt", [2 * TT, P], BF16), sb("neg", [P, NT], BF16)
        pick2 = sb("pick2", [P, P], BF16)
        kvs = [sb(f"kvs{t}", [P, 64]) for t in range(TPB)]
        total = sb("total", [P, 2, HALF])
        ones = sb("ones", [P, 64])
        counted = sb("counted", [P, NB])
        table_warm = sb("table_warm", [P, 1])
        prob = sb("prob", [P, 6, HALF])
        zero = sb("zero", [1, HALF], BF16)
        rec, o = sb("rec", [P, HALF]), sb("o", [P, HALF])
        odup = sb("odup", [P, NT])
        (kv_ps, kv_sb, g_ps, g_sb, g_parts, init, a_scores, a_maxed, hl_ready, mt_ps, mt_ready, neg_ready, kvs_ready, scores,
         probs, used, summed, pv_done, o_ready, o_in) = (m.sem(f"{name}_{s}") for s in (
             "kvps", "kvsb", "gps", "gsb", "gparts", "init", "ascores", "amaxed", "hl", "mtps", "mt", "neg", "kvs", "scores",
             "probs", "used", "summed", "pvdone", "o", "oin"))
        groups = [(g * TT, min(TT, KT - g * TT)) for g in range(-(-KT // TT))]
        with nc.Block() as block:
            @block.tensor
            def _(pe):
                for h in range(2):
                    nc.tensor.matmul(m.ps[:, 4 + h, :], w_out[:], fT[:, h * HALF:(h + 1) * HALF], start=True, stop=True).then_inc(g_ps, 1)
                for i, (t0, n) in enumerate(groups):
                    if i >= 2:
                        pe.wait_ge(kv_sb, i - 1)
                    for t in range(n):
                        ins = nc.tensor.matmul(m.ps[:, i % 2, t * 64:(t + 1) * 64], qimg[:, (t0 + t) * P:(t0 + t + 1) * P], wT[:],
                                               start=True, stop=True)
                    ins.then_inc(kv_ps, 1)

            @block.scalar
            def _(act):
                nc.scalar.activation(table_warm[:], m.eps[:], ACT.Exp)
                for h in range(2):
                    act.wait_ge(g_ps, h + 1)
                    nc.scalar.activation(g32[:, h * HALF:(h + 1) * HALF], m.ps[:, 4 + h, :], ACT.Copy, scale=scale).then_inc(g_sb, 1)

            @block.vector
            def _(dve):
                nc.vector.memset(neg[:], 0.0)
                nc.vector.memset(total[:], 0.0)
                nc.vector.memset(ones[:], 1.0)
                nc.vector.memset(pick2[:], 0.0)
                m.dve(dve, nc.vector.memset(counted[:], 1.0))
                nc.vector.tensor_copy(counted[:, NB - 1:NB], m.padm[:])
                dve.wait_ge(g_sb, 2)
                split3(m, dve, g32[:], gp[0][:], gp[1][:], gp[2][:], rest[:], g_parts)
                for i, (t0, n) in enumerate(groups):
                    dve.wait_ge(kv_ps, i + 1)
                    nc.vector.scalar_tensor_tensor(kv[:, t0:t0 + n, 0:64],
                                                   m.ps[:, i % 2, 0:n * 64].rearrange("p (t c) -> p t c", c=64), scale,
                                                   b_row[:].unsqueeze(1).to_broadcast([P, n, 64]), ALU.mult, ALU.add).then_inc(kv_sb, 1)
                dve.wait_ge(kv_sb, len(groups))
                nc.vector.tensor_scalar(kv[:, KT - 1, :], kv[:, KT - 1, :], m.padm[:, 0:1], None, ALU.mult)
                nc.vector.memset(pick2[0:2, :], 1.0)
                nc.vector.memset(zero[:], 0.0)

        with nc.Block() as block:
            @block.tensor
            def _(pe):
                with pe.Fori(0, NB) as c:
                    for u in range(4):
                        pe.wait_ge(a_maxed, c * 4 + u + 1)
                        for j in range(2):
                            q = (2 * u + j) * P
                            for i in range(2):
                                ins = nc.tensor.matmul(m.ps[:, 2 * u + j, 0:BLK], gp[i][:, q:q + P],
                                                       qimg[:, bass.ds(c * BLK, BLK)], start=i == 0, stop=i == 1)
                        ins.then_inc(a_scores, 1)
                pe.wait_ge(hl_ready, 1)
                nc.tensor.transpose(m.ps[0:2 * TT, 0, 0:P // 2].bitcast(BF16), hl[:].rearrange("p a b -> p (a b)"),
                                    m.identb[:]).then_inc(mt_ps, 1)

            @block.vector
            def _(dve):
                dve.sem_inc(a_maxed, 4)
                with dve.Fori(0, NB) as c:
                    for u in range(4):
                        dve.wait_ge(a_scores, c * 4 + u + 1)
                        nc.vector.tensor_reduce(mx[:, 2 * u:2 * u + 2, bass.ds(c, 1)], m.ps[:, 2 * u:2 * u + 2, 0:BLK],
                                                AX.X, ALU.max).then_inc(a_maxed, 1)
                dve.wait_ge(a_maxed, 4 * NB + 4)
                m.dve(dve, nc.vector.tensor_reduce(top[:], mx[:], AX.X, ALU.max))
                m.dve(dve, nc.vector.tensor_scalar(hl[:, 0, :], top[:], -1.0, None, ALU.mult))
                nc.vector.scalar_tensor_tensor(hl[:, 1, :], top[:], -1.0, hl[:, 0, :], ALU.mult, ALU.subtract).then_inc(hl_ready, 1)
                dve.wait_ge(mt_ps, 1)
                nc.vector.tensor_copy(mt[:], m.ps[0:2 * TT, 0, 0:P // 2].bitcast(BF16)).then_inc(mt_ready, 1)

            @block.sync
            def _(sp):
                sp.wait_ge(mt_ready, 1)
                sp.dma_start(neg[0:2, :], mt[:]).then_inc(neg_ready, 16)
                sp.wait_ge(neg_ready, 16)

        O, D = m.ps[:, 6, :], m.ps[:, 7, :]
        with nc.Block() as block:
            @block.tensor
            def _(pe):
                def value_step(c, t):
                    pe.wait_ge(kvs_ready, c * TPB + t + 1)
                    pe.wait_ge(probs, c * 6 + 2 * t + 2 + 3)
                    for h in range(2):
                        ins = nc.tensor.matmul(O[64 * h:64 * h + 64, :], kvs[t][:], prob[:, 2 * t + h, :], start=False, stop=False)
                    ins.then_inc(used, 1)

                def attend(c, first=False):
                    for i in range(6):
                        t, h = i // 2, i % 2
                        pe.wait_ge(probs, c * 6 + i + 1)
                        x = slice(h * HALF, (h + 1) * HALF)
                        for j in range(3):
                            nc.tensor.matmul(m.ps[:, i % 3, :], qimg[:, bass.ds(c * BLK + t * P, P)], gp[j][:, x],
                                             start=j == 0, stop=False)
                        nc.tensor.matmul(m.ps[:, i % 3, :], pick2[:], neg[:, x], start=False, stop=True).then_inc(scores, 1)
                        if i in (3, 5):
                            value_step(c, i // 2 - 1)
                        elif i == 1 and not first:
                            value_step(c - 1, 2)

                for h in range(2):
                    nc.tensor.matmul(O[64 * h:64 * h + 64, :], zero[0:1, 0:64], zero[0:1, :], start=True, stop=False)
                pe.sem_inc(used, 3)
                attend(0, first=True)
                with pe.Fori(0, NB - 1) as c:
                    attend(c + 1)
                value_step(NB - 1, 2)
                pe.wait_ge(summed, 6 * NB + 6)
                for h in range(2):
                    nc.tensor.matmul(O[64 * h:64 * h + 64, :], zero[0:1, 0:64], zero[0:1, :], start=False, stop=True)
                    ins = nc.tensor.matmul(D[64 * h:64 * h + 64, :], ones[:], total[:, h, :], start=True, stop=True)
                ins.then_inc(pv_done, 1)

            @block.scalar
            def _(act):
                act.sem_inc(probs, 3)
                with act.Fori(0, NB) as c:
                    for i in range(6):
                        if i % 2 == 0:
                            act.wait_ge(used, c * TPB + i // 2 + 1)
                        act.wait_ge(summed, c * 6 + i + 1)
                        act.wait_ge(scores, c * 6 + i + 1)
                        nc.scalar.activation(prob[:, i, :], m.ps[:, i % 3, :], ACT.Exp, scale=1.0 / float(np.sqrt(P))).then_inc(probs, 1)

            @block.gpsimd
            def _(pool):
                with pool.Fori(0, NB) as c:
                    for t in range(TPB):
                        pool.wait_ge(used, c * TPB + t + 1)
                        nc.gpsimd.tensor_copy(kvs[t][:], kv[:, bass.ds(c * TPB + t, 1), :].rearrange("p a b -> p (a b)")).then_inc(kvs_ready, 1)

            @block.vector
            def _(dve):
                dve.sem_inc(summed, 6)
                with dve.Fori(0, NB) as c:
                    for i in range(6):
                        dve.wait_ge(probs, c * 6 + i + 1 + 3)
                        dve.wait_ge(summed, c * 6 + i + 5)
                        o_sum = total[:, i % 2, :]
                        if i < 4:
                            nc.vector.tensor_tensor(o_sum, o_sum, prob[:, i, :], ALU.add).then_inc(summed, 1)
                        else:
                            nc.vector.scalar_tensor_tensor(o_sum, prob[:, i, :], counted[:, bass.ds(c, 1)], o_sum,
                                                           ALU.mult, ALU.add).then_inc(summed, 1)
                dve.wait_ge(pv_done, 1)
                m.dve(dve, nc.vector.reciprocal(rec[:], D))
                nc.vector.scalar_tensor_tensor(o[:], O, 0.1, rec[:], ALU.mult, ALU.mult).then_inc(o_ready, 1)
                dve.wait_ge(o_in, 64)
                nc.vector.tensor_tensor(fT[:], fT[:], odup[:], ALU.add)

            @block.sync
            def _(sp):
                sp.wait_ge(o_ready, 1)
                for h in range(2):
                    for d in range(2):
                        sp.dma_start(odup[64 * d:64 * d + 64, h * HALF:(h + 1) * HALF], o[64 * h:64 * h + 64, :]).then_inc(o_in, 16)


def vision_mlp(m, fT, avg, wsc, tern, bf1, bf2):
    nc = m.nc
    with ExitStack() as ctx:
        def sb(n, shape, dt=F32):
            return m.sb("vm_" + n, shape, dt, ctx)

        tops, top = sb("tops", [P, 2]), sb("top", [P, 2])
        big, inv, prod, step, inv2, prod2, hmax, htop = (
            sb(n, [P, 1]) for n in ("big", "inv", "prod", "step", "inv2", "prod2", "hmax", "htop"))
        tmp, qf = sb("tmp", [P, NT]), sb("qf", [P, NT], BF16)
        tav, qav = sb("tav", [P, 1]), sb("qav", [P, HALF], BF16)
        hid, qh = sb("hid", [P, 4, NT]), sb("qh", [P, 4, NT], BF16)
        htops = sb("htops", [P, 8])
        yb = sb("yb", [P, TT, P])
        mm, ev, q2, y_ps = (m.sem("vm_" + n) for n in ("mm", "ev", "q2", "y"))
        with nc.Block() as block:
            @block.vector
            def _(dve):
                nc.vector.tensor_reduce(tops[:, 0:1], fT[:], AX.X, ALU.max, apply_absolute_value=True)
                nc.vector.tensor_reduce(tops[:, 1:2], avg[:], AX.X, ALU.max, apply_absolute_value=True)
        all_partitions(m, "f", tops[:], top[:], RMAX)
        with nc.Block() as block:
            @block.vector
            def _(dve):
                nc.vector.tensor_tensor(big[:], top[:, 0:1], top[:, 1:2], ALU.max)
        input_scale(m, big[:], [wsc[:, W_F1:W_F1 + 1]], inv[:], [prod[:]], step[:])
        with nc.Block() as block:
            @block.vector
            def _(dve):
                q = m.sem("vm_q")
                m.dve(dve, nc.vector.tensor_scalar(tmp[:], fT[:], inv[:], MAGIC, ALU.mult, ALU.add))
                m.dve(dve, nc.vector.tensor_scalar(tav[:], avg[:], inv[:], MAGIC, ALU.mult, ALU.add))
                nc.vector.tensor_scalar(qav[:], tav[:].to_broadcast([P, HALF]), MAGIC, 127.0, ALU.subtract, ALU.min).then_inc(q2, 1)
                nc.vector.tensor_scalar(qf[:], tmp[:], MAGIC, 127.0, ALU.subtract, ALU.min).then_inc(q2, 1)
                for i in range(8):
                    dve.wait_ge(ev, i + 1)
                    ins = nc.vector.tensor_reduce(htops[:, i:i + 1], hid[:, i // 2, i % 2 * HALF:(i % 2 + 1) * HALF], AX.X, ALU.max)
                m.dve(dve, ins)
                nc.vector.tensor_reduce(hmax[:], htops[:], AX.X, ALU.max)

            @block.tensor
            def _(pe):
                pe.wait_ge(q2, 2)
                for i in range(8):
                    c, h = i // 2, i % 2
                    if i >= 4:
                        pe.wait_ge(ev, i - 3)
                    nc.tensor.matmul(m.ps[:, i % 4, :], tern[W_F1][:, c * P:(c + 1) * P], qf[:, h * HALF:(h + 1) * HALF], start=True, stop=False)
                    nc.tensor.matmul(m.ps[:, i % 4, :], tern[W_F1][:, FF0 + c * P:FF0 + (c + 1) * P], qav[:], start=False,
                                     stop=True).then_inc(mm, 1)

            @block.scalar
            def _(act):
                for i in range(8):
                    act.wait_ge(mm, i + 1)
                    nc.scalar.activation(hid[:, i // 2, i % 2 * HALF:(i % 2 + 1) * HALF], m.ps[:, i % 4, :], ACT.Relu,
                                         scale=prod[:, 0:1], bias=bf1[:, i // 2:i // 2 + 1]).then_inc(ev, 1)
        all_partitions(m, "h", hmax[:], htop[:], RMAX)
        input_scale(m, htop[:], [wsc[:, W_F2:W_F2 + 1]], inv2[:], [prod2[:]], step[:])
        with nc.Block() as block:
            @block.vector
            def _(dve):
                q = 0
                for c in range(4):
                    m.dve(dve, nc.vector.tensor_scalar(hid[:, c, :], hid[:, c, :], inv2[:], MAGIC, ALU.mult, ALU.add))
                    ins = nc.vector.tensor_scalar(qh[:, c, :], hid[:, c, :], MAGIC, 127.0, ALU.subtract, ALU.min)
                ins.then_inc(y_ps, 1)
                dve.wait_ge(y_ps, 2)
                yp = m.ps[:, 4:6, :].rearrange("p a (b c) -> p (a b) c", c=P)
                nc.vector.scalar_tensor_tensor(yb[:], yp, prod2[:, 0:1], bf2[:].unsqueeze(1).to_broadcast([P, TT, P]), ALU.mult, ALU.add)

            @block.tensor
            def _(pe):
                pe.wait_ge(y_ps, 1)
                for t in range(TT):
                    for c in range(4):
                        ins = nc.tensor.matmul(m.ps[:, 4 + t // 4, t % 4 * P:(t % 4 + 1) * P], qh[:, c, t * P:(t + 1) * P],
                                               tern[W_F2][:, c * P:(c + 1) * P], start=c == 0, stop=c == 3)
                ins.then_inc(y_ps, 1)
        layernorm(m, "ln4", yb)


STAGES = [deform_attention, cross_attention, experts_gelu, s4_layer, vision_attention, experts_silu]


def decoder_kernel(nc, a, out, first=0, last=6):
    with ExitStack() as ctx:
        m = Machine(nc, ctx, a)
        m.out = out
        setup(m)
        for s in STAGES[first:last]:
            s(m)
            m.end_stage()
        if last < 6:
            done = m.sem("dbg")
            with nc.Block() as block:
                @block.sync
                def _(sp):
                    sp.dma_start(out.rearrange("(t p) d -> p t d", p=P), m.xtok[:]).then_inc(done, 16)
                    sp.wait_ge(done, 16)


def layout(i):
    f = np.float32

    def row(v):
        return np.reshape(v, (1, -1))

    def col(v):
        return np.reshape(v, (-1, 1))

    def both(v):
        return np.concatenate([v.T, v.T], 0)

    x = i["x"][0]
    re = (np.arange(P) < NS).astype(f)
    l = np.arange(NT)
    turn = np.outer(l, l) % (2 * NF) * (np.pi / NF)
    alt = (1 - 2 * (l % 2)).astype(f)
    quarter, zero = np.full(P, 0.25, f), np.zeros(P, f)
    a = {
        "c_ident": np.eye(P, dtype=f), "c_iota": np.arange(P, dtype=f).reshape(P, 1),
        "c_pad": (np.arange(P) < LASTV).astype(f).reshape(P, 1),
        "c_flip": np.eye(HPO, dtype=f)[::-1],
        "x_tok": x, "x_T": x.T, "ctx_T": i["ctx_768"][0].T,
        "da_w": np.concatenate([i["L0_attn_W_off"][:, 0::2], i["L0_attn_W_attn"]], 1),
        "da_b": row(np.concatenate([i["L0_attn_b_off"][0::2], i["L0_attn_b_attn"]])),
        "da_wout": i["L0_attn_W_out"], "da_bout": row(i["L0_attn_b_out"]),
        "ca_wk": np.concatenate([i["L0_xattn_wk"].T, row(i["L0_xattn_bk"])], 0),
        "ca_wv": np.concatenate([i["L0_xattn_wv"].T, row(i["L0_xattn_bv"])], 0),
        "ca_wq": i["L0_xattn_wq"].T, "ca_bq": col(i["L0_xattn_bq"]),
        "c_rev": np.tile(np.arange(NE, 0, -1, dtype=f), (P, 1)),
        "m0_gate": i["L0_ffn_gate_w"], "m0_w1": i["L0_ffn_w1"], "m0_w2": i["L0_ffn_w2"],
        "m0_b1": i["L0_ffn_b1"].reshape(NE, FF0 // P, P).transpose(0, 2, 1), "m0_b2": i["L0_ffn_b2"].T,
        "m1_gate": i["L1_ffn_gate_w"].T, "m1_wg": i["L1_ffn_w_gate"], "m1_wu": i["L1_ffn_w_up"], "m1_wd": i["L1_ffn_w_down"],
        "c_s4": np.stack([quarter * re, np.pi / 2 * re, quarter * (1 - re), np.pi / 2 * (1 - re), 4 * re - 2, zero, zero, zero],
                         1).astype(f),
        "c_bsteps": np.tile(np.arange(32, dtype=f), (P, 1)), "c_asteps": np.tile(np.arange(0, NT, 32, dtype=f), (P, 1)),
        "c_dft": np.concatenate([np.cos(turn), np.sin(turn)], 1).astype(f), "c_altc": alt[0:P].reshape(P, 1), "c_altr": row(alt),
        "s4_ldt": np.broadcast_to(i["L1_attn_log_dt"], (P, P)), "s4_arl": both(i["L1_attn_A_real_log"]),
        "s4_aim": both(i["L1_attn_A_imag"]), "s4_cre": both(i["L1_attn_C_real"]), "s4_cim": both(i["L1_attn_C_imag"]),
        "s4_d": col(i["L1_attn_D"]), "s4_wout": i["L1_attn_W_out"], "s4_bout": row(i["L1_attn_b_out"]),
        "va_w0": i["L1_xattn_W_d2v"].T, "va_w1": i["L1_xattn_W_img"].T, "va_w2": i["L1_xattn_W_txt"].T,
        "va_w3": i["L1_xattn_W_att0"].T, "va_w4": i["L1_xattn_W_att1"].T,
        "va_w5": i["L1_xattn_W_f1"].T.reshape(2, P, FF0).transpose(1, 0, 2).reshape(P, 2 * FF0),
        "va_w6": i["L1_xattn_W_f2"].T.reshape(4, P, P).transpose(1, 0, 2).reshape(P, 4 * P),
        "va_wo0": np.concatenate([i["L1_xattn_W_att0"]] * 2, 0), "va_wo1": np.concatenate([i["L1_xattn_W_att1"]] * 2, 0),
        "c_inv": np.tile(np.array([1 / (CD * P), 1 / (P * P), 1 / (P * P), 1 / (64 * P), 1 / (64 * P), 1 / (2 * P * FF0), 1 / (P * FF0)], f), (P, 1)),
        "va_bias": np.stack([i["L1_xattn_b_d2v"], i["L1_xattn_b_img"], i["L1_xattn_b_txt"]], 1),
        "va_batt0": np.broadcast_to(i["L1_xattn_b_att0"], (P, 64)), "va_batt1": np.broadcast_to(i["L1_xattn_b_att1"], (P, 64)),
        "va_bf1": i["L1_xattn_b_f1"].reshape(4, P).T, "va_bf2": np.broadcast_to(i["L1_xattn_b_f2"], (P, P)),
        "ca_wo": i["L0_xattn_wo"].T, "ca_bo": row(i["L0_xattn_bo"]),
    }
    return {k: np.ascontiguousarray(v) for k, v in a.items()}


def kernel(**inputs):
    import concourse.bacc as bacc
    from concourse.bass_utils import run_bass_kernel_spmd

    arrays = layout({k: np.asarray(v) for k, v in inputs.items()})
    nc = bacc.Bacc("TRN2", target_bir_lowering=False, num_devices=1)
    a = {k: nc.dram_tensor(k, v.shape, mybir.dt.from_np(v.dtype), kind="ExternalInput").ap() for k, v in arrays.items()}
    out = nc.dram_tensor("out", (NT, P), F32, kind="ExternalOutput").ap()
    decoder_kernel(nc, a, out)
    r = run_bass_kernel_spmd(nc, [arrays], core_ids=[0])
    return np.reshape(r.results[0]["out"], (1, NT, P))
```

```python
from contextlib import ExitStack

import numpy as np

import concourse.bass as bass
from concourse import mybir

F32 = mybir.dt.float32
BF16 = mybir.dt.bfloat16
ALU = mybir.AluOpType
ACT = mybir.ActivationFunctionType
AX = mybir.AxisListType
RADD = bass.bass_isa.ReduceOp.add
RMAX = bass.bass_isa.ReduceOp.max

P = 128
NT = 1024
TT = NT // P
HALF = 512
KV = 6404
KT = -(-KV // P)
KP = KT * P
CD = 96
TPB = 3
NB = KT // TPB
BLK = TPB * P
LASTV = KV - (KT - 1) * P
NH, HD = 16, 8
NPAIR = NH // 2
HPO = 32
NE = 8
FF0, FF1 = 512, 256
NF = 1024
NS = 64
MAGIC = 12582912.0
TWO_PI = 6.283185307179586
TWO_PI_HI = 6.28125
TWO_PI_LO = TWO_PI - TWO_PI_HI
PI_BELOW = 3.1415925
LN2 = 0.6931471805599453
LN2_HI = 0.693359375
LN2_LO = LN2 - LN2_HI
EPS = 1e-5
BIG = 1.0e38
Q_PART = (0, 0, 1, 1, 0, 2)
K_PART = (0, 1, 0, 1, 2, 0)
SPLIT_ROWS = len(Q_PART) * HD
ATTENTION_STEP = "m0 s0 s1 s2 v2 m1 s3 s4 m2 s5 s6 m3 s7 s8 m4 v0 m5 s9 s10 m6 s11 v1 m7"
LAST_STEP = "s0 s1 s2 v2 s3 s4 f s5 s6 n0 s7 s8 v0 n1 s9 s10 n2 s11 v1 n3"
LAST_STEP_ALONE = "s0 s1 s2 v2 s3 s4 f s5 s6 s7 s8 v0 s9 s10 s11 v1"


class Chain:

    def __init__(self, sem):
        self.sem, self.n = sem, 0

    def __call__(self, eng, ins):
        self.n += 1
        ins.then_inc(self.sem, 1)
        eng.wait_ge(self.sem, self.n)


class Machine:

    def __init__(self, nc, ctx, a):
        self.nc, self.ctx, self.a = nc, ctx, a
        self.stage_sems = []
        self.ps = ctx.enter_context(nc.psum_tensor("ps", [P, 8, 512], F32))
        self.ident = self.sb("ident", [P, P])
        self.identb = self.sb("identb", [P, P], BF16)
        self.ones_row = self.sb("ones_row", [1, HALF])
        self.eps = self.sb("eps", [P, 1])
        self.xtok = self.sb("xtok", [P, TT, P])
        self.xT = self.sb("xT", [P, NT])
        self.padm = self.sb("padm", [P, 1])
        self.dve = Chain(self.sem("dve_own"))
        self.act = Chain(self.sem("act_own"))
        self.pool = Chain(self.sem("pool_own"))
        self.stage_sems = []

    def sb(self, name, shape, dt=F32, ctx=None):
        return (ctx or self.ctx).enter_context(self.nc.sbuf_tensor(name + "_sb", shape, dt))

    def sem(self, name):
        self.stage_sems.append(self.nc.alloc_semaphore(name))
        return self.stage_sems[-1]

    def end_stage(self):
        self.nc.clear_and_free_semaphores(self.stage_sems)
        self.nc.all_engine_barrier()
        self.stage_sems = []


def setup(m):
    nc, a = m.nc, m.a
    loaded = m.sem("setup_loaded")
    with nc.Block() as block:
        @block.sync
        def _(sp):
            sp.dma_start(m.ident[:], a["c_ident"]).then_inc(loaded, 16)
            sp.dma_start(m.padm[:], a["c_pad"]).then_inc(loaded, 16)
            sp.dma_start(m.xtok[:], a["x_tok"].rearrange("(t p) d -> p t d", p=P)).then_inc(loaded, 16)
            sp.dma_start(m.xT[:], a["x_T"]).then_inc(loaded, 16)

        @block.vector
        def _(dve):
            nc.vector.memset(m.ones_row[:], 1.0)
            nc.vector.memset(m.eps[:], EPS)
            dve.wait_ge(loaded, 64)
            nc.vector.tensor_copy(m.identb[:], m.ident[:])


def layernorm(m, name, y, out=None):
    nc = m.nc
    with ExitStack() as ctx:
        res = m.sb(name + "_res", [P, TT, P], ctx=ctx)
        stats = m.sb(name + "_stats", [P, TT, 6], ctx=ctx)
        mv = m.sb(name + "_mv", [P, TT, 2], ctx=ctx)
        std = m.sb(name + "_std", [P, TT], ctx=ctx)
        rstd = m.sb(name + "_rstd", [P, TT], ctx=ctx)
        sum_ready, stats_ready, var_ready, std_ready, x_ready, xt_ps, stored = (
            m.sem(f"{name}_{s}") for s in ("sum", "stats", "var", "std", "x", "xt", "stored"))
        block = ctx.enter_context(nc.Block())

        @block.vector
        def _(dve):
            for g in range(2):
                nc.vector.tensor_tensor(res[:, 4 * g:4 * g + 4, :], y[:, 4 * g:4 * g + 4, :],
                                        m.xtok[:, 4 * g:4 * g + 4, :], ALU.add).then_inc(sum_ready, 1)
            for t in range(TT):
                dve.wait_ge(sum_ready, 1 + t // 4)
                nc.vector.bn_stats(stats[:, t, :], res[:, t, :]).then_inc(stats_ready, 1)
            dve.wait_ge(stats_ready, TT)
            for t in range(TT):
                last = nc.vector.bn_aggr(mv[:, t, :], stats[:, t, :])
                last.then_inc(var_ready, 1)
            dve.wait_ge(std_ready, 1)
            m.dve(dve, nc.vector.reciprocal(rstd[:], std[:]))
            for t in range(TT):
                nc.vector.tensor_scalar(m.xtok[:, t, :], res[:, t, :], mv[:, t, 0:1], rstd[:, t:t + 1],
                                        ALU.subtract, ALU.mult).then_inc(x_ready, 1)
            if out is None:
                dve.wait_ge(xt_ps, 1)
                nc.vector.tensor_copy(m.xT[:, 0:HALF], m.ps[:, 6, :])

        @block.scalar
        def _(act):
            act.wait_ge(var_ready, TT)
            nc.scalar.activation(std[:], mv[:, :, 1], ACT.Sqrt, bias=m.eps[:, 0:1]).then_inc(std_ready, 1)
            if out is None:
                act.wait_ge(xt_ps, 2)
                nc.scalar.activation(m.xT[:, HALF:NT], m.ps[:, 7, :], ACT.Copy)

        @block.tensor
        def _(pe):
            if out is None:
                for t in range(TT):
                    pe.wait_ge(x_ready, t + 1)
                    ins = nc.tensor.transpose(m.ps[:, 6 + t // 4, (t % 4) * P:(t % 4 + 1) * P], m.xtok[:, t, :], m.ident[:])
                    if t % 4 == 3:
                        ins.then_inc(xt_ps, 1)

        @block.sync
        def _(sp):
            if out is not None:
                sp.wait_ge(x_ready, TT)
                sp.dma_start(out.rearrange("(t p) d -> p t d", p=P), m.xtok[:]).then_inc(stored, 16)
                sp.wait_ge(stored, 16)


def deform_attention(m):
    nc, a = m.nc, m.a
    with ExitStack() as ctx:
        def sb(name, shape, dt=F32):
            return m.sb("da_" + name, shape, dt, ctx)

        w = sb("w", [P, 2 * HPO])
        b = sb("b", [1, 2 * HPO])
        wout = sb("wout", [P, P])
        bout = sb("bout", [1, P])
        iota = sb("iota", [P, 1])
        ones = sb("ones", [P, 3 * HPO])
        sh = [P, TT, HPO]
        lg, off, mag, fl, gt, sg, neg, idx, prob = (sb(n, sh) for n in ("lg", "off", "mag", "fl", "gt", "sg", "neg", "idx", "prob"))
        prob3 = sb("prob3", [P, TT, 3, HPO])
        mx, den = sb("mx", [P, TT * 8]), sb("den", [P, TT * 8])
        x0r = sb("x0r", [P, 1])
        zx = sb("zx", [P, 4 * HPO], BF16)
        blank = sb("blank", [P, HALF], BF16)
        flip = sb("flip", [HPO, HPO])
        sel = sb("sel", [P, HPO, P], BF16)
        idxT = sb("idxT", [P, NT], BF16)
        wT = sb("wT", [3 * HPO, NT])
        hot = sb("hot", [P, 4, HALF], BF16)
        gw = sb("gw", [3 * HPO, NT])
        cs = sb("cs", [3 * HPO, P])
        loaded, proj, lg_ready, e_ready, t_ready, tps, oh_in, bc, oh, cs_ps, gsum, gw_ready = (
            m.sem("da_" + s) for s in ("loaded", "proj", "lg", "exp", "tok", "tps", "ohin", "bcast", "onehot", "cs", "gsum", "gw"))
        op = m.ps[:, 0, :].rearrange("p (t c) -> p t c", t=TT)

        def g4(t):
            return t[:].rearrange("p t (h q) -> p (t h) q", q=4)

        def b4(t):
            return t[:].unsqueeze(2).to_broadcast([P, TT * 8, 4])

        with nc.Block() as block:
            @block.sync
            def _(sp):
                for dst, src in ((w, "da_w"), (b, "da_b"), (wout, "da_wout"), (bout, "da_bout"), (iota, "c_iota"),
                                 (flip, "c_flip")):
                    sp.dma_start(dst[:], a[src]).then_inc(loaded, 16)

            @block.tensor
            def _(pe):
                pe.wait_ge(loaded, 96)
                for t in range(TT):
                    nc.tensor.matmul(op[:, t, :], m.xT[:, t * P:(t + 1) * P], w[:], start=True, stop=False)
                    nc.tensor.matmul(op[:, t, :], m.ones_row[0:1, 0:P], b[:], start=False, stop=True).then_inc(proj, 1)
                pe.wait_ge(t_ready, 2)
                for t in range(TT):
                    c = slice((t % 4) * P, (t % 4 + 1) * P)
                    nc.tensor.transpose(m.ps[0:HPO, 1 + t // 4, c], idx[:, t, :], m.ident[:])
                    nc.tensor.transpose(m.ps[0:3 * HPO, 3 + t // 4, c], prob3[:, t].rearrange("p s k -> p (s k)"), m.ident[:]).then_inc(tps, 1)
                pe.wait_ge(oh_in, 1)
                nc.tensor.matmul(m.ps[0:3 * HPO, 5, 0:P], ones[:], wout[:], start=True, stop=True).then_inc(cs_ps, 1)

            @block.vector
            def _(dve):
                def own(ins):
                    m.dve(dve, ins)

                nc.vector.memset(ones[:], 1.0).then_inc(oh_in, 1)
                nc.vector.memset(blank[:], 0.0)
                nc.vector.memset(idxT[:], 0.0)
                own(nc.vector.memset(sel[:], 0.0))
                own(nc.vector.memset(zx[:], 0.0))
                own(nc.vector.tensor_copy(zx[:, HPO - 1:HPO], m.xT[:, 0:1]))
                own(nc.vector.tensor_tensor(x0r[:], m.xT[:, 0:1], zx[:, HPO - 1:HPO], ALU.subtract))
                own(nc.vector.tensor_copy(zx[:, 2 * HPO - 1:2 * HPO], x0r[:]))
                own(nc.vector.tensor_tensor(zx[:, 3 * HPO - 1:3 * HPO], x0r[:], zx[:, 2 * HPO - 1:2 * HPO], ALU.subtract))
                dve.wait_ge(loaded, 96)
                own(nc.vector.tensor_copy(sel[0:HPO], flip[:].unsqueeze(2).to_broadcast([HPO, HPO, P])))
                dve.wait_ge(proj, TT)
                own(nc.vector.tensor_copy(lg[:], op[:, :, HPO:2 * HPO]))
                own(nc.vector.tensor_reduce(mx[:], g4(lg), AX.X, ALU.max))
                nc.vector.tensor_tensor(g4(lg), g4(lg), b4(mx), ALU.subtract).then_inc(lg_ready, 1)
                own(nc.vector.tensor_copy(off[:], op[:, :, 0:HPO]))
                own(nc.vector.scalar_tensor_tensor(mag[:], off[:], -1.0, off[:], ALU.mult, ALU.max))
                own(nc.vector.tensor_scalar(mag[:], mag[:], 1000.0, None, ALU.min))
                own(nc.vector.tensor_scalar(fl[:], mag[:], MAGIC, MAGIC, ALU.add, ALU.subtract))
                own(nc.vector.tensor_tensor(gt[:], fl[:], mag[:], ALU.is_gt))
                own(nc.vector.tensor_tensor(fl[:], fl[:], gt[:], ALU.subtract))
                own(nc.vector.tensor_scalar(sg[:], off[:], 0.0, -2.0, ALU.is_lt, ALU.mult))
                own(nc.vector.tensor_scalar(sg[:], sg[:], 1.0, None, ALU.add))
                own(nc.vector.tensor_tensor(fl[:], fl[:], sg[:], ALU.mult))
                own(nc.vector.tensor_scalar(neg[:], fl[:], 0.0, float(P), ALU.is_lt, ALU.mult))
                own(nc.vector.tensor_tensor(fl[:], fl[:], neg[:], ALU.add))
                nc.vector.tensor_scalar(idx[:], fl[:], 0.0, float(P - 1), ALU.max, ALU.min).then_inc(t_ready, 1)
                dve.wait_ge(e_ready, 1)
                own(nc.vector.tensor_reduce(den[:], g4(lg), AX.X, ALU.add))
                own(nc.vector.reciprocal(den[:], den[:]))
                own(nc.vector.tensor_tensor(g4(prob), g4(lg), b4(den), ALU.mult))
                nc.vector.tensor_copy(prob3[:], prob[:].unsqueeze(2).to_broadcast([P, TT, 3, HPO])).then_inc(t_ready, 1)
                dve.wait_ge(tps, TT)
                nc.vector.tensor_copy(idxT[0:HPO, :], m.ps[0:HPO, 1:3, :].rearrange("p a b -> p (a b)"))
                nc.vector.tensor_copy(wT[:], m.ps[0:3 * HPO, 3:5, :].rearrange("p a b -> p (a b)"))
                dve.wait_ge(cs_ps, 1)
                nc.vector.tensor_copy(cs[:], m.ps[0:3 * HPO, 5, 0:P])

            @block.scalar
            def _(act):
                act.wait_ge(lg_ready, 1)
                nc.scalar.activation(lg[:], lg[:], ACT.Exp).then_inc(e_ready, 1)

        G = m.ps[0:3 * HPO, 4:6, :]
        with nc.Block() as block:
            @block.tensor
            def _(pe):
                def spread(k2, i):
                    nc.tensor.matmul(m.ps[:, i, :], sel[:, bass.ds(k2 * 2 + i // 2, 1), :].rearrange("p a b -> p (a b)"),
                                     idxT[:, i % 2 * HALF:(i % 2 + 1) * HALF], start=True, stop=True).then_inc(bc, 1)

                def gather(k2, i):
                    pe.wait_ge(oh, k2 * 4 + i + 1)
                    nc.tensor.matmul(G[:, i % 2, :], zx[:, bass.ds(k2 * 2 + i // 2, 3 * HPO)],
                                     hot[:, i, :], start=False, stop=False).then_inc(gsum, 1)

                def two_steps(k2, first=False):
                    spread(k2, 0)
                    spread(k2, 1)
                    if not first:
                        gather(k2 - 1, 2)
                        gather(k2 - 1, 3)
                    spread(k2, 2)
                    spread(k2, 3)
                    gather(k2, 0)
                    gather(k2, 1)

                for h in range(2):
                    nc.tensor.matmul(G[:, h, :], blank[:, 0:3 * HPO], blank[:], start=True, stop=False)
                two_steps(0, first=True)
                with pe.Fori(0, HPO // 2 - 1) as k:
                    two_steps(k + 1)
                gather(HPO // 2 - 1, 2)
                gather(HPO // 2 - 1, 3)
                for h in range(2):
                    nc.tensor.matmul(G[:, h, :], blank[:, 0:3 * HPO], blank[:], start=False, stop=True).then_inc(gsum, 1)
                pe.wait_ge(gw_ready, 1)
                for t in range(TT):
                    o = m.ps[:, 6 + t // 4, (t % 4) * P:(t % 4 + 1) * P]
                    nc.tensor.matmul(o, gw[:, t * P:(t + 1) * P], cs[:], start=True, stop=False)
                    nc.tensor.matmul(o, m.ones_row[0:1, 0:P], bout[:], start=False, stop=True)

            @block.vector
            def _(dve):
                dve.sem_inc(gsum, 4)
                with dve.Fori(0, HPO // 2) as k2:
                    for i in range(4):
                        dve.wait_ge(bc, k2 * 4 + i + 1)
                        dve.wait_ge(gsum, k2 * 4 + i + 1)
                        nc.vector.tensor_scalar(hot[:, i, :], m.ps[:, i, :], iota[:, 0:1], None, ALU.is_equal).then_inc(oh, 1)
                dve.wait_ge(gsum, 2 * HPO + 2 + 4)
                nc.vector.tensor_tensor(gw[:], G.rearrange("p a b -> p (a b)"), wT[:], ALU.mult).then_inc(gw_ready, 1)
        layernorm(m, "ln0", m.ps[:, 6:8, :].rearrange("p a (b c) -> p (a b) c", c=P))


def split3(m, dve, src, p1, p2, p3, rest, done):
    nc = m.nc
    m.dve(dve, nc.vector.tensor_copy(p1, src))
    m.dve(dve, nc.vector.tensor_tensor(rest, src, p1, ALU.subtract))
    m.dve(dve, nc.vector.tensor_copy(p2, rest))
    nc.vector.tensor_tensor(p3, rest, p2, ALU.subtract).then_inc(done, 1)


def cross_attention(m):
    nc, a = m.nc, m.a
    with ExitStack() as ctx:
        def sb(name, shape, dt=F32, c=ctx):
            return m.sb("ca_" + name, shape, dt, c)

        sem = {n: m.sem("ca_" + n) for n in (
            "loaded", "ctx0", "ctx1", "ctx2", "k_ps", "k_sb", "k_top", "k_mid", "k_parts", "k_stored0", "k_stored1", "k_stored2", "k_stored3", "v_ps", "v_sb",
            "ones", "filler", "filled", "k_stacked", "q_stacked", "cleared")}
        c0 = ctx.enter_context(ExitStack())
        ks = sb("ks", [P, NPAIR * KP], BF16, c0)
        vs = sb("vs", [P, KT, NH, HD + 1], F32, c0)
        q_stack = sb("qs", [P, 2, NPAIR * NT], BF16, c0)
        qs = [q_stack[:, h, :] for h in range(2)]
        prob = sb("prob", [P, 12, HALF], F32, c0)
        kd = nc.dram_tensor("k_parts", (3, P, KP), BF16, kind="Internal").ap()
        qd = nc.dram_tensor("q_parts", (3, P, NT), BF16, kind="Internal").ap()
        od = nc.dram_tensor("pair_sums", (P, NPAIR * HALF), F32, kind="Internal").ap()
        chunks = [(c * HALF, min(HALF, KP - c * HALF)) for c in range(-(-KP // HALF))]

        with ExitStack() as c1:
            ctxT = q_stack[:].rearrange("p h n -> p (h n)").bitcast(F32)[0:CD + 1, 0:KP]
            wk = sb("wk", [CD + 1, P], F32, c1)
            wv = sb("wv", [CD + 1, P], F32, c1)
            wq = sb("wq", [P, P], F32, c1)
            bq = sb("bq", [P, 1], F32, c1)
            table_warm = sb("table_warm", [P, 1], F32, c1)
            filler = sb("filler", [64 - SPLIT_ROWS, HALF], BF16, c1)
            k32 = prob[:, 0:2, :]
            rest = prob[:, 2:4, :]
            kp = prob[:, 4:10, :].rearrange("p a b -> p (a b)").bitcast(BF16).rearrange("p (i s n) -> p i s n", i=4, s=3)
            block = c1.enter_context(nc.Block())
            n_k = len(chunks)

            pieces = ((0, 3), (3, 7), (7, n_k))
            n_v = -(-KT // 4)

            @block.sync
            def _(sp):
                def stored(n):
                    for slot in range(4):
                        sp.wait_ge(sem[f"k_stored{slot}"], 16 * ((n + 3 - slot) // 4))

                def stack(dst, src, parts, done, lo, hi):
                    for part in range(len(parts)):
                        for h in range(2):
                            r = 64 * h + HD * part
                            sp.dma_start(dst[h][r:r + HD, :].rearrange("p (g n) -> p g n", g=NPAIR)[:, :, lo:hi],
                                         src[parts[part]].rearrange("(g h d) n -> h d g n", h=2, d=HD)[h][:, :, lo:hi]).then_inc(done, 16)

                for dst, src in ((wk, "ca_wk"), (wv, "ca_wv"), (wq, "ca_wq"), (bq, "ca_bq")):
                    sp.dma_start(dst[:], a[src]).then_inc(sem["loaded"], 16)
                for j, (c0_, c1_) in enumerate(pieces):
                    lo, hi = c0_ * HALF, min(c1_ * HALF, KV)
                    sp.dma_start(ctxT[0:CD, lo:hi], a["ctx_T"][:, lo:hi]).then_inc(sem[f"ctx{j}"], 16)
                sp.dma_start(ctxT[0:CD, KV:KP], a["ctx_T"][:, 0:KP - KV]).then_inc(sem["ctx2"], 16)
                sp.wait_ge(sem["filler"], 1)
                for h in range(2):
                    r = 64 * h + SPLIT_ROWS
                    sp.dma_start(ks[r:64 * h + 64, :].rearrange("p (a b) -> p a b", b=HALF),
                                 filler[:].unsqueeze(1).to_broadcast([64 - SPLIT_ROWS, NPAIR * KP // HALF, HALF])).then_inc(sem["filled"], 16)
                for i, (c, n) in enumerate(chunks):
                    sp.wait_ge(sem["k_parts"], i + 1)
                    sp.dma_start(kd[:, :, c:c + n].rearrange("s p n -> p s n"), kp[:, i % 4, :, 0:n]).then_inc(sem[f"k_stored{i % 4}"], 16)
                    for lo, hi in pieces[:-1]:
                        if i == hi + 1:
                            stored(i)
                            stack((ks, ks), kd, K_PART, sem["k_stacked"], lo * HALF, hi * HALF)
                for i in range(2):
                    sp.wait_ge(sem["k_parts"], n_k + i + 1)
                    sp.dma_start(qd[:, :, i * HALF:(i + 1) * HALF].rearrange("s p n -> p s n"),
                                 kp[:, (n_k + i) % 4, :, :]).then_inc(sem[f"k_stored{(n_k + i) % 4}"], 16)
                stored(n_k + 2)
                stack((ks, ks), kd, K_PART, sem["k_stacked"], pieces[-1][0] * HALF, KP)
                sp.wait_ge(sem["cleared"], 2)
                stack(qs, qd, Q_PART, sem["q_stacked"], 0, NT)
                sp.wait_ge(sem["filled"], 32)
                sp.wait_ge(sem["k_stacked"], 16 * 12 * len(pieces))
                sp.wait_ge(sem["q_stacked"], 16 * 12)

            @block.tensor
            def _(pe):
                pe.wait_ge(sem["loaded"], 64)
                pe.wait_ge(sem["ones"], 1)
                for i in range(n_k + 2):
                    for j, (lo, _) in enumerate(pieces):
                        if i == lo:
                            pe.wait_ge(sem[f"ctx{j}"], 32 if j == len(pieces) - 1 else 16)
                    if i >= 2:
                        pe.wait_ge(sem["k_top"], i - 1)
                    if i < n_k:
                        c, n = chunks[i]
                        nc.tensor.matmul(m.ps[:, i % 2, 0:n], wk[:], ctxT[:, c:c + n], start=True, stop=True).then_inc(sem["k_ps"], 1)
                    else:
                        h = i - n_k
                        nc.tensor.matmul(m.ps[:, i % 2, :], wq[:], m.xT[:, h * HALF:(h + 1) * HALF],
                                         start=True, stop=True).then_inc(sem["k_ps"], 1)
                    if i >= n_v:
                        continue
                    if i >= 2:
                        pe.wait_ge(sem["v_sb"], i - 1)
                    for t in range(4 * i, min(4 * i + 4, KT)):
                        ins = nc.tensor.matmul(m.ps[:, 2 + i % 2, (t % 4) * P:(t % 4 + 1) * P], ctxT[:, t * P:(t + 1) * P], wv[:],
                                               start=True, stop=True)
                    ins.then_inc(sem["v_ps"], 1)

            @block.scalar
            def _(act):
                nc.scalar.activation(table_warm[:], m.eps[:], ACT.Exp)
                act.wait_ge(sem["loaded"], 64)
                for i, (_, n) in enumerate(chunks + [(0, HALF), (HALF, HALF)]):
                    act.wait_ge(sem["k_ps"], i + 1)
                    if i >= 2:
                        act.wait_ge(sem["k_mid"], i - 1)
                    if i >= 4:
                        act.wait_ge(sem[f"k_stored{i % 4}"], 16 * (i // 4))
                    bias = {} if i < n_k else {"bias": bq[:, 0:1]}
                    nc.scalar.activation(k32[:, i % 2, 0:n], m.ps[:, i % 2, 0:n], ACT.Identity, **bias).then_inc(sem["k_sb"], 1)
                    nc.scalar.activation(kp[:, i % 4, 0, 0:n], m.ps[:, i % 2, 0:n], ACT.Identity, **bias).then_inc(sem["k_top"], 1)
                    if i < n_v:
                        n = min(4, KT - 4 * i)
                        act.wait_ge(sem["v_ps"], i + 1)
                        nc.scalar.activation(vs[:, 4 * i:4 * i + n, :, 0:HD],
                                             m.ps[:, 2 + i % 2, 0:n * P].rearrange("p (t h d) -> p t h d", h=NH, d=HD),
                                             ACT.Copy).then_inc(sem["v_sb"], 1)

            @block.vector
            def _(dve):
                nc.vector.memset(ctxT[CD:CD + 1, :], 1.0).then_inc(sem["ones"], 1)
                nc.vector.memset(filler[:], 1.0).then_inc(sem["filler"], 1)
                for i, (_, n) in enumerate(chunks + [(0, HALF), (HALF, HALF)]):
                    dve.wait_ge(sem["k_sb"], i + 1)
                    dve.wait_ge(sem["k_top"], i + 1)
                    if i >= 2:
                        dve.wait_ge(sem["k_parts"], i - 1)
                    if i >= 4:
                        dve.wait_ge(sem[f"k_stored{i % 4}"], 16 * (i // 4))
                    m.dve(dve, nc.vector.tensor_tensor(rest[:, i % 2, 0:n], k32[:, i % 2, 0:n], kp[:, i % 4, 0, 0:n], ALU.subtract))
                    nc.vector.tensor_copy(kp[:, i % 4, 1, 0:n], rest[:, i % 2, 0:n]).then_inc(sem["k_mid"], 1)
                dve.wait_ge(sem["v_ps"], n_v)
                dve.wait_ge(sem["k_ps"], n_k + 2)
                for h in range(2):
                    nc.vector.memset(qs[h], 0.0).then_inc(sem["cleared"], 1)
                dve.wait_ge(sem["v_sb"], n_v)
                m.dve(dve, nc.vector.memset(vs[:, :, :, HD:HD + 1], 1.0))
                nc.vector.tensor_scalar(vs[:, KT - 1, :, :], vs[:, KT - 1, :, :], m.padm[:, 0:1], None, ALU.mult)

            @block.gpsimd
            def _(pool):
                for i, (_, n) in enumerate(chunks + [(0, HALF), (HALF, HALF)]):
                    pool.wait_ge(sem["k_mid"], i + 1)
                    nc.gpsimd.tensor_tensor(kp[:, i % 4, 2, 0:n], rest[:, i % 2, 0:n], kp[:, i % 4, 1, 0:n],
                                            ALU.subtract).then_inc(sem["k_parts"], 1)

        attention_loop(m, c0, ks, vs, qs, prob, od)
        c0.close()

        with ExitStack() as c2:
            ao = sb("ao", [P, NPAIR, HALF], F32, c2)
            rec = sb("rec", [P, 2, 16], F32, c2)
            att = sb("att", [P, TT, P], F32, c2)
            attT = sb("attT", [P, NT], F32, c2)
            wo = sb("wo", [P, P], F32, c2)
            bo = sb("bo", [1, P], F32, c2)
            tr, nrm, atr, acp, ld, back = (m.sem("ca_" + s) for s in ("o_tr", "o_nrm", "o_atr", "o_acp", "o_loaded", "o_back"))
            block = c2.enter_context(nc.Block())

            @block.sync
            def _(sp):
                sp.dma_start(ao[:], od.rearrange("p (g n) -> p g n", g=NPAIR)).then_inc(back, 16)
                sp.dma_start(wo[:], a["ca_wo"]).then_inc(ld, 16)
                sp.dma_start(bo[:], a["ca_bo"]).then_inc(ld, 16)

            @block.tensor
            def _(pe):
                pe.wait_ge(back, 16)
                for g in range(NPAIR):
                    if g >= 2:
                        pe.wait_ge(nrm, 2 * (g - 1))
                    for c in range(4):
                        ins = nc.tensor.transpose(m.ps[:, g % 2, c * P:(c + 1) * P], ao[:, g, c * P:(c + 1) * P], m.ident[:])
                    ins.then_inc(tr, 1)
                pe.wait_ge(nrm, 2 * NPAIR)
                for t in range(TT):
                    ins = nc.tensor.transpose(m.ps[:, 2 + t // 4, (t % 4) * P:(t % 4 + 1) * P], att[:, t, :], m.ident[:])
                ins.then_inc(atr, 1)
                pe.wait_ge(acp, 2)
                pe.wait_ge(ld, 32)
                for t in range(TT):
                    o = m.ps[:, 4 + t // 4, (t % 4) * P:(t % 4 + 1) * P]
                    nc.tensor.matmul(o, attT[:, t * P:(t + 1) * P], wo[:], start=True, stop=False)
                    nc.tensor.matmul(o, m.ones_row[0:1, 0:P], bo[:], start=False, stop=True)

            @block.vector
            def _(dve):
                for g in range(NPAIR):
                    dve.wait_ge(tr, g + 1)
                    t = m.ps[:, g % 2, :].rearrange("p (c k r) -> p c k r", c=4, k=4)
                    r = rec[:, g % 2, :].rearrange("p (c k) -> p c k", c=4)
                    m.dve(dve, nc.vector.reciprocal(r.unsqueeze(3), t[:, :, :, HD:HD + 1]))
                    for h in range(2):
                        o = att[:, :, (2 * g + h) * HD:(2 * g + h + 1) * HD].rearrange("p (a c) d -> p c a d", a=2)
                        nc.vector.tensor_tensor(o, t[:, :, 2 * h:2 * h + 2, 0:HD],
                                                r[:, :, 2 * h:2 * h + 2].unsqueeze(3).to_broadcast([P, 4, 2, HD]),
                                                ALU.mult).then_inc(nrm, 1)
                dve.wait_ge(atr, 1)
                nc.vector.tensor_copy(attT[:, 0:HALF], m.ps[:, 2, :]).then_inc(acp, 1)

            @block.scalar
            def _(act):
                act.wait_ge(atr, 1)
                nc.scalar.activation(attT[:, HALF:NT], m.ps[:, 3, :], ACT.Copy).then_inc(acp, 1)
    layernorm(m, "ln1", m.ps[:, 4:6, :].rearrange("p a (b c) -> p (a b) c", c=P))


def attention_loop(m, ctx, ks, vs, qs, prob, od):
    nc = m.nc

    def sb(name, shape, dt=F32):
        return m.sb("at_" + name, shape, dt, ctx)

    def sem(name):
        return m.sem("at_" + name)

    vb = [sb(f"vb{t}", [P, 2, 32]) for t in range(TPB)]
    zero = sb("zero", [P, HALF], BF16)
    mx = sb("mx", [P, 16, NB])
    top = sb("top", [P, 16])
    hl = sb("hl", [P, 2, 2, TT], BF16)
    mt = sb("mt", [32, P], BF16)
    sums = sb("sums", [P, HALF])
    (ready0, v_ready, scores, probs, v_used, a_scores, a_maxed, pv_done, pv_free, sums_stored, fin, hl_ready, mt_ps,
     mt_ready, mrow) = (sem(n) for n in (
         "init", "v_ready", "scores", "probs", "v_used", "a_scores", "a_maxed", "pv_done", "pv_free", "sums_stored", "fin",
         "hl_ready", "mt_ps", "mt_ready", "mrow"))
    S = [m.ps[:, i, :] for i in range(3)]
    A = [m.ps[:, 3 + 2 * u:5 + 2 * u, 0:BLK] for u in range(2)]
    PV = m.ps[:, 7, :]
    mt_bank = m.ps[0:32, 3, 0:P // 2].bitcast(BF16)
    FREE_S, FREE_V, FREE_A = 3, TPB, 2
    scale = float(np.float32(1.0) / np.sqrt(np.float32(HD)))
    block = ctx.enter_context(nc.Block())

    @block.tensor
    def _(pe):
        def score_step(g, c, ib, i):
            t, h, half = i // 4, i // 2 % 2, i % 2
            pe.wait_ge(probs, ib * 12 + i + 1)
            nc.tensor.matmul(S[i % 3], ks[:, bass.ds(g * KP + c * BLK + t * P, P)], qs[h][:, bass.ds(g * NT + half * HALF, HALF)],
                             start=True, stop=True).then_inc(scores, 1)

        def value_step(ib, t):
            pe.wait_ge(v_ready, ib * TPB + t + 1)
            pe.wait_ge(probs, ib * 12 + 4 * t + 4 + FREE_S)
            for k in range(4):
                ins = nc.tensor.matmul(PV[32 * k:32 * k + 32, :], vb[t][:, k // 2, :], prob[:, 4 * t + k, :],
                                       start=False, stop=False)
            ins.then_inc(v_used, 1)

        def max_step(ga, c, ia, u):
            pe.wait_ge(a_maxed, ia * 8 + u + 1)
            for n in range(2):
                h, t = (2 * u + n) // TT, (2 * u + n) % TT
                ins = nc.tensor.matmul(A[u % 2][:, n, :], qs[h][:, bass.ds(ga * NT + t * P, P)], ks[:, bass.ds(ga * KP + c * BLK, BLK)],
                                       start=True, stop=True)
            ins.then_inc(a_scores, 1)

        def open_pair(g):
            pe.wait_ge(mrow, g * 32 + 32)
            pe.wait_ge(pv_free, g + 1)
            for k in range(4):
                nc.tensor.matmul(PV[32 * k:32 * k + 32, :], zero[:, 0:32], zero[:], start=True, stop=False)

        def close_pair():
            for k in range(4):
                ins = nc.tensor.matmul(PV[32 * k:32 * k + 32, :], zero[:, 0:32], zero[:], start=False, stop=True)
            ins.then_inc(pv_done, 1)

        def flip_maximum(ga):
            pe.wait_ge(hl_ready, ga + 1)
            nc.tensor.transpose(mt_bank, hl[:].rearrange("p a b c -> p (a b c)"), m.identb[:]).then_inc(mt_ps, 1)

        def attend(g, c, order=ATTENTION_STEP, first=False, with_maximum=True):
            ib = g * NB + c
            for step in order.split():
                kind, i = step[0], int(step[1:] or 0)
                if kind == "s":
                    score_step(g, c, ib, i)
                elif kind == "v" and i == TPB - 1:
                    if not first:
                        value_step(ib - 1, i)
                elif kind == "v":
                    value_step(ib, i)
                elif kind == "m" and with_maximum:
                    max_step(g + 1, c + 1, ib + NB + 1, i)
                elif kind == "f":
                    flip_maximum(g + 1)
                elif kind == "n":
                    next_first_step(g, i)

        def next_first_step(g, u):
            if u == 0:
                pe.wait_ge(mt_ready, g + 2)
            max_step(g + 2, 0, g * NB + 2 * NB, u)

        def pair(g, last_step):
            open_pair(g)
            attend(g, 0, first=True)
            with pe.Fori(0, NB - 2) as c:
                attend(g, c + 1)
            attend(g, NB - 1, order=last_step)
            value_step(g * NB + NB - 1, TPB - 1)
            close_pair()

        pe.wait_ge(ready0, 4)
        with pe.Fori(0, NB) as c:
            for u in range(8):
                max_step(0, c, c, u)
        flip_maximum(0)
        pe.sem_inc(v_used, FREE_V)
        pe.wait_ge(mt_ready, 1)
        for u in range(8):
            max_step(1, 0, NB, u)
        with pe.Fori(0, NPAIR - 2) as g:
            pair(g, LAST_STEP)
            for u in range(4, 8):
                next_first_step(g, u)
        pair(NPAIR - 2, LAST_STEP_ALONE)
        last = NPAIR - 1
        open_pair(last)
        attend(last, 0, first=True, with_maximum=False)
        with pe.Fori(0, NB - 1) as c:
            attend(last, c + 1, with_maximum=False)
        value_step(last * NB + NB - 1, TPB - 1)
        close_pair()

    @block.scalar
    def _(act):
        act.sem_inc(probs, FREE_S)
        with act.Fori(0, NPAIR) as g:
            with act.Fori(0, NB) as c:
                ib = g * NB + c
                for i in range(12):
                    if i % 4 == 0:
                        act.wait_ge(v_used, ib * TPB + i // 4 + 1)
                    act.wait_ge(scores, ib * 12 + i + 1)
                    nc.scalar.activation(prob[:, i, :], S[i % 3], ACT.Exp, scale=scale).then_inc(probs, 1)

    @block.vector
    def _(dve):
        def reduce_steps(ia, c, first=0, last=8):
            for u in range(first, last):
                dve.wait_ge(a_scores, ia * 8 + u + 1)
                nc.vector.tensor_reduce(mx[:, 2 * u:2 * u + 2, bass.ds(c, 1)], A[u % 2], AX.X, ALU.max).then_inc(a_maxed, 1)

        def finish_maximum(ga, rows_delivered):
            dve.wait_ge(a_maxed, ga * (8 * NB) + 8 * NB + FREE_A)
            nc.vector.tensor_reduce(top[:], mx[:], AX.X, ALU.max).then_inc(fin, 1)
            t2 = top[:].rearrange("p (h q) -> p h q", h=2)
            dve.wait_ge(fin, ga * 2 + 1)
            nc.vector.tensor_scalar(hl[:, :, 0, :], t2, -1.0, None, ALU.mult).then_inc(fin, 1)
            dve.wait_ge(fin, ga * 2 + 2)
            nc.vector.scalar_tensor_tensor(hl[:, :, 1, :], t2, -1.0, hl[:, :, 0, :], ALU.mult, ALU.subtract).then_inc(hl_ready, 1)
            dve.wait_ge(mt_ps, ga + 1)
            if rows_delivered is not None:
                dve.wait_ge(mrow, rows_delivered)
            nc.vector.tensor_copy(mt[:], mt_bank).then_inc(mt_ready, 1)

        def copy_sums(g):
            dve.wait_ge(pv_done, g + 1)
            dve.wait_ge(sums_stored, g * 16 + 16)
            nc.vector.tensor_copy(sums[:], PV).then_inc(pv_free, 1)

        for z in vb:
            nc.vector.memset(z[:], 0.0).then_inc(ready0, 1)
        nc.vector.memset(zero[:], 0.0).then_inc(ready0, 1)
        dve.sem_inc(a_maxed, FREE_A)
        dve.sem_inc(pv_free, 1)
        with dve.Fori(0, NB) as c:
            reduce_steps(c, c)
        finish_maximum(0, None)
        reduce_steps(NB, 0)
        with dve.Fori(0, NPAIR - 2) as g:
            with dve.Fori(0, NB - 1) as c:
                reduce_steps(g * NB + c + NB + 1, c + 1)
            finish_maximum(g + 1, g * 32 + 32)
            reduce_steps(g * NB + 2 * NB, 0, 0, 4)
            copy_sums(g)
            reduce_steps(g * NB + 2 * NB, 0, 4, 8)
        with dve.Fori(0, NB - 1) as c:
            reduce_steps(c + (NPAIR - 1) * NB + 1, c + 1)
        finish_maximum(NPAIR - 1, (NPAIR - 1) * 32)
        copy_sums(NPAIR - 2)
        copy_sums(NPAIR - 1)

    @block.gpsimd
    def _(pool):
        pool.wait_ge(ready0, 4)
        with pool.Fori(0, NPAIR) as g:
            with pool.Fori(0, NB) as c:
                for t in range(TPB):
                    pool.wait_ge(v_used, g * (NB * TPB) + c * TPB + t + 1)
                    nc.gpsimd.tensor_copy(vb[t][:, :, 0:HD + 1],
                                          vs[:].rearrange("p t h d -> p (t h) d")[:, bass.ds(c * (TPB * NH) + g * 2 + t * NH, 2), :]).then_inc(v_ready, 1)

    @block.sync
    def _(sp):
        def deliver_maxima(ga):
            sp.wait_ge(mt_ready, ga + 1)
            for h in range(2):
                r = 64 * h + SPLIT_ROWS
                sp.dma_start(qs[h][r:r + 2, bass.ds(ga * NT, NT)], mt[16 * h:16 * h + 16, :]).then_inc(mrow, 16)

        def store_sums(g):
            sp.wait_ge(pv_free, g + 2)
            sp.dma_start(od[:, bass.ds(g * HALF, HALF)], sums[:]).then_inc(sums_stored, 16)

        sp.sem_inc(sums_stored, 16)
        deliver_maxima(0)
        with sp.Fori(0, NPAIR - 1) as g:
            deliver_maxima(g + 1)
            store_sums(g)
        store_sums(NPAIR - 1)
        sp.wait_ge(mrow, 32 * NPAIR)
        sp.wait_ge(sums_stored, 16 * (NPAIR + 1))


def first_mask(m, dve, src, top, rev, tmp, tmp_top, mask):
    nc = m.nc

    def wide(t):
        return t[:].unsqueeze(2).to_broadcast([P, TT, NE])

    m.dve(dve, nc.vector.tensor_tensor(tmp[:], src[:], wide(top), ALU.is_equal))
    m.dve(dve, nc.vector.tensor_tensor(tmp[:], tmp[:], rev[:].unsqueeze(1).to_broadcast([P, TT, NE]), ALU.mult))
    m.dve(dve, nc.vector.tensor_reduce(tmp_top[:], tmp[:], AX.X, ALU.max))
    m.dve(dve, nc.vector.tensor_tensor(mask[:], tmp[:], wide(tmp_top), ALU.is_equal))


def route(m, name, gate_key, top_k, wide_w):
    nc, a = m.nc, m.a
    with ExitStack() as ctx:
        def sb(n, shape):
            return m.sb(f"{name}_{n}", shape, F32, ctx)

        gate, rev, sel = sb("gate", [P, NE]), sb("rev", [P, NE]), sb("sel", [P, NE, P])
        lg, ex, tmp, mask, mask2, w = (sb(n, [P, TT, NE]) for n in ("lg", "ex", "tmp", "mask", "mask2", "w"))
        top, top2, t1, t2, t3 = (sb(n, [P, TT]) for n in ("top", "top2", "t1", "t2", "t3"))
        wT = sb("wT", [P, NT])
        loaded, logits, ex_in, ex_out, w_ready, w_ps, w_rows, wide_ps, wide_sb = (
            m.sem(f"{name}_{s}") for s in ("loaded", "logits", "exin", "exout", "w", "wps", "wrows", "wideps", "widesb"))
        lp = m.ps[:, 0, 0:TT * NE].rearrange("p (t e) -> p t e", e=NE)

        def wide(t):
            return t[:].unsqueeze(2).to_broadcast([P, TT, NE])

        block = ctx.enter_context(nc.Block())

        @block.sync
        def _(sp):
            sp.dma_start(gate[:], a[gate_key]).then_inc(loaded, 16)
            sp.dma_start(rev[:], a["c_rev"]).then_inc(loaded, 16)

        @block.tensor
        def _(pe):
            pe.wait_ge(loaded, 32)
            for t in range(TT):
                ins = nc.tensor.matmul(lp[:, t, :], m.xT[:, t * P:(t + 1) * P], gate[:], start=True, stop=True)
            ins.then_inc(logits, 1)
            pe.wait_ge(w_ready, 1)
            for t in range(TT):
                ins = nc.tensor.transpose(m.ps[0:NE, 1 + t // 4, t % 4 * P:(t % 4 + 1) * P], w[:, t, :], m.ident[:])
            ins.then_inc(w_ps, 1)
            pe.wait_ge(w_rows, 2)
            for i in range(2 * NE):
                e, h = i // 2, i % 2
                if i >= 4:
                    pe.wait_ge(wide_sb, i - 3)
                nc.tensor.matmul(m.ps[:, 4 + i % 4, :], sel[:, e, :], wT[:, h * HALF:(h + 1) * HALF],
                                 start=True, stop=True).then_inc(wide_ps, 1)

        @block.vector
        def _(dve):
            def own(ins):
                m.dve(dve, ins)

            nc.vector.tensor_copy(sel[:], m.ident[:, 0:NE].unsqueeze(2).to_broadcast([P, NE, P])).then_inc(w_rows, 1)
            own(nc.vector.memset(wT[:], 0.0))
            dve.wait_ge(loaded, 32)
            dve.wait_ge(logits, 1)
            own(nc.vector.tensor_copy(lg[:], lp))
            own(nc.vector.tensor_reduce(top[:], lg[:], AX.X, ALU.max))
            if top_k == 1:
                first_mask(m, dve, lg, top, rev, tmp, t1, mask)
                nc.vector.tensor_tensor(ex[:], lg[:], wide(top), ALU.subtract).then_inc(ex_in, 1)
                dve.wait_ge(ex_out, 1)
                own(nc.vector.tensor_reduce(t2[:], ex[:], AX.X, ALU.add))
                own(nc.vector.reciprocal(t3[:], t2[:]))
                nc.vector.tensor_tensor(w[:], mask[:], wide(t3), ALU.mult).then_inc(w_ready, 1)
            else:
                first_mask(m, dve, lg, top, rev, tmp, t1, mask)
                own(nc.vector.scalar_tensor_tensor(lg[:], mask[:], -BIG, lg[:], ALU.mult, ALU.add))
                own(nc.vector.tensor_reduce(top2[:], lg[:], AX.X, ALU.max))
                first_mask(m, dve, lg, top2, rev, tmp, t1, mask2)
                nc.vector.tensor_tensor(t2[:], top2[:], top[:], ALU.subtract).then_inc(ex_in, 1)
                dve.wait_ge(ex_out, 1)
                own(nc.vector.tensor_scalar(t1[:], t3[:], 1.0, None, ALU.add))
                own(nc.vector.reciprocal(t1[:], t1[:]))
                own(nc.vector.tensor_tensor(t2[:], t3[:], t1[:], ALU.mult))
                own(nc.vector.tensor_tensor(mask[:], mask[:], wide(t1), ALU.mult))
                own(nc.vector.tensor_tensor(mask2[:], mask2[:], wide(t2), ALU.mult))
                nc.vector.tensor_tensor(w[:], mask[:], mask2[:], ALU.add).then_inc(w_ready, 1)
            dve.wait_ge(w_ps, 1)
            nc.vector.tensor_copy(wT[0:NE, :], m.ps[0:NE, 1:3, :].rearrange("p a b -> p (a b)")).then_inc(w_rows, 1)

        @block.scalar
        def _(act):
            act.wait_ge(ex_in, 1)
            if top_k == 1:
                nc.scalar.activation(ex[:], ex[:], ACT.Exp).then_inc(ex_out, 1)
            else:
                nc.scalar.activation(t3[:], t2[:], ACT.Exp).then_inc(ex_out, 1)
            for i in range(2 * NE):
                act.wait_ge(wide_ps, i + 1)
                nc.scalar.activation(wide_w[:, i // 2, i % 2 * HALF:(i % 2 + 1) * HALF], m.ps[:, 4 + i % 4, :],
                                     ACT.Copy).then_inc(wide_sb, 1)


def to_token_tiles(m, name, acc):
    nc = m.nc
    with nc.Block() as block:
        @block.tensor
        def _(pe):
            for t in range(TT):
                nc.tensor.transpose(m.ps[:, 4 + t // 4, t % 4 * P:(t % 4 + 1) * P], acc[:, t * P:(t + 1) * P], m.ident[:])


class S4Tables:

    def __init__(self, m, ctx):
        self.m = m

        def sb(n, shape, dt=F32):
            return m.sb("sk_" + n, shape, dt, ctx)

        self.cc = sb("cc", [P, 8])
        self.b_steps, self.a_steps = sb("bsteps", [P, 32]), sb("asteps", [P, 32])
        self.logs, self.turns, self.red, self.ex = (sb(n, [P, 2, P]) for n in ("logs", "turns", "red", "ex"))
        self.power = sb("power", [P, 2, P], mybir.dt.int32)
        self.aim, self.cre, self.cim = (sb(n, [P, P]) for n in ("aim", "cre", "cim"))
        self.small = [sb(n, [P, P]) for n in ("dr", "wi", "er", "ei", "t1", "t2", "t3", "nr", "ni", "alpha", "beta")]
        self.th, self.rn, self.e2, self.g1, self.g2 = (sb(n, [P, P, 32]) for n in ("th", "rn", "e2", "g1", "g2"))
        self.decay = sb("decay", [P, P, 24])
        self.weight = sb("weight", [P, 2, P, 4])
        self.loaded, self.asked, self.answered = (m.sem("sk_" + n) for n in ("loaded", "asked", "answered"))
        er, ei, t3, nr = self.small[2], self.small[3], self.small[6], self.small[7]
        self.functions = [(self.red, ACT.Tanh), (er, ACT.Sin), (ei, ACT.Sin), (nr, ACT.Sin), (t3, ACT.Tanh), (self.e2, ACT.Sin),
                          (self.decay, ACT.Tanh), (self.g1, ACT.Sin), (self.g2, ACT.Sin)]

    def load(self, sp):
        a = self.m.a
        for dst, src in ((self.cc, "c_s4"), (self.b_steps, "c_bsteps"), (self.a_steps, "c_asteps"), (self.aim, "s4_aim"),
                         (self.cre, "s4_cre"), (self.cim, "s4_cim")):
            sp.dma_start(dst[:], a[src]).then_inc(self.loaded, 16)
        sp.dma_start(self.logs[:, 0, :], a["s4_ldt"]).then_inc(self.loaded, 16)
        sp.dma_start(self.logs[:, 1, :], a["s4_arl"]).then_inc(self.loaded, 16)

    def answer(self, act, first, last):
        for i in range(first, last):
            buf, f = self.functions[i]
            act.wait_ge(self.asked, i + 1)
            self.m.nc.scalar.activation(buf[:], buf[:], f, scale=0.5 if f == ACT.Tanh else 1.0).then_inc(self.answered, 1)

    def compute(s, dve):
        m, nc = s.m, s.m.nc
        cc, red, ex, power, aim, cre, cim = s.cc, s.red, s.ex, s.power, s.aim, s.cre, s.cim
        dr, wi, er, ei, t1, t2, t3, nr, ni, alpha, beta = s.small
        th, rn, e2, g1, g2, decay, weight = s.th, s.rn, s.e2, s.g1, s.g2, s.decay, s.weight

        def own(ins):
            m.dve(dve, ins)

        def ask(ins):
            ins.then_inc(s.asked, 1)

        def take(n):
            dve.wait_ge(s.answered, n)

        def reduced_angle(out, angle, turn, rad, tmp):
            own(nc.vector.tensor_scalar(tmp, angle, 1.0 / TWO_PI, turn, ALU.mult, ALU.add))
            own(nc.vector.tensor_scalar(tmp, tmp, MAGIC, MAGIC, ALU.add, ALU.subtract))
            own(nc.vector.scalar_tensor_tensor(out, tmp, -TWO_PI_HI, angle, ALU.mult, ALU.add))
            own(nc.vector.scalar_tensor_tensor(out, tmp, -TWO_PI_LO, out, ALU.mult, ALU.add))
            own(nc.vector.tensor_scalar(out, out, rad, PI_BELOW, ALU.add, ALU.min))
            ask(nc.vector.tensor_scalar(out, out, -PI_BELOW, None, ALU.max))

        tt, ts, stt = nc.vector.tensor_tensor, nc.vector.tensor_scalar, nc.vector.scalar_tensor_tensor
        dve.wait_ge(s.loaded, 16 * 8)
        own(ts(s.turns[:], s.logs[:], 1.0 / LN2, MAGIC, ALU.mult, ALU.add))
        own(ts(s.turns[:], s.turns[:], MAGIC, None, ALU.subtract))
        own(ts(s.turns[:], s.turns[:], -126.0, 127.0, ALU.max, ALU.min))
        own(stt(red[:], s.turns[:], -LN2_HI, s.logs[:], ALU.mult, ALU.add))
        ask(stt(red[:], s.turns[:], -LN2_LO, red[:], ALU.mult, ALU.add))
        own(ts(power[:], s.turns[:], 127.0, 8388608.0, ALU.add, ALU.mult))
        take(1)
        own(ts(ex[:], red[:], -1.0, 1.0, ALU.mult, ALU.add))
        own(nc.vector.reciprocal(ex[:], ex[:]))
        own(stt(ex[:], red[:], 1.0, ex[:], ALU.add, ALU.mult))
        own(tt(ex[:], ex[:], power[:].bitcast(F32), ALU.mult))
        dt, are = ex[:, 0, :], ex[:, 1, :]
        own(stt(dr[:], dt, -1.0, are, ALU.mult, ALU.mult))
        own(tt(wi[:], dt, aim[:], ALU.mult))
        reduced_angle(er[:], wi[:], 0.25, TWO_PI / 4, t1[:])
        reduced_angle(ei[:], wi[:], 0.0, 0.0, t1[:])
        own(ts(t2[:], wi[:], 0.5, None, ALU.mult))
        reduced_angle(nr[:], t2[:], 0.0, 0.0, t1[:])
        ask(ts(t3[:], dr[:], 1.0, None, ALU.mult))
        def steps(out, rate, which):
            n = which.shape[-1]
            return tt(out, rate[:].unsqueeze(2).to_broadcast([P, P, n]), which.unsqueeze(1).to_broadcast([P, P, n]), ALU.mult)

        own(steps(th[:], wi, s.b_steps[:]))
        reduced_angle(e2[:], th[:], cc[:, 0:1], cc[:, 1:2], rn[:])
        for at, which in ((0, s.b_steps[:, 0:8]), (8, s.b_steps[:, 0:32:8]), (12, s.a_steps[:, 0:8])):
            own(steps(decay[:, :, at:at + which.shape[-1]], dr, which))
        ask(steps(decay[:, :, 20:24], dr, s.a_steps[:, 0:32:8]))
        own(steps(th[:], wi, s.a_steps[:]))
        take(6)
        own(ts(t1[:], t3[:], -1.0, 1.0, ALU.mult, ALU.add))
        own(nc.vector.reciprocal(t1[:], t1[:]))
        own(stt(t3[:], t3[:], 2.0, t1[:], ALU.mult, ALU.mult))
        own(tt(er[:], er[:], t3[:], ALU.mult))
        own(stt(nr[:], nr[:], 2.0, nr[:], ALU.mult, ALU.mult))
        own(tt(er[:], er[:], nr[:], ALU.subtract))
        own(stt(ei[:], t3[:], 1.0, ei[:], ALU.add, ALU.mult))
        own(tt(nr[:], cre[:], er[:], ALU.mult))
        own(tt(t1[:], cim[:], ei[:], ALU.mult))
        own(tt(nr[:], nr[:], t1[:], ALU.subtract))
        own(tt(ni[:], cre[:], ei[:], ALU.mult))
        own(tt(t1[:], cim[:], er[:], ALU.mult))
        own(tt(ni[:], ni[:], t1[:], ALU.add))
        own(tt(t1[:], are, are, ALU.mult))
        own(tt(t2[:], aim[:], aim[:], ALU.mult))
        own(tt(t1[:], t1[:], t2[:], ALU.add))
        own(nc.vector.reciprocal(t1[:], t1[:]))
        own(tt(t2[:], ni[:], aim[:], ALU.mult))
        own(tt(t3[:], nr[:], are, ALU.mult))
        own(tt(alpha[:], t2[:], t3[:], ALU.subtract))
        own(tt(alpha[:], alpha[:], t1[:], ALU.mult))
        own(ts(alpha[:], alpha[:], cc[:, 4:5], None, ALU.mult))
        own(tt(t2[:], ni[:], are, ALU.mult))
        own(tt(t3[:], nr[:], aim[:], ALU.mult))
        own(tt(beta[:], t2[:], t3[:], ALU.add))
        own(stt(beta[:], beta[:], 2.0, t1[:], ALU.mult, ALU.mult))
        reduced_angle(g1[:], th[:], cc[:, 0:1], cc[:, 1:2], rn[:])
        reduced_angle(g2[:], th[:], cc[:, 2:3], cc[:, 3:4], rn[:])
        take(7)
        own(ts(decay[:], decay[:], -1.0, 1.0, ALU.mult, ALU.add))
        own(nc.vector.reciprocal(decay[:], decay[:]))
        own(ts(decay[:], decay[:], 2.0, 1.0, ALU.mult, ALU.subtract))
        split = [P, P, 4, 8]

        def by_step(t):
            return t[:].rearrange("p h (i j) -> p h i j", j=8)

        own(tt(by_step(e2), by_step(e2), decay[:, :, 0:8].unsqueeze(2).to_broadcast(split), ALU.mult))
        own(tt(by_step(e2), by_step(e2), decay[:, :, 8:12].unsqueeze(3).to_broadcast(split), ALU.mult))
        for i, rate in enumerate((alpha, beta)):
            own(tt(weight[:, i], decay[:, :, 20:24], rate[:].unsqueeze(2).to_broadcast([P, P, 4]), ALU.mult))
        take(9)
        for i, g in enumerate((g1, g2)):
            own(tt(by_step(g), by_step(g), weight[:, i].unsqueeze(3).to_broadcast(split), ALU.mult))
        own(tt(g1[:], g1[:], g2[:], ALU.add))
        tt(by_step(g1), by_step(g1), decay[:, :, 12:20].unsqueeze(2).to_broadcast(split), ALU.mult)

    def finish(s, kern, inputs_loaded):
        m, nc = s.m, s.m.nc
        k_ps = m.sem("sk_kps")
        with nc.Block() as block:
            @block.sync
            def _(sp):
                sp.wait_ge(inputs_loaded, 16 * 13)

            sums = m.ps[:, 0:2, :].rearrange("p a b -> p (a b)").rearrange("p (i c k) -> p i c k", c=TT, k=4)

            @block.tensor
            def _(pe):
                kp = m.ps[:, 0:2, :].rearrange("p a b -> p (a b)").rearrange("p (i a) -> p i a", a=32)
                for h in range(P):
                    j = h % 4
                    ins = nc.tensor.matmul(kp[32 * j:32 * j + 32, h // 4, :], s.e2[:, h, :], s.g1[:, h, :], start=True, stop=True)
                ins.then_inc(k_ps, 1)

            def place(j, k):
                dst = kern[32 * k:32 * k + 32].rearrange("p c (i j) -> p j i c", j=4)[:, j]
                return dst, sums[32 * j:32 * j + 32, :, :, k]

            @block.vector
            def _(dve):
                dve.wait_ge(k_ps, 1)
                for j in range(4):
                    for k in range(4):
                        nc.vector.tensor_copy(*place(j, k))


def experts_gelu(m):
    nc, a = m.nc, m.a
    FC = FF0 // P
    m.s4_ctx = m.ctx.enter_context(ExitStack())
    tables = m.s4_tables = S4Tables(m, m.s4_ctx)
    with ExitStack() as ctx:
        def sb(n, shape):
            return m.sb("m0_" + n, shape, F32, ctx)

        ww = sb("ww", [P, NE, NT])
        acc = sb("acc", [P, NT])
        route(m, "m0r", "m0_gate", 1, ww)
        w1 = [sb(f"w1_{i}", [P, FF0]) for i in range(2)]
        w2 = [sb(f"w2_{i}", [P, FC, P]) for i in range(2)]
        b1 = [sb(f"b1_{i}", [P, FC]) for i in range(2)]
        b2 = sb("b2", [P, NE])
        hid = sb("hid", [P, 2, FC, NT])
        part = sb("part", [P, 2, 2, HALF])
        loaded, cleared, up_ps, gelu, y_ps, y_read, weighted, added = (
            m.sem("m0_" + s) for s in ("loaded", "cleared", "up", "gelu", "y", "yread", "weighted", "added"))
        w_in = [m.sem(f"m0_w{i}") for i in range(2)]
        c3 = ctx.enter_context(ExitStack())
        block = c3.enter_context(nc.Block())

        @block.sync
        def _(sp):
            sp.dma_start(b2[:], a["m0_b2"]).then_inc(loaded, 16)
            tables.load(sp)
            with sp.Fori(0, NE // 2) as e2:
                for i in range(2):
                    e = e2 * 2 + i
                    sp.wait_ge(y_ps, e * 2 + 2)
                    sp.dma_start(b1[i][:], a["m0_b1"][bass.ds(e, 1)].rearrange("e p f -> p (e f)")).then_inc(w_in[i], 16)
                    sp.dma_start(w1[i][:], a["m0_w1"][bass.ds(e, 1)].rearrange("e p f -> p (e f)")).then_inc(w_in[i], 16)
                    sp.dma_start(w2[i][:], a["m0_w2"][bass.ds(e, 1)].rearrange("e (c p) d -> p (e c) d", p=P)).then_inc(w_in[i], 16)

        @block.tensor
        def _(pe):
            pe.sem_inc(y_ps, 4)
            with pe.Fori(0, NE // 2) as e2:
                for par in range(2):
                    e = e2 * 2 + par
                    pe.wait_ge(w_in[par], e2 * 48 + 48)
                    for i in range(2 * FC):
                        c, h = i // 2, i % 2
                        pe.wait_ge(gelu, e * 8 + i + 1)
                        nc.tensor.matmul(m.ps[:, i % 4, :], w1[par][:, c * P:(c + 1) * P], m.xT[:, h * HALF:(h + 1) * HALF],
                                         start=True, stop=True).then_inc(up_ps, 1)
                    for i in range(2 * FC):
                        c, h = i // 2, i % 2
                        pe.wait_ge(gelu, e * 8 + i + 1 + 4)
                        if c == 0:
                            pe.wait_ge(y_read, e * 2 + h + 1)
                        ins = nc.tensor.matmul(m.ps[:, 4 + 2 * par + h, :], w2[par][:, c, :],
                                               hid[:, par, c, h * HALF:(h + 1) * HALF], start=c == 0, stop=c == FC - 1)
                        if c == FC - 1:
                            ins.then_inc(y_ps, 1)

        @block.scalar
        def _(act):
            table_steps = ((1, 5), (5, 6), (6, 7), (7, 7), (7, 8), (8, 8), (8, 9), (9, 9))
            act.sem_inc(gelu, 4)
            tables.answer(act, 0, 1)
            act.wait_ge(loaded, 16)
            for e in range(NE):
                par = e % 2
                act.wait_ge(y_ps, e * 2 + 2)
                act.wait_ge(w_in[par], e // 2 * 48 + 48)
                for i in range(2 * FC):
                    c, h = i // 2, i % 2
                    act.wait_ge(up_ps, e * 8 + i + 1)
                    nc.scalar.activation(hid[:, par, c, h * HALF:(h + 1) * HALF], m.ps[:, i % 4, :], ACT.Gelu,
                                         bias=b1[par][:, c:c + 1]).then_inc(gelu, 1)
                tables.answer(act, *table_steps[e])
                for h in range(2):
                    act.wait_ge(y_ps, e * 2 + h + 1 + 4)
                    act.wait_ge(added, e * 2 + h + 1)
                    nc.scalar.activation(part[:, par, h, :], m.ps[:, 4 + 2 * par + h, :], ACT.Identity,
                                         bias=b2[:, e:e + 1]).then_inc(y_read, 1)

        @block.vector
        def _(dve):
            nc.vector.memset(acc[:], 0.0).then_inc(cleared, 1)
            tables.compute(dve)

        @block.gpsimd
        def _(pool):
            pool.sem_inc(added, 4)
            pool.sem_inc(y_read, 4)
            pool.wait_ge(cleared, 1)
            with pool.Fori(0, NE // 2) as e2:
                for par in range(2):
                    e = e2 * 2 + par
                    for h in range(2):
                        y = part[:, par, h, :]
                        pool.wait_ge(y_read, e * 2 + h + 1 + 4)
                        nc.gpsimd.tensor_tensor(y, y, ww[:, bass.ds(e, 1), h * HALF:(h + 1) * HALF].rearrange("p a b -> p (a b)"),
                                                ALU.mult).then_inc(weighted, 1)
                        pool.wait_ge(weighted, e * 2 + h + 1)
                        pool.wait_ge(added, e * 2 + h + 1 + 2)
                        o = acc[:, h * HALF:(h + 1) * HALF]
                        nc.gpsimd.tensor_tensor(o, o, y, ALU.add).then_inc(added, 1)

        c3.close()
        to_token_tiles(m, "m0", acc)
    s4_prefetch(m)
    layernorm(m, "ln2", m.ps[:, 4:6, :].rearrange("p a (b c) -> p (a b) c", c=P))


def experts_silu(m):
    nc, a = m.nc, m.a
    FC = FF1 // P
    with ExitStack() as ctx:
        def sb(n, shape):
            return m.sb("m1_" + n, shape, F32, ctx)

        ww = sb("ww", [P, NE, NT])
        acc = sb("acc", [P, NT])
        route(m, "m1r", "m1_gate", 2, ww)
        wg = [sb(f"wg_{i}", [P, FF1]) for i in range(2)]
        wu = [sb(f"wu_{i}", [P, FF1]) for i in range(2)]
        wd = [sb(f"wd_{i}", [P, FC, P]) for i in range(2)]
        sil = sb("sil", [P, 4, HALF])
        hid = sb("hid", [P, 2, FC, NT])
        part = sb("part", [P, 2, 2, HALF])
        cleared, g_ps, u_ps, silu, h_ready, y_ps, y_read, added = (
            m.sem("m1_" + s) for s in ("cleared", "g", "u", "silu", "h", "y", "yread", "added"))
        w_in = [m.sem(f"m1_w{i}") for i in range(2)]
        c3 = ctx.enter_context(ExitStack())
        block = c3.enter_context(nc.Block())

        @block.sync
        def _(sp):
            with sp.Fori(0, NE // 2) as e2:
                for i in range(2):
                    e = e2 * 2 + i
                    sp.wait_ge(y_ps, e * 2 + 2)
                    sp.dma_start(wg[i][:], a["m1_wg"][bass.ds(e, 1)].rearrange("e p f -> p (e f)")).then_inc(w_in[i], 16)
                    sp.dma_start(wu[i][:], a["m1_wu"][bass.ds(e, 1)].rearrange("e p f -> p (e f)")).then_inc(w_in[i], 16)
                    sp.dma_start(wd[i][:], a["m1_wd"][bass.ds(e, 1)].rearrange("e (c p) d -> p (e c) d", p=P)).then_inc(w_in[i], 16)

        @block.tensor
        def _(pe):
            pe.sem_inc(y_ps, 4)
            with pe.Fori(0, NE // 2) as e2:
                for par in range(2):
                    e = e2 * 2 + par
                    pe.wait_ge(w_in[par], e2 * 48 + 48)
                    for i in range(2 * FC):
                        c, h = i // 2, i % 2
                        x = m.xT[:, h * HALF:(h + 1) * HALF]
                        pe.wait_ge(h_ready, e * 4 + i + 3)
                        nc.tensor.matmul(m.ps[:, i % 2, :], wg[par][:, c * P:(c + 1) * P], x, start=True, stop=True).then_inc(g_ps, 1)
                        nc.tensor.matmul(m.ps[:, 2 + i % 2, :], wu[par][:, c * P:(c + 1) * P], x, start=True, stop=True).then_inc(u_ps, 1)
                    for i in range(2 * FC):
                        c, h = i // 2, i % 2
                        pe.wait_ge(h_ready, e * 4 + i + 1 + 4)
                        if c == 0:
                            pe.wait_ge(y_read, e * 2 + h + 1)
                        ins = nc.tensor.matmul(m.ps[:, 4 + 2 * par + h, :], wd[par][:, c, :],
                                               hid[:, par, c, h * HALF:(h + 1) * HALF], start=c == 0, stop=c == FC - 1)
                        if c == FC - 1:
                            ins.then_inc(y_ps, 1)

        @block.scalar
        def _(act):
            with act.Fori(0, NE) as e:
                for i in range(4):
                    act.wait_ge(g_ps, e * 4 + i + 1)
                    act.wait_ge(h_ready, e * 4 + i + 1)
                    nc.scalar.activation(sil[:, i, :], m.ps[:, i % 2, :], ACT.Silu).then_inc(silu, 1)

        @block.vector
        def _(dve):
            nc.vector.memset(acc[:], 0.0).then_inc(cleared, 1)
            dve.sem_inc(y_read, 4)
            dve.sem_inc(h_ready, 4)
            with dve.Fori(0, NE // 2) as e2:
                for par in range(2):
                    e = e2 * 2 + par
                    dve.wait_ge(y_ps, e * 2 + 2)
                    for i in range(4):
                        c, h = i // 2, i % 2
                        dve.wait_ge(silu, e * 4 + i + 1)
                        dve.wait_ge(u_ps, e * 4 + i + 1)
                        nc.vector.tensor_tensor(hid[:, par, c, h * HALF:(h + 1) * HALF], m.ps[:, 2 + i % 2, :], sil[:, i, :],
                                                ALU.mult).then_inc(h_ready, 1)
                    for h in range(2):
                        dve.wait_ge(y_ps, e * 2 + h + 1 + 4)
                        dve.wait_ge(added, e * 2 + h + 1)
                        nc.vector.tensor_tensor(
                            part[:, par, h, :], m.ps[:, 4 + 2 * par + h, :],
                            ww[:, bass.ds(e, 1), h * HALF:(h + 1) * HALF].rearrange("p a b -> p (a b)"), ALU.mult).then_inc(y_read, 1)

        @block.gpsimd
        def _(pool):
            pool.sem_inc(added, 4)
            pool.wait_ge(cleared, 1)
            with pool.Fori(0, NE // 2) as e2:
                for par in range(2):
                    e = e2 * 2 + par
                    for h in range(2):
                        pool.wait_ge(y_read, e * 2 + h + 1 + 4)
                        pool.wait_ge(added, e * 2 + h + 1 + 2)
                        o = acc[:, h * HALF:(h + 1) * HALF]
                        nc.gpsimd.tensor_tensor(o, o, part[:, par, h, :], ALU.add).then_inc(added, 1)

        c3.close()
        to_token_tiles(m, "m1", acc)
    layernorm(m, "ln5", m.ps[:, 4:6, :].rearrange("p a (b c) -> p (a b) c", c=P), out=m.out)


def s4_prefetch(m):
    nc, a = m.nc, m.a

    def sb(n, shape):
        return m.sb("s4_" + n, shape, F32, m.s4_ctx)

    dft = sb("dft", [P, TT, 2 * NF])
    altc, altr = sb("altc", [P, 1]), sb("altr", [1, NT])
    dcol, wout, bout = sb("dcol", [P, 1]), sb("wout", [P, 2 * P]), sb("bout", [1, 2 * P])
    loaded = m.sem("s4_loaded")
    m.s4_inputs = dft, altc, altr, dcol, wout, bout, loaded
    with nc.Block() as block:
        @block.sync
        def _(sp):
            for t in range(TT):
                sp.dma_start(dft[:, t, :], a["c_dft"][t * P:(t + 1) * P, :]).then_inc(loaded, 16)
            for dst, src in ((altc, "c_altc"), (altr, "c_altr"), (dcol, "s4_d"), (wout, "s4_wout"), (bout, "s4_bout")):
                sp.dma_start(dst[:], a[src]).then_inc(loaded, 16)


def s4_layer(m):
    nc, a = m.nc, m.a
    with ExitStack() as ctx:
        def sb(n, shape, c=ctx):
            return m.sb("s4_" + n, shape, F32, c)

        kern = sb("kern", [P, TT, P])
        dft, altc, altr, dcol, wout, bout, loaded = m.s4_inputs
        m.s4_tables.finish(kern, loaded)
        spare = [t[:].rearrange("p h n -> p (h n)") for t in (m.s4_tables.th, m.s4_tables.rn, m.s4_tables.g2)]
        kh, yh = (spare[0][:, i * 2 * NF:(i + 1) * 2 * NF].rearrange("p (s f) -> p s f", s=2) for i in range(2))
        t1 = spare[1][:, 0:NF]
        yT = spare[1][:, NF:NF + 2 * TT * P].rearrange("p (f h) -> p f h", h=P)
        u, gT = spare[2][:, 0:NT], spare[2][:, NT:2 * NT]
        sig, yb = (spare[2][:, i * NT:(i + 1) * NT].rearrange("p (t h) -> p t h", h=P) for i in (2, 3))
        khn, yhn, yrow = sb("khn", [P, 1]), sb("yhn", [P, 1]), sb("yrow", [1, P])
        (k_ps, k_sb, x_ps, y_sb, t_ps, t_sb, inv_ps, u_sb, g_sb, z_ps, s_sb) = (
            m.sem("s4_" + s) for s in ("kps", "ksb", "xps", "ysb", "tps", "tsb", "invps", "usb", "gsb", "zps", "ssb"))
        spec = m.ps[:, 4:8, :].rearrange("p (a b) c -> p a (b c)", a=2)
        scale = 1.0 / NF
        zp = m.ps[:, 0:4, :].rearrange("p a (b c) -> p (a b) c", c=2 * P)
        with nc.Block() as block:
            @block.tensor
            def _(pe):
                def forward(src, nyq, done):
                    for j in range(4):
                        for c in range(TT):
                            ins = nc.tensor.matmul(m.ps[:, 4 + j, :], src[:, c, :], dft[:, c, j * 512:(j + 1) * 512],
                                                   start=c == 0, stop=c == TT - 1)
                        ins.then_inc(done, 1)
                    for c in range(TT):
                        ins = nc.tensor.matmul(nyq, src[:, c, :], altc[:], start=c == 0, stop=c == TT - 1)
                    ins.then_inc(done, 1)

                forward(kern, m.ps[:, 0, 0:1], k_ps)
                pe.wait_ge(k_sb, 3)
                forward(m.xtok, m.ps[:, 1, 0:1], x_ps)
                pe.wait_ge(y_sb, 1)
                nc.tensor.matmul(m.ps[0:1, 2, 0:P], yhn[:], m.ident[:], start=True, stop=True).then_inc(t_ps, 1)
                for j in range(4):
                    pe.wait_ge(y_sb, 2 + j // 2)
                    if j == 2:
                        pe.wait_ge(t_sb, 1)
                    for c in range(4):
                        f = 4 * j + c
                        ins = nc.tensor.transpose(m.ps[:, (0, 1, 2, 3)[j], c * P:(c + 1) * P],
                                                  yh[:, f // TT, f % TT * P:(f % TT + 1) * P], m.ident[:])
                    ins.then_inc(t_ps, 1)
                pe.wait_ge(t_sb, 5)
                for h in range(2):
                    for f in range(2 * TT):
                        nc.tensor.matmul(m.ps[:, 4 + h, :], yT[:, f, :],
                                         dft[:, f % TT, f // TT * NF + h * HALF:f // TT * NF + (h + 1) * HALF],
                                         start=f == 0, stop=False)
                    nc.tensor.matmul(m.ps[:, 4 + h, :], yrow[:], altr[:, h * HALF:(h + 1) * HALF], start=False,
                                     stop=True).then_inc(inv_ps, 1)
                for t in range(TT):
                    pe.wait_ge(g_sb, 1 + t // 4)
                    nc.tensor.matmul(zp[:, t, :], gT[:, t * P:(t + 1) * P], wout[:], start=True, stop=False)
                    nc.tensor.matmul(zp[:, t, :], m.ones_row[0:1, 0:P], bout[:], start=False, stop=True).then_inc(z_ps, 1)

            @block.vector
            def _(dve):
                def own(ins):
                    m.dve(dve, ins)

                tt, ts = nc.vector.tensor_tensor, nc.vector.tensor_scalar
                dve.wait_ge(k_ps, 5)
                for s in range(2):
                    own(ts(kh[:, s, :], spec[:, s, :], scale, None, ALU.mult))
                    ts(kh[:, s, 0:1], kh[:, s, 0:1], 0.5, None, ALU.mult).then_inc(k_sb, 1)
                ts(khn[:], m.ps[:, 0, 0:1], 0.5 * scale, None, ALU.mult).then_inc(k_sb, 1)
                dve.wait_ge(k_sb, 3)
                dve.wait_ge(x_ps, 5)
                tt(yhn[:], khn[:], m.ps[:, 1, 0:1], ALU.mult).then_inc(y_sb, 1)
                own(tt(yh[:, 0, :], kh[:, 0, :], spec[:, 0, :], ALU.mult))
                own(tt(t1[:], kh[:, 1, :], spec[:, 1, :], ALU.mult))
                tt(yh[:, 0, :], yh[:, 0, :], t1[:], ALU.subtract).then_inc(y_sb, 1)
                dve.wait_ge(y_sb, 2)
                own(tt(yh[:, 1, :], kh[:, 1, :], spec[:, 0, :], ALU.mult))
                own(tt(t1[:], kh[:, 0, :], spec[:, 1, :], ALU.mult))
                tt(yh[:, 1, :], yh[:, 1, :], t1[:], ALU.add).then_inc(y_sb, 1)
                dve.wait_ge(t_ps, 1)
                nc.vector.tensor_copy(yrow[:], m.ps[0:1, 2, 0:P]).then_inc(t_sb, 1)
                for j in range(4):
                    dve.wait_ge(t_ps, 2 + j)
                    nc.vector.tensor_copy(yT[:, 4 * j:4 * j + 4, :].rearrange("p a b -> p (a b)"), m.ps[:, j, :]).then_inc(t_sb, 1)
                for h in range(2):
                    dve.wait_ge(inv_ps, h + 1)
                    nc.vector.scalar_tensor_tensor(u[:, h * HALF:(h + 1) * HALF], m.xT[:, h * HALF:(h + 1) * HALF], dcol[:, 0:1],
                                                   m.ps[:, 4 + h, :], ALU.mult, ALU.add).then_inc(u_sb, 1)
                for g in range(4):
                    dve.wait_ge(s_sb, g + 1)
                    tt(yb[:, 2 * g:2 * g + 2, :], zp[:, 2 * g:2 * g + 2, 0:P], sig[:, 2 * g:2 * g + 2, :], ALU.mult)

            @block.scalar
            def _(act):
                for h in range(2):
                    act.wait_ge(u_sb, h + 1)
                    nc.scalar.activation(gT[:, h * HALF:(h + 1) * HALF], u[:, h * HALF:(h + 1) * HALF],
                                         ACT.Gelu_apprx_tanh).then_inc(g_sb, 1)
                for g in range(4):
                    act.wait_ge(z_ps, 2 * g + 2)
                    nc.scalar.activation(sig[:, 2 * g:2 * g + 2, :], zp[:, 2 * g:2 * g + 2, P:2 * P], ACT.Sigmoid).then_inc(s_sb, 1)
        layernorm(m, "ln3", yb)
    m.s4_ctx.close()


W_D2V, W_IMG, W_TXT, W_ATT0, W_ATT1, W_F1, W_F2 = range(7)


def all_partitions(m, name, col, out, op):
    with m.nc.Block() as block:
        @block.gpsimd
        def _(pool):
            m.nc.gpsimd.partition_all_reduce(out, col, P, op)


def input_scale(m, top, weight_scale, inv, product, step):
    nc = m.nc
    with nc.Block() as block:
        @block.vector
        def _(dve):
            m.dve(dve, nc.vector.tensor_scalar(step, top, 1e-8, 1.0 / 127.0, ALU.max, ALU.mult))
            m.dve(dve, nc.vector.reciprocal(inv, step))
            for w, p in zip(weight_scale, product):
                nc.vector.tensor_tensor(p, step, w, ALU.mult)


def bit_layer(m, name, src, k, n, inv, quant, weight, out, scale, bias, max_out, real=None):
    nc = m.nc
    real = real or n
    chunks = [(c, min(HALF, n - c)) for c in range(0, n, HALF)]
    with ExitStack() as ctx:
        tmp = m.sb(name + "_tmp", [P, 4, HALF], F32, ctx)
        tops = m.sb(name + "_tops", [P, len(chunks)], F32, ctx)
        rounded, q, mm, ev = (m.sem(f"{name}_{s}") for s in ("rounded", "quant", "mm", "out"))
        block = ctx.enter_context(nc.Block())

        @block.gpsimd
        def _(pool):
            for i, (c, w) in enumerate(chunks):
                if i >= 4:
                    pool.wait_ge(q, i - 3)
                nc.gpsimd.tensor_scalar(tmp[0:k, i % 4, 0:w], src[0:k, c:c + w], inv[0:k, :], MAGIC, ALU.mult, ALU.add).then_inc(rounded, 1)

        @block.vector
        def _(dve):
            behind = 3
            for i in range(len(chunks) + behind):
                if i < len(chunks):
                    c, w = chunks[i]
                    dve.wait_ge(rounded, i + 1)
                    nc.vector.tensor_scalar(quant[0:k, c:c + w], tmp[0:k, i % 4, 0:w], MAGIC, 127.0, ALU.subtract, ALU.min).then_inc(q, 1)
                if i >= behind:
                    i -= behind
                    c, w = chunks[i]
                    dve.wait_ge(ev, i + 1)
                    w = min(w, real - c)
                    last = nc.vector.tensor_reduce(tops[:, i:i + 1], out[:, c:c + w], AX.X, ALU.max, apply_absolute_value=True)
            m.dve(dve, last)
            nc.vector.tensor_reduce(max_out, tops[:], AX.X, ALU.max)

        @block.tensor
        def _(pe):
            for i, (c, w) in enumerate(chunks):
                pe.wait_ge(q, i + 1)
                if i >= 4:
                    pe.wait_ge(ev, i - 3)
                nc.tensor.matmul(m.ps[:, i % 4, 0:w], weight, quant[0:k, c:c + w], start=True, stop=True).then_inc(mm, 1)

        @block.scalar
        def _(act):
            for i, (c, w) in enumerate(chunks):
                act.wait_ge(mm, i + 1)
                nc.scalar.activation(out[:, c:c + w], m.ps[:, i % 4, 0:w], ACT.Identity, scale=scale, bias=bias).then_inc(ev, 1)


def vision_attention(m):
    nc, a = m.nc, m.a
    with ExitStack() as ctx:
        def sb(n, shape, dt=F32, c=ctx):
            return m.sb("va_" + n, shape, dt, c)

        qimg = sb("qimg", [P, KP], BF16)
        fT = sb("fT", [P, NT])
        shapes = {W_D2V: (CD, P), W_IMG: (P, P), W_TXT: (P, P), W_ATT0: (P, 64), W_ATT1: (P, 64), W_F1: (P, 2 * FF0), W_F2: (P, 4 * P)}
        tern = {w: sb(f"tern{w}", list(shapes[w]), BF16) for w in shapes}
        tern_out = [sb(f"ternout{i}", [P, P]) for i in range(2)]
        bias = sb("bias", [P, 3])
        batt = [sb(f"batt{i}", [P, 64]) for i in range(2)]
        bf1, bf2 = sb("bf1", [P, 4]), sb("bf2", [P, P])
        wsc = sb("wsc", [P, 7])
        avg = sb("avg", [P, 1])
        img_step = sb("img_step", [P, 1])
        satt = sb("satt", [P, 2])
        with ExitStack() as c1:
            raw = {w: sb(f"raw{w}", list(shapes[w]), F32, c1) for w in shapes}
            raw_out = [sb(f"rawout{i}", [P, P], F32, c1) for i in range(2)]
            inv_n, sums, thr, nthr = (sb(n, [P, 7], F32, c1) for n in ("invn", "sums", "thr", "nthr"))
            tmp = sb("tmp", [P, 2 * FF0], F32, c1)
            tmpb = sb("tmpb", [P, P], F32, c1)
            tops, top = sb("tops", [P, 4], F32, c1), sb("top", [P, 4], F32, c1)
            vec, vis = sb("vec", [P, KP], F32, c1), sb("vis", [P, KP], F32, c1)
            qtmp = sb("qtmp", [P, KP], BF16, c1)
            halves = sb("halves", [P, 2], F32, c1)
            loaded = m.sem("va_loaded")
            with nc.Block() as block:
                @block.sync
                def _(sp):
                    for dst, src in [(raw[w], f"va_w{w}") for w in shapes] + [(raw_out[0], "va_wo0"), (raw_out[1], "va_wo1"),
                                     (inv_n, "c_inv"), (bias, "va_bias"), (batt[0], "va_batt0"), (batt[1], "va_batt1"),
                                     (bf1, "va_bf1"), (bf2, "va_bf2")]:
                        sp.dma_start(dst[:], a[src]).then_inc(loaded, 16)
                    sp.dma_start(vec[0:CD, 0:KV], a["ctx_T"]).then_inc(loaded, 16)
                    sp.dma_start(vec[0:CD, KV:KP], a["ctx_T"][:, 0:KP - KV]).then_inc(loaded, 16)

                @block.vector
                def _(dve):
                    m.dve(dve, nc.vector.memset(sums[:], 0.0))
                    m.dve(dve, nc.vector.memset(tops[:], 0.0))
                    dve.wait_ge(loaded, 16 * 17)
                    for w, (k, _) in shapes.items():
                        nc.vector.tensor_reduce(sums[0:k, w:w + 1], raw[w][:], AX.X, ALU.add, apply_absolute_value=True)
                    nc.vector.tensor_reduce(tops[0:CD, 0:1], vec[0:CD, 0:KV], AX.X, ALU.max, apply_absolute_value=True)
                    nc.vector.tensor_reduce(tops[:, 1:2], m.xT[:], AX.X, ALU.max, apply_absolute_value=True)
            all_partitions(m, "w", sums[:], wsc[:], RADD)
            all_partitions(m, "x", tops[:], top[:], RMAX)
            with nc.Block() as block:
                @block.vector
                def _(dve):
                    def own(ins):
                        m.dve(dve, ins)

                    own(nc.vector.tensor_tensor(wsc[:], wsc[:], inv_n[:], ALU.mult))
                    own(nc.vector.tensor_scalar(wsc[:], wsc[:], 1e-5, None, ALU.max))
                    own(nc.vector.tensor_scalar(thr[:], wsc[:], 0.5, None, ALU.mult))
                    own(nc.vector.tensor_scalar(nthr[:], wsc[:], -0.5, None, ALU.mult))

                    def ternary(dst, src, k, w, t):
                        own(nc.vector.tensor_scalar(t, src[:], nthr[0:k, w:w + 1], None, ALU.is_lt))
                        own(nc.vector.scalar_tensor_tensor(dst[:], src[:], thr[0:k, w:w + 1], t, ALU.is_gt, ALU.subtract))

                    for w, (k, n) in shapes.items():
                        ternary(tern[w], raw[w], k, w, tmp[0:k, 0:n])
                    for i in range(2):
                        ternary(tern_out[i], raw_out[i], P, W_ATT0 + i, tmpb[:])
            sc = {n: sb("s_" + n, [P, 1], F32, c1) for n in ("inv_x", "p_x", "inv_c", "p_c", "inv_v", "p_v", "step", "max_v", "max_i", "top_v", "top_i",
                                         "inv_i", "max_f")}
            input_scale(m, top[:, 0:1], [wsc[:, W_D2V:W_D2V + 1]], sc["inv_c"][:], [sc["p_c"][:]], sc["step"][:])
            bit_layer(m, "va_d2v", vec, CD, KP, sc["inv_c"], qtmp, tern[W_D2V][:], vis, sc["p_c"][:, 0:1], bias[:, 0:1],
                      sc["max_v"][:], real=KV)
            all_partitions(m, "v", sc["max_v"][:], sc["top_v"][:], RMAX)
            input_scale(m, sc["top_v"][:], [wsc[:, W_IMG:W_IMG + 1]], sc["inv_v"][:], [sc["p_v"][:]], sc["step"][:])
            bit_layer(m, "va_img", vis, P, KP, sc["inv_v"], qtmp, tern[W_IMG][:], vec, sc["p_v"][:, 0:1], bias[:, 1:2],
                      sc["max_i"][:], real=KV)
            all_partitions(m, "i", sc["max_i"][:], sc["top_i"][:], RMAX)
            input_scale(m, sc["top_i"][:], [wsc[:, W_ATT0 + i:W_ATT0 + i + 1] for i in range(2)], sc["inv_i"][:],
                        [satt[:, i:i + 1] for i in range(2)], img_step[:])
            input_scale(m, top[:, 1:2], [wsc[:, W_TXT:W_TXT + 1]], sc["inv_x"][:], [sc["p_x"][:]], sc["step"][:])
            with nc.Block() as block:
                @block.vector
                def _(dve):
                    m.dve(dve, nc.vector.tensor_scalar(vis[:], vec[:], sc["inv_i"][:], MAGIC, ALU.mult, ALU.add))
                    nc.vector.tensor_scalar(qimg[:], vis[:], MAGIC, 127.0, ALU.subtract, ALU.min)

                @block.scalar
                def _(act):
                    for i in range(2):
                        m.act(act, nc.scalar.activation(qtmp[:].bitcast(F32)[:, 0:KV // 2], vec[:, i * (KV // 2):(i + 1) * (KV // 2)],
                                                        ACT.Copy, accum_out=halves[:, i:i + 1]))
                    m.act(act, nc.scalar.activation(avg[:], halves[:, 0:1], ACT.Identity, bias=halves[:, 1:2]))
                    nc.scalar.activation(avg[:], avg[:], ACT.Copy, scale=1.0 / KV)
            bit_layer(m, "va_txt", m.xT, P, NT, sc["inv_x"], qtmp, tern[W_TXT][:], fT, sc["p_x"][:, 0:1], bias[:, 2:3],
                      sc["max_f"][:])

        for layer in range(2):
            one_head_attention(m, f"v{layer}", qimg, fT, tern[W_ATT0 + layer], tern_out[layer], satt[:, layer:layer + 1], batt[layer])
        vision_mlp(m, fT, avg, wsc, tern, bf1, bf2)


def one_head_attention(m, name, qimg, fT, wT, w_out, scale, b_row):
    nc = m.nc
    with ExitStack() as ctx:
        def sb(n, shape, dt=F32):
            return m.sb(f"{name}_{n}", shape, dt, ctx)

        kv = sb("kv", [P, KT, 64])
        g32, rest = sb("g32", [P, NT]), sb("rest", [P, NT])
        gp = [sb(f"g{i}", [P, NT], BF16) for i in range(3)]
        mx, top = sb("mx", [P, TT, NB]), sb("top", [P, TT])
        hl, mt, neg = sb("hl", [P, 2, TT], BF16), sb("mt", [2 * TT, P], BF16), sb("neg", [P, NT], BF16)
        pick2 = sb("pick2", [P, P], BF16)
        minus = sb("minus", [P, NT])
        minus_ps, minus_ready, counted = (m.sem(f"{name}_{s}") for s in ("minusps", "minus", "counted"))
        kvs = [sb(f"kvs{t}", [P, 64]) for t in range(TPB)]
        total = sb("total", [P, 2, HALF])
        ones = sb("ones", [P, 64])
        filling = sb("filling", [P, 1])
        table_warm = sb("table_warm", [P, 1])
        prob = sb("prob", [P, 6, HALF])
        zero = sb("zero", [1, HALF], BF16)
        rec, o = sb("rec", [P, HALF]), sb("o", [P, HALF])
        odup = sb("odup", [P, NT])
        (kv_ps, kv_sb, g_ps, g_sb, g_parts, a_scores, a_maxed, hl_ready, mt_ps, mt_ready, neg_ready, kvs_ready, scores,
         probs, used, shifted, summed0, summed1, pv_done, o_ready, o_in) = (m.sem(f"{name}_{s}") for s in (
             "kvps", "kvsb", "gps", "gsb", "gparts", "ascores", "amaxed", "hl", "mtps", "mt", "neg", "kvs", "scores",
             "probs", "used", "shifted", "summed0", "summed1", "pvdone", "o", "oin"))
        groups = [(g * TT, min(TT, KT - g * TT)) for g in range(-(-KT // TT))]
        with nc.Block() as block:
            @block.tensor
            def _(pe):
                for h in range(2):
                    nc.tensor.matmul(m.ps[:, 4 + h, :], w_out[:], fT[:, h * HALF:(h + 1) * HALF], start=True, stop=True).then_inc(g_ps, 1)
                for i, (t0, n) in enumerate(groups):
                    if i >= 2:
                        pe.wait_ge(kv_sb, i - 1)
                    for t in range(n):
                        ins = nc.tensor.matmul(m.ps[:, i % 2, t * 64:(t + 1) * 64], qimg[:, (t0 + t) * P:(t0 + t + 1) * P], wT[:],
                                               start=True, stop=True)
                    ins.then_inc(kv_ps, 1)

            @block.scalar
            def _(act):
                nc.scalar.activation(table_warm[:], m.eps[:], ACT.Exp)
                for h in range(2):
                    act.wait_ge(g_ps, h + 1)
                    nc.scalar.activation(g32[:, h * HALF:(h + 1) * HALF], m.ps[:, 4 + h, :], ACT.Copy, scale=scale).then_inc(g_sb, 1)

            @block.vector
            def _(dve):
                nc.vector.memset(neg[:], 0.0)
                nc.vector.memset(total[:], 0.0)
                nc.vector.memset(ones[:], 1.0)
                nc.vector.memset(pick2[:], 0.0)
                nc.vector.tensor_scalar(filling[:], m.padm[:], -1.0, None, ALU.add)
                dve.wait_ge(g_sb, 2)
                split3(m, dve, g32[:], gp[0][:], gp[1][:], gp[2][:], rest[:], g_parts)
                for i, (t0, n) in enumerate(groups):
                    dve.wait_ge(kv_ps, i + 1)
                    nc.vector.scalar_tensor_tensor(kv[:, t0:t0 + n, 0:64],
                                                   m.ps[:, i % 2, 0:n * 64].rearrange("p (t c) -> p t c", c=64), scale,
                                                   b_row[:].unsqueeze(1).to_broadcast([P, n, 64]), ALU.mult, ALU.add).then_inc(kv_sb, 1)
                dve.wait_ge(kv_sb, len(groups))
                nc.vector.tensor_scalar(kv[:, KT - 1, :], kv[:, KT - 1, :], m.padm[:, 0:1], None, ALU.mult)
                nc.vector.memset(pick2[0:2, :], 1.0)
                nc.vector.memset(zero[:], 0.0)

        with nc.Block() as block:
            @block.tensor
            def _(pe):
                with pe.Fori(0, NB) as c:
                    for u in range(4):
                        pe.wait_ge(a_maxed, c * 4 + u + 1)
                        for j in range(2):
                            q = (2 * u + j) * P
                            for i in range(2):
                                ins = nc.tensor.matmul(m.ps[:, 2 * u + j, 0:BLK], gp[i][:, q:q + P],
                                                       qimg[:, bass.ds(c * BLK, BLK)], start=i == 0, stop=i == 1)
                        ins.then_inc(a_scores, 1)
                pe.wait_ge(hl_ready, 1)
                nc.tensor.transpose(m.ps[0:2 * TT, 0, 0:P // 2].bitcast(BF16), hl[:].rearrange("p a b -> p (a b)"),
                                    m.identb[:]).then_inc(mt_ps, 1)

            @block.vector
            def _(dve):
                dve.sem_inc(a_maxed, 4)
                with dve.Fori(0, NB) as c:
                    for u in range(4):
                        dve.wait_ge(a_scores, c * 4 + u + 1)
                        nc.vector.tensor_reduce(mx[:, 2 * u:2 * u + 2, bass.ds(c, 1)], m.ps[:, 2 * u:2 * u + 2, 0:BLK],
                                                AX.X, ALU.max).then_inc(a_maxed, 1)
                dve.wait_ge(a_maxed, 4 * NB + 4)
                m.dve(dve, nc.vector.tensor_reduce(top[:], mx[:], AX.X, ALU.max))
                m.dve(dve, nc.vector.tensor_scalar(hl[:, 0, :], top[:], -1.0, None, ALU.mult))
                nc.vector.scalar_tensor_tensor(hl[:, 1, :], top[:], -1.0, hl[:, 0, :], ALU.mult, ALU.subtract).then_inc(hl_ready, 1)
                dve.wait_ge(mt_ps, 1)
                nc.vector.tensor_copy(mt[:], m.ps[0:2 * TT, 0, 0:P // 2].bitcast(BF16)).then_inc(mt_ready, 1)

            @block.sync
            def _(sp):
                sp.wait_ge(mt_ready, 1)
                sp.dma_start(neg[0:2, :], mt[:]).then_inc(neg_ready, 16)
                sp.wait_ge(neg_ready, 16)

        O, D = m.ps[:, 6, :], m.ps[:, 7, :]
        with nc.Block() as block:
            @block.tensor
            def _(pe):
                def value_step(c, t):
                    pe.wait_ge(kvs_ready, c * TPB + t + 1)
                    pe.wait_ge(probs, c * 6 + 2 * t + 2 + 3)
                    for h in range(2):
                        ins = nc.tensor.matmul(O[64 * h:64 * h + 64, :], kvs[t][:], prob[:, 2 * t + h, :], start=False, stop=False)
                    ins.then_inc(used, 1)

                def attend(c, first=False):
                    for i in range(6):
                        t, h = i // 2, i % 2
                        pe.wait_ge(shifted, c * 6 + i + 1)
                        x = slice(h * HALF, (h + 1) * HALF)
                        for j in range(3):
                            ins = nc.tensor.matmul(m.ps[:, i % 3, :], qimg[:, bass.ds(c * BLK + t * P, P)], gp[j][:, x],
                                                   start=j == 0, stop=j == 2)
                        ins.then_inc(scores, 1)
                        if i in (3, 5):
                            value_step(c, i // 2 - 1)
                        elif i == 1 and not first:
                            value_step(c - 1, 2)

                for h in range(2):
                    nc.tensor.matmul(m.ps[:, h, :], pick2[:], neg[:, h * HALF:(h + 1) * HALF], start=True, stop=True).then_inc(minus_ps, 1)
                for h in range(2):
                    nc.tensor.matmul(O[64 * h:64 * h + 64, :], zero[0:1, 0:64], zero[0:1, :], start=True, stop=False)
                pe.wait_ge(minus_ready, 2)
                pe.sem_inc(used, 3)
                attend(0, first=True)
                with pe.Fori(0, NB - 1) as c:
                    attend(c + 1)
                value_step(NB - 1, 2)
                pe.wait_ge(counted, 2)
                for h in range(2):
                    nc.tensor.matmul(O[64 * h:64 * h + 64, :], zero[0:1, 0:64], zero[0:1, :], start=False, stop=True)
                    ins = nc.tensor.matmul(D[64 * h:64 * h + 64, :], ones[:], total[:, h, :], start=True, stop=True)
                ins.then_inc(pv_done, 1)

            @block.scalar
            def _(act):
                act.sem_inc(probs, 3)
                with act.Fori(0, NB) as c:
                    for i in range(6):
                        act.wait_ge(shifted, c * 6 + i + 1 + 3)
                        nc.scalar.activation(prob[:, i, :], prob[:, i, :], ACT.Exp, scale=1.0 / float(np.sqrt(P))).then_inc(probs, 1)

            @block.gpsimd
            def _(pool):
                with pool.Fori(0, NB) as c:
                    for t in range(TPB):
                        pool.wait_ge(used, c * TPB + t + 1)
                        nc.gpsimd.tensor_copy(kvs[t][:], kv[:, bass.ds(c * TPB + t, 1), :].rearrange("p a b -> p (a b)")).then_inc(kvs_ready, 1)
                        pool.wait_ge(probs, c * 6 + 2 * t + 2 + 3)
                        pool.wait_ge(summed1, c * 3 + t + 3)
                        nc.gpsimd.tensor_tensor(total[:, 1, :], total[:, 1, :], prob[:, 2 * t + 1, :], ALU.add).then_inc(summed1, 1)

            @block.vector
            def _(dve):
                def shift(c, i):
                    h = i % 2
                    dve.wait_ge(scores, c * 6 + i + 1)
                    dve.wait_ge(used, c * TPB + i // 2 + 1)
                    dve.wait_ge((summed0, summed1)[h], c * 3 + i // 2 + 1)
                    nc.vector.tensor_tensor(prob[:, i, :], m.ps[:, i % 3, :], minus[:, h * HALF:(h + 1) * HALF],
                                            ALU.add).then_inc(shifted, 1)

                for h in range(2):
                    dve.wait_ge(minus_ps, h + 1)
                    nc.vector.tensor_copy(minus[:, h * HALF:(h + 1) * HALF], m.ps[:, h, :]).then_inc(minus_ready, 1)
                dve.wait_ge(minus_ready, 2)
                dve.sem_inc(shifted, 3)
                dve.sem_inc(summed0, 3)
                dve.sem_inc(summed1, 3)
                with dve.Fori(0, NB) as c:
                    for t in range(TPB):
                        shift(c, 2 * t)
                        shift(c, 2 * t + 1)
                        dve.wait_ge(probs, c * 6 + 2 * t + 1 + 3)
                        dve.wait_ge(summed0, c * 3 + t + 3)
                        nc.vector.tensor_tensor(total[:, 0, :], total[:, 0, :], prob[:, 2 * t, :], ALU.add).then_inc(summed0, 1)
                dve.wait_ge(summed0, 3 * NB + 3)
                dve.wait_ge(summed1, 3 * NB + 3)
                for h in range(2):
                    nc.vector.scalar_tensor_tensor(total[:, h, :], prob[:, 4 + h, :], filling[:], total[:, h, :],
                                                   ALU.mult, ALU.add).then_inc(counted, 1)
                dve.wait_ge(pv_done, 1)
                m.dve(dve, nc.vector.reciprocal(rec[:], D))
                nc.vector.scalar_tensor_tensor(o[:], O, 0.1, rec[:], ALU.mult, ALU.mult).then_inc(o_ready, 1)
                dve.wait_ge(o_in, 64)
                nc.vector.tensor_tensor(fT[:], fT[:], odup[:], ALU.add)

            @block.sync
            def _(sp):
                sp.wait_ge(o_ready, 1)
                for h in range(2):
                    for d in range(2):
                        sp.dma_start(odup[64 * d:64 * d + 64, h * HALF:(h + 1) * HALF], o[64 * h:64 * h + 64, :]).then_inc(o_in, 16)


def vision_mlp(m, fT, avg, wsc, tern, bf1, bf2):
    nc = m.nc
    with ExitStack() as ctx:
        def sb(n, shape, dt=F32):
            return m.sb("vm_" + n, shape, dt, ctx)

        tops, top = sb("tops", [P, 2]), sb("top", [P, 2])
        big, inv, prod, step, inv2, prod2, hmax, htop = (
            sb(n, [P, 1]) for n in ("big", "inv", "prod", "step", "inv2", "prod2", "hmax", "htop"))
        tmp, qf = sb("tmp", [P, NT]), sb("qf", [P, NT], BF16)
        tav, qav = sb("tav", [P, 1]), sb("qav", [P, HALF], BF16)
        hid, qh = sb("hid", [P, 4, NT]), sb("qh", [P, 4, NT], BF16)
        htops = sb("htops", [P, 8])
        yb = sb("yb", [P, TT, P])
        mm, ev, q2, y_ps = (m.sem("vm_" + n) for n in ("mm", "ev", "q2", "y"))
        with nc.Block() as block:
            @block.vector
            def _(dve):
                nc.vector.tensor_reduce(tops[:, 0:1], fT[:], AX.X, ALU.max, apply_absolute_value=True)
                nc.vector.tensor_reduce(tops[:, 1:2], avg[:], AX.X, ALU.max, apply_absolute_value=True)
        all_partitions(m, "f", tops[:], top[:], RMAX)
        with nc.Block() as block:
            @block.vector
            def _(dve):
                nc.vector.tensor_tensor(big[:], top[:, 0:1], top[:, 1:2], ALU.max)
        input_scale(m, big[:], [wsc[:, W_F1:W_F1 + 1]], inv[:], [prod[:]], step[:])
        with nc.Block() as block:
            @block.vector
            def _(dve):
                m.dve(dve, nc.vector.tensor_scalar(tmp[:], fT[:], inv[:], MAGIC, ALU.mult, ALU.add))
                m.dve(dve, nc.vector.tensor_scalar(tav[:], avg[:], inv[:], MAGIC, ALU.mult, ALU.add))
                nc.vector.tensor_scalar(qav[:], tav[:].to_broadcast([P, HALF]), MAGIC, 127.0, ALU.subtract, ALU.min).then_inc(q2, 1)
                nc.vector.tensor_scalar(qf[:], tmp[:], MAGIC, 127.0, ALU.subtract, ALU.min).then_inc(q2, 1)
                for i in range(8):
                    dve.wait_ge(ev, i + 1)
                    ins = nc.vector.tensor_reduce(htops[:, i:i + 1], hid[:, i // 2, i % 2 * HALF:(i % 2 + 1) * HALF], AX.X, ALU.max)
                m.dve(dve, ins)
                nc.vector.tensor_reduce(hmax[:], htops[:], AX.X, ALU.max)

            @block.tensor
            def _(pe):
                pe.wait_ge(q2, 2)
                for i in range(8):
                    c, h = i // 2, i % 2
                    if i >= 4:
                        pe.wait_ge(ev, i - 3)
                    nc.tensor.matmul(m.ps[:, i % 4, :], tern[W_F1][:, c * P:(c + 1) * P], qf[:, h * HALF:(h + 1) * HALF], start=True, stop=False)
                    nc.tensor.matmul(m.ps[:, i % 4, :], tern[W_F1][:, FF0 + c * P:FF0 + (c + 1) * P], qav[:], start=False,
                                     stop=True).then_inc(mm, 1)

            @block.scalar
            def _(act):
                for i in range(8):
                    act.wait_ge(mm, i + 1)
                    nc.scalar.activation(hid[:, i // 2, i % 2 * HALF:(i % 2 + 1) * HALF], m.ps[:, i % 4, :], ACT.Relu,
                                         scale=prod[:, 0:1], bias=bf1[:, i // 2:i // 2 + 1]).then_inc(ev, 1)
        all_partitions(m, "h", hmax[:], htop[:], RMAX)
        input_scale(m, htop[:], [wsc[:, W_F2:W_F2 + 1]], inv2[:], [prod2[:]], step[:])
        with nc.Block() as block:
            @block.vector
            def _(dve):
                for c in range(4):
                    m.dve(dve, nc.vector.tensor_scalar(hid[:, c, :], hid[:, c, :], inv2[:], MAGIC, ALU.mult, ALU.add))
                    ins = nc.vector.tensor_scalar(qh[:, c, :], hid[:, c, :], MAGIC, 127.0, ALU.subtract, ALU.min)
                ins.then_inc(y_ps, 1)
                dve.wait_ge(y_ps, 2)
                yp = m.ps[:, 4:6, :].rearrange("p a (b c) -> p (a b) c", c=P)
                nc.vector.scalar_tensor_tensor(yb[:], yp, prod2[:, 0:1], bf2[:].unsqueeze(1).to_broadcast([P, TT, P]), ALU.mult, ALU.add)

            @block.tensor
            def _(pe):
                pe.wait_ge(y_ps, 1)
                for t in range(TT):
                    for c in range(4):
                        ins = nc.tensor.matmul(m.ps[:, 4 + t // 4, t % 4 * P:(t % 4 + 1) * P], qh[:, c, t * P:(t + 1) * P],
                                               tern[W_F2][:, c * P:(c + 1) * P], start=c == 0, stop=c == 3)
                ins.then_inc(y_ps, 1)
        layernorm(m, "ln4", yb)


STAGES = [deform_attention, cross_attention, experts_gelu, s4_layer, vision_attention, experts_silu]


def decoder_kernel(nc, a, out):
    with ExitStack() as ctx:
        m = Machine(nc, ctx, a)
        m.out = out
        setup(m)
        for stage in STAGES:
            stage(m)
            if stage is not experts_gelu:
                m.end_stage()


def layout(i):
    f = np.float32

    def row(v):
        return np.reshape(v, (1, -1))

    def col(v):
        return np.reshape(v, (-1, 1))

    def both(v):
        return np.concatenate([v.T, v.T], 0)

    x = i["x"][0]
    re = (np.arange(P) < NS).astype(f)
    l = np.arange(NT)
    turn = np.outer(l, l) % (2 * NF) * (np.pi / NF)
    alt = (1 - 2 * (l % 2)).astype(f)
    quarter, zero = np.full(P, 0.25, f), np.zeros(P, f)
    a = {
        "c_ident": np.eye(P, dtype=f), "c_iota": np.arange(P, dtype=f).reshape(P, 1),
        "c_pad": (np.arange(P) < LASTV).astype(f).reshape(P, 1),
        "c_flip": np.eye(HPO, dtype=f)[::-1],
        "x_tok": x, "x_T": x.T, "ctx_T": i["ctx_768"][0].T,
        "da_w": np.concatenate([i["L0_attn_W_off"][:, 0::2], i["L0_attn_W_attn"]], 1),
        "da_b": row(np.concatenate([i["L0_attn_b_off"][0::2], i["L0_attn_b_attn"]])),
        "da_wout": i["L0_attn_W_out"], "da_bout": row(i["L0_attn_b_out"]),
        "ca_wk": np.concatenate([i["L0_xattn_wk"].T, row(i["L0_xattn_bk"])], 0),
        "ca_wv": np.concatenate([i["L0_xattn_wv"].T, row(i["L0_xattn_bv"])], 0),
        "ca_wq": i["L0_xattn_wq"].T, "ca_bq": col(i["L0_xattn_bq"]),
        "c_rev": np.tile(np.arange(NE, 0, -1, dtype=f), (P, 1)),
        "m0_gate": i["L0_ffn_gate_w"], "m0_w1": i["L0_ffn_w1"], "m0_w2": i["L0_ffn_w2"],
        "m0_b1": i["L0_ffn_b1"].reshape(NE, FF0 // P, P).transpose(0, 2, 1), "m0_b2": i["L0_ffn_b2"].T,
        "m1_gate": i["L1_ffn_gate_w"].T, "m1_wg": i["L1_ffn_w_gate"], "m1_wu": i["L1_ffn_w_up"], "m1_wd": i["L1_ffn_w_down"],
        "c_s4": np.stack([quarter * re, np.pi / 2 * re, quarter * (1 - re), np.pi / 2 * (1 - re), 4 * re - 2, zero, zero, zero],
                         1).astype(f),
        "c_bsteps": np.tile(np.arange(32, dtype=f), (P, 1)), "c_asteps": np.tile(np.arange(0, NT, 32, dtype=f), (P, 1)),
        "c_dft": np.concatenate([np.cos(turn), np.sin(turn)], 1).astype(f), "c_altc": alt[0:P].reshape(P, 1), "c_altr": row(alt),
        "s4_ldt": np.broadcast_to(i["L1_attn_log_dt"], (P, P)), "s4_arl": both(i["L1_attn_A_real_log"]),
        "s4_aim": both(i["L1_attn_A_imag"]), "s4_cre": both(i["L1_attn_C_real"]), "s4_cim": both(i["L1_attn_C_imag"]),
        "s4_d": col(i["L1_attn_D"]), "s4_wout": i["L1_attn_W_out"], "s4_bout": row(i["L1_attn_b_out"]),
        "va_w0": i["L1_xattn_W_d2v"].T, "va_w1": i["L1_xattn_W_img"].T, "va_w2": i["L1_xattn_W_txt"].T,
        "va_w3": i["L1_xattn_W_att0"].T, "va_w4": i["L1_xattn_W_att1"].T,
        "va_w5": i["L1_xattn_W_f1"].T.reshape(2, P, FF0).transpose(1, 0, 2).reshape(P, 2 * FF0),
        "va_w6": i["L1_xattn_W_f2"].T.reshape(4, P, P).transpose(1, 0, 2).reshape(P, 4 * P),
        "va_wo0": np.concatenate([i["L1_xattn_W_att0"]] * 2, 0), "va_wo1": np.concatenate([i["L1_xattn_W_att1"]] * 2, 0),
        "c_inv": np.tile(np.array([1 / (CD * P), 1 / (P * P), 1 / (P * P), 1 / (64 * P), 1 / (64 * P), 1 / (2 * P * FF0), 1 / (P * FF0)], f), (P, 1)),
        "va_bias": np.stack([i["L1_xattn_b_d2v"], i["L1_xattn_b_img"], i["L1_xattn_b_txt"]], 1),
        "va_batt0": np.broadcast_to(i["L1_xattn_b_att0"], (P, 64)), "va_batt1": np.broadcast_to(i["L1_xattn_b_att1"], (P, 64)),
        "va_bf1": i["L1_xattn_b_f1"].reshape(4, P).T, "va_bf2": np.broadcast_to(i["L1_xattn_b_f2"], (P, P)),
        "ca_wo": i["L0_xattn_wo"].T, "ca_bo": row(i["L0_xattn_bo"]),
    }
    return {k: np.ascontiguousarray(v) for k, v in a.items()}


def kernel(**inputs):
    import concourse.bacc as bacc
    from concourse.bass_utils import run_bass_kernel_spmd

    arrays = layout({k: np.asarray(v) for k, v in inputs.items()})
    nc = bacc.Bacc("TRN2", target_bir_lowering=False, num_devices=1)
    a = {k: nc.dram_tensor(k, v.shape, mybir.dt.from_np(v.dtype), kind="ExternalInput").ap() for k, v in arrays.items()}
    out = nc.dram_tensor("out", (NT, P), F32, kind="ExternalOutput").ap()
    decoder_kernel(nc, a, out)
    r = run_bass_kernel_spmd(nc, [arrays], core_ids=[0])
    return np.reshape(r.results[0]["out"], (1, NT, P))
```
